# Optimizing a Trainium2 kernel written in Bass

```python
import numpy as np
import jax
import jax.numpy as jnp

def _softmax(x, axis=-1):
    return jax.nn.softmax(x, axis=axis)

def _gelu(x):
    return jax.nn.gelu(x, approximate=True)

def _silu(x):
    return jax.nn.silu(x)

def _sigmoid(x):
    return jax.nn.sigmoid(x)

def _layernorm(x, axis=-1, eps=1e-05):
    m = jnp.mean(x, axis=axis, keepdims=True)
    v = jnp.var(x, axis=axis, keepdims=True)
    return (x - m) / jnp.sqrt(v + eps)

def _scatter_add(tgt, idx, src, axis=0):
    return tgt.at[idx].add(src)

def _segment_sum(src, seg, n):
    return jax.ops.segment_sum(src, seg, n)
kernel_name = 'mk_decoder_postln_d1_seqx_r8_e98489'

def setup_inputs(seed: int=0):
    np.random.seed(seed)
    _w = jnp.asarray

    def _rec_inputs():
        import jax
        import jax.numpy as jnp
        _rk = jax.random.key(seed)
        x = -0.0002928 + 1 * jax.random.normal(jax.random.fold_in(_rk, 1), (32, 56, 128), jnp.float32)
        _lenS = 56 - jax.random.randint(jax.random.fold_in(_rk, 7), (32,), 0, max(1, 56 // 4) + 1, jnp.int32)
        _lenS2 = 1500 - jax.random.randint(jax.random.fold_in(_rk, 8), (32,), 0, max(1, 1500 // 4) + 1, jnp.int32)
        _ctx_1024P = jax.random.normal(jax.random.fold_in(_rk, 11), (32, 16, 128), jnp.float32)
        _ctx_1024c = jax.random.dirichlet(jax.random.fold_in(_rk, 511), 0.3 * jnp.ones((16,), jnp.float32), (32, 1500))
        _ctx_1024t = jnp.einsum('bsk,bkd->bsd', _ctx_1024c, _ctx_1024P)
        _ctx_1024t = _ctx_1024t * jax.lax.rsqrt(jnp.mean(jnp.square(_ctx_1024t)) + 1e-12) * 0.953939
        ctx_1024 = -1.39393e-06 + 0.999914 * (_ctx_1024t + 0.3 * jax.random.normal(jax.random.fold_in(_rk, 611), (32, 1500, 128), jnp.float32))
        return (x, ctx_1024)
    x, ctx_1024 = _rec_inputs()

    def _L0_attn_setup():
        import jax, jax.numpy as jnp
        import numpy as np
        import math
        N_HEAD = 16
        N_KV_HEAD = 4
        WINDOW = 64
        EPS = 1e-06

        def _rotate_half(t):
            t1, t2 = jnp.split(t, 2, axis=-1)
            return jnp.concatenate([-t2, t1], axis=-1)

        def _rope_tables(T, head_dim):
            theta = 1.0 / 10000.0 ** (jnp.arange(0, head_dim, 2, dtype=jnp.float32) / head_dim)
            pos = jnp.arange(T, dtype=jnp.float32)
            freqs = jnp.outer(pos, theta)
            cos = jnp.concatenate([jnp.cos(freqs), jnp.cos(freqs)], axis=-1)
            sin = jnp.concatenate([jnp.sin(freqs), jnp.sin(freqs)], axis=-1)
            return (cos, sin)
        key = jax.random.key(seed)
        k1, k2, k3, k4 = jax.random.split(key, 4)
        B, T, C = (1, 256, 128)
        kv_out = 2 * N_KV_HEAD * (C // N_HEAD)
        x = jax.random.normal(k1, (B, T, C), dtype=jnp.float32)
        Wq = jax.random.normal(k2, (C, C), dtype=jnp.float32) * 0.02
        Wkv = jax.random.normal(k3, (kv_out, C), dtype=jnp.float32) * 0.02
        Wproj = jax.random.normal(k4, (C, C), dtype=jnp.float32) * 0.02
        return {'x': x, 'Wq': Wq, 'Wkv': Wkv, 'Wproj': Wproj}
    _L0_attn_all = _L0_attn_setup()
    _L0_attn_in = {k: v for k, v in _L0_attn_all.items() if k in ('Wq', 'Wkv', 'Wproj')}
    del _L0_attn_all

    def _L0_xattn_setup():
        import jax, jax.numpy as jnp
        import numpy as np
        D_MODEL = 128
        NUM_HEADS = 16
        HEAD_DIM = D_MODEL // NUM_HEADS
        SCALE = HEAD_DIM ** (-0.5)
        BIAS_LEN = 128
        ROPE_BASE = 10000.0
        LN_EPS = 1e-05

        def _layernorm(x, gamma, beta):
            mu = jnp.mean(x, axis=-1, keepdims=True)
            var = jnp.mean(jnp.square(x - mu), axis=-1, keepdims=True)
            return (x - mu) * jax.lax.rsqrt(var + LN_EPS) * gamma + beta

        def _rope(x, cos, sin):
            half = HEAD_DIM // 2
            c = cos[None, None, :, :]
            s = sin[None, None, :, :]
            x_even, x_odd = (x[..., :half], x[..., half:])
            return jnp.concatenate([x_even * c - x_odd * s, x_even * s + x_odd * c], axis=-1)

        def _temporal_bias(L_q, L_kv):
            pos = jnp.arange(BIAS_LEN, dtype=jnp.float32)
            dist = jnp.abs(pos[None, :] - pos[:, None])
            bias = jnp.exp(-dist * 0.1) - dist * 0.05
            if L_q <= BIAS_LEN and L_kv <= BIAS_LEN:
                return bias[:L_q, :L_kv]
            return jax.image.resize(bias, (L_q, L_kv), method='bilinear')
        key = jax.random.key(seed)
        ks = jax.random.split(key, 8)
        B, Lq, Lkv = (8, 64, 64)
        return {'decoder_hidden': jax.random.normal(ks[0], (B, Lq, D_MODEL), jnp.float32), 'encoder_output': jax.random.normal(ks[1], (B, Lkv, D_MODEL), jnp.float32), 'Wqkv': jax.random.normal(ks[2], (3 * D_MODEL, D_MODEL), jnp.float32) * 0.02, 'Wout': jax.random.normal(ks[3], (D_MODEL, D_MODEL), jnp.float32) * 0.02, 'b_out': jnp.zeros((D_MODEL,), jnp.float32), 'Wgate': jax.random.normal(ks[4], (D_MODEL, D_MODEL), jnp.float32) * 0.02, 'b_gate': jnp.zeros((D_MODEL,), jnp.float32), 'gamma': jnp.ones((D_MODEL,), jnp.float32), 'beta': jnp.zeros((D_MODEL,), jnp.float32)}
    _L0_xattn_all = _L0_xattn_setup()
    _L0_xattn_in = {k: v for k, v in _L0_xattn_all.items() if k in ('Wqkv', 'Wout', 'b_out', 'Wgate', 'b_gate', 'gamma', 'beta')}
    del _L0_xattn_all

    def _L0_ffn_setup():
        import jax, jax.numpy as jnp
        import numpy as np
        B, T, D, F_FF, E, TOP_K = (8, 256, 128, 512, 8, 2)
        CAP_FACTOR = 1.25
        key = jax.random.key(seed)
        ks = jax.random.split(key, 7)
        s = 0.02
        return {'x': jax.random.normal(ks[0], (B, T, D), dtype=jnp.float32), 'w_router': jax.random.normal(ks[1], (D, E), dtype=jnp.float32) * s, 'b_router': jnp.zeros((E,), dtype=jnp.float32), 'w1': jax.random.normal(ks[2], (E, D, F_FF), dtype=jnp.float32) * s, 'b1': jnp.zeros((E, F_FF), dtype=jnp.float32), 'w2': jax.random.normal(ks[3], (E, F_FF, D), dtype=jnp.float32) * s, 'b2': jnp.zeros((E, D), dtype=jnp.float32)}
    _L0_ffn_all = _L0_ffn_setup()
    _L0_ffn_in = {k: v for k, v in _L0_ffn_all.items() if k in ('w_router', 'b_router', 'w1', 'b1', 'w2', 'b2')}
    del _L0_ffn_all
    return {'x': x, 'ctx_1024': ctx_1024, 'L0_attn_Wq': _L0_attn_in['Wq'], 'L0_attn_Wkv': _L0_attn_in['Wkv'], 'L0_attn_Wproj': _L0_attn_in['Wproj'], 'L0_xattn_Wqkv': _L0_xattn_in['Wqkv'], 'L0_xattn_Wout': _L0_xattn_in['Wout'], 'L0_xattn_b_out': _L0_xattn_in['b_out'], 'L0_xattn_Wgate': _L0_xattn_in['Wgate'], 'L0_xattn_b_gate': _L0_xattn_in['b_gate'], 'L0_xattn_gamma': _L0_xattn_in['gamma'], 'L0_xattn_beta': _L0_xattn_in['beta'], 'L0_ffn_w_router': _L0_ffn_in['w_router'], 'L0_ffn_b_router': _L0_ffn_in['b_router'], 'L0_ffn_w1': _L0_ffn_in['w1'], 'L0_ffn_b1': _L0_ffn_in['b1'], 'L0_ffn_w2': _L0_ffn_in['w2'], 'L0_ffn_b2': _L0_ffn_in['b2']}

def reference(x, ctx_1024, L0_attn_Wq, L0_attn_Wkv, L0_attn_Wproj, L0_xattn_Wqkv, L0_xattn_Wout, L0_xattn_b_out, L0_xattn_Wgate, L0_xattn_b_gate, L0_xattn_gamma, L0_xattn_beta, L0_ffn_w_router, L0_ffn_b_router, L0_ffn_w1, L0_ffn_b1, L0_ffn_w2, L0_ffn_b2):
    import jax
    import jax.numpy as jnp

    def _L0_attn_ref(x, Wq, Wkv, Wproj):
        import jax, jax.numpy as jnp
        import numpy as np
        import math
        N_HEAD = 16
        N_KV_HEAD = 4
        WINDOW = 64
        EPS = 1e-06

        def _rotate_half(t):
            t1, t2 = jnp.split(t, 2, axis=-1)
            return jnp.concatenate([-t2, t1], axis=-1)

        def _rope_tables(T, head_dim):
            theta = 1.0 / 10000.0 ** (jnp.arange(0, head_dim, 2, dtype=jnp.float32) / head_dim)
            pos = jnp.arange(T, dtype=jnp.float32)
            freqs = jnp.outer(pos, theta)
            cos = jnp.concatenate([jnp.cos(freqs), jnp.cos(freqs)], axis=-1)
            sin = jnp.concatenate([jnp.sin(freqs), jnp.sin(freqs)], axis=-1)
            return (cos, sin)
        B, T, C = x.shape
        H, KV = (N_HEAD, N_KV_HEAD)
        d = C // H
        n_rep = H // KV
        q = (x @ Wq.T).reshape(B, T, H, d).transpose(0, 2, 1, 3)
        kv = x @ Wkv.T
        k, v = jnp.split(kv, 2, axis=2)
        k = k.reshape(B, T, KV, d).transpose(0, 2, 1, 3)
        v = v.reshape(B, T, KV, d).transpose(0, 2, 1, 3)
        q = q / (jnp.linalg.norm(q, axis=-1, keepdims=True) + EPS)
        k = k / (jnp.linalg.norm(k, axis=-1, keepdims=True) + EPS)
        cos, sin = _rope_tables(T, d)
        cos = cos[None, None]
        sin = sin[None, None]
        q = q * cos + _rotate_half(q) * sin
        k = k * cos + _rotate_half(k) * sin
        k = jnp.repeat(k, n_rep, axis=1)
        v = jnp.repeat(v, n_rep, axis=1)
        rows = jnp.arange(T)[:, None]
        cols = jnp.arange(T)[None, :]
        mask = (cols <= rows) & (cols > rows - WINDOW)
        scale = 1.0 / math.sqrt(d)
        scores = jnp.einsum('bhqd,bhkd->bhqk', q, k) * scale
        scores = jnp.where(mask[None, None], scores, -jnp.inf)
        attn = jax.nn.softmax(scores, axis=-1)
        y = jnp.einsum('bhqk,bhkd->bhqd', attn, v)
        y = y.transpose(0, 2, 1, 3).reshape(B, T, C)
        return y @ Wproj.T

    def _L0_xattn_ref(decoder_hidden, encoder_output, Wqkv, Wout, b_out, Wgate, b_gate, gamma, beta):
        import jax, jax.numpy as jnp
        import numpy as np
        D_MODEL = 128
        NUM_HEADS = 16
        HEAD_DIM = D_MODEL // NUM_HEADS
        SCALE = HEAD_DIM ** (-0.5)
        BIAS_LEN = 128
        ROPE_BASE = 10000.0
        LN_EPS = 1e-05

        def _layernorm(x, gamma, beta):
            mu = jnp.mean(x, axis=-1, keepdims=True)
            var = jnp.mean(jnp.square(x - mu), axis=-1, keepdims=True)
            return (x - mu) * jax.lax.rsqrt(var + LN_EPS) * gamma + beta

        def _rope(x, cos, sin):
            half = HEAD_DIM // 2
            c = cos[None, None, :, :]
            s = sin[None, None, :, :]
            x_even, x_odd = (x[..., :half], x[..., half:])
            return jnp.concatenate([x_even * c - x_odd * s, x_even * s + x_odd * c], axis=-1)

        def _temporal_bias(L_q, L_kv):
            pos = jnp.arange(BIAS_LEN, dtype=jnp.float32)
            dist = jnp.abs(pos[None, :] - pos[:, None])
            bias = jnp.exp(-dist * 0.1) - dist * 0.05
            if L_q <= BIAS_LEN and L_kv <= BIAS_LEN:
                return bias[:L_q, :L_kv]
            return jax.image.resize(bias, (L_q, L_kv), method='bilinear')
        B, L_q, _ = decoder_hidden.shape
        L_kv = encoder_output.shape[1]
        residual = decoder_hidden
        q_in = _layernorm(decoder_hidden, gamma, beta)
        kv_in = _layernorm(encoder_output, gamma, beta)
        q = q_in @ Wqkv[:D_MODEL].T
        k = kv_in @ Wqkv[D_MODEL:2 * D_MODEL].T
        v = kv_in @ Wqkv[2 * D_MODEL:].T
        q = q.reshape(B, L_q, NUM_HEADS, HEAD_DIM).transpose(0, 2, 1, 3)
        k = k.reshape(B, L_kv, NUM_HEADS, HEAD_DIM).transpose(0, 2, 1, 3)
        v = v.reshape(B, L_kv, NUM_HEADS, HEAD_DIM).transpose(0, 2, 1, 3)
        L = max(L_q, L_kv)
        inv_freq = 1.0 / ROPE_BASE ** (jnp.arange(0, HEAD_DIM, 2, dtype=jnp.float32) / HEAD_DIM)
        freqs = jnp.arange(L, dtype=jnp.float32)[:, None] * inv_freq[None, :]
        cos, sin = (jnp.cos(freqs), jnp.sin(freqs))
        q = _rope(q, cos[:L_q], sin[:L_q])
        k = _rope(k, cos[:L_kv], sin[:L_kv])
        scores = jnp.einsum('bhqd,bhkd->bhqk', q, k) * SCALE
        scores = scores + _temporal_bias(L_q, L_kv)[None, None, :, :]
        attn = jax.nn.softmax(scores, axis=-1)
        attended = jnp.einsum('bhqk,bhkd->bhqd', attn, v)
        attended = attended.transpose(0, 2, 1, 3).reshape(B, L_q, D_MODEL)
        attended = attended @ Wout.T + b_out
        gate = jax.nn.sigmoid(attended @ Wgate.T + b_gate)
        output = gate * attended + (1.0 - gate) * residual
        return output

    def _L0_ffn_ref(x, w_router, b_router, w1, b1, w2, b2):
        import jax, jax.numpy as jnp
        import numpy as np
        B, T, D, F_FF, E, TOP_K = (8, 256, 128, 512, 8, 2)
        CAP_FACTOR = 1.25
        b, t, d = x.shape
        n = b * t
        e = w_router.shape[1]
        xf = x.reshape(n, d)
        logits = xf.astype(jnp.float32) @ w_router + b_router
        gates = jax.nn.softmax(logits, axis=-1)
        topv, topi = jax.lax.top_k(gates, TOP_K)
        cap = max(1, int(CAP_FACTOR * n / e))
        e_flat = topi.reshape(-1)
        g_flat = topv.reshape(-1)
        tok = jnp.repeat(jnp.arange(n), TOP_K)
        onehot = jax.nn.one_hot(e_flat, e, dtype=jnp.int32)
        pos = jnp.cumsum(onehot, axis=0)[jnp.arange(n * TOP_K), e_flat] - 1
        keep = pos < cap
        posc = jnp.minimum(pos, cap - 1)
        buf = jnp.zeros((e, cap, d), x.dtype).at[e_flat, posc].add(jnp.where(keep[:, None], xf[tok], 0.0))
        h = jax.nn.gelu(jnp.einsum('ecd,edf->ecf', buf, w1) + b1[:, None, :], approximate=False)
        out = jnp.einsum('ecf,efd->ecd', h, w2) + b2[:, None, :]
        og = out[e_flat, posc]
        w = jnp.where(keep, g_flat, 0.0).astype(x.dtype)
        y = jnp.zeros((n, d), x.dtype).at[tok].add(w[:, None] * og)
        ws = jnp.zeros((n,), x.dtype).at[tok].add(w)
        y = jnp.where((ws > 0.0)[:, None], y / jnp.maximum(ws, 1e-06)[:, None], y)
        return y.reshape(b, t, d)
    x = _layernorm(x + _L0_attn_ref(x, L0_attn_Wq, L0_attn_Wkv, L0_attn_Wproj), axis=-1)
    x = _layernorm(x + _L0_xattn_ref(x, ctx_1024, L0_xattn_Wqkv, L0_xattn_Wout, L0_xattn_b_out, L0_xattn_Wgate, L0_xattn_b_gate, L0_xattn_gamma, L0_xattn_beta), axis=-1)
    x = _layernorm(x + _L0_ffn_ref(x, L0_ffn_w_router, L0_ffn_b_router, L0_ffn_w1, L0_ffn_b1, L0_ffn_w2, L0_ffn_b2), axis=-1)
    return x

_drawn_inputs = setup_inputs


def setup_inputs(seed=0):
    import zlib

    import numpy as np

    out = dict(_drawn_inputs(seed))
    spreads = {'L0_xattn_b_out': (0.0, 0.1),
     'L0_xattn_b_gate': (0.0, 0.36),
     'L0_xattn_gamma': (1.0, 0.6),
     'L0_xattn_beta': (0.0, 0.8),
     'L0_ffn_b_router': (0.0, 0.1),
     'L0_ffn_b1': (0.0, 0.512),
     'L0_ffn_b2': (0.0, 0.1)}
    factors = {'ctx_1024': 4.24,
     'L0_attn_Wq': 8.0,
     'L0_attn_Wkv': 3.076,
     'L0_attn_Wproj': 3.325,
     'L0_xattn_Wqkv': 4.468,
     'L0_xattn_Wout': 4.233,
     'L0_xattn_Wgate': 7.873}
    for name, (base, spread) in spreads.items():
        noise = np.random.default_rng([zlib.crc32(name.encode()), seed]).standard_normal(out[name].shape)
        drawn = base * np.exp(spread * noise) if base else spread * noise
        out[name] = jnp.asarray(drawn.astype(out[name].dtype))
    for name, factor in factors.items():
        out[name] = (out[name] * factor).astype(out[name].dtype)
    return out
```

```python
from contextlib import ExitStack

import numpy as np

import concourse.bass as bass
from concourse import mybir

F32 = mybir.dt.float32
F32R = mybir.dt.float32r
U32 = mybir.dt.uint32
ALU = mybir.AluOpType
ACT = mybir.ActivationFunctionType
AX = mybir.AxisListType

B, T, D = 32, 56, 128
S = 1500
NH, HD = 16, 8
NKV = 4
N = B * T
TP = 2 * T
NT = N // TP
CH = 125
NC = S // CH
KB = 500
NB = S // KB
HQ = NH * T
HALF = HQ // 2
GH = 4
NG = NH // GH
GC = GH * T
VH = 2
NMX = HQ // 128
E, F, TOPK = 8, 512, 2
CAP = max(1, int(1.25 * N / E))
FT = F // 128
EPS_LN = 1e-5
EPS_NORM = 1e-6
BIAS_LEN = 128
HAT = 13

W_COLS = [("qk", D + NKV * HD), ("v", NKV * HD), ("proj", D), ("xq", D), ("xqp", D), ("xk", D), ("xkp", D),
          ("xv", D), ("out", D), ("gate", D), ("gamma", 1), ("beta", 1), ("b_out", D), ("b_gate", D),
          ("router", E), ("b_router", E)]
C_COLS = [("ident", 128), ("mask16", NH), ("mask4", GH), ("cosq", T), ("sinq", T), ("causal", T),
          ("cosa", HD), ("sina", HD), ("before", TP), ("ones", TP), ("iota", E)]


def columns(cols):
    at, out = 0, {}
    for name, n in cols:
        out[name] = (at, at + n)
        at += n
    return out, at


W_AT, W_N = columns(W_COLS)
C_AT, C_N = columns(C_COLS)


def strided(ap, dims, off=0):
    return bass.AP(ap.tensor, ap.offset + off, [list(ap.ap[0])] + [list(d) for d in dims])


def positive(eng, sem, value):
    if not isinstance(value, int) or value > 0:
        eng.wait_ge(sem, value)


class Own:

    def __init__(self, eng, sem):
        self.eng, self.sem, self.n = eng, sem, 0

    def mark(self, ins):
        ins.then_inc(self.sem, 1)
        self.n += 1

    def settle(self):
        self.eng.wait_ge(self.sem, self.n)

    def link(self, ins):
        self.mark(ins)
        self.settle()


class Core:

    def __init__(self, nc, ctx):
        self.nc, self.ctx = nc, ctx

    def sb(self, name, shape, dt=F32):
        return self.ctx.enter_context(self.nc.sbuf_tensor(name, shape, dt))

    def sem(self, name):
        return self.ctx.enter_context(self.nc.semaphore(name))


def layernorm_dve(own, rows, src, dst, stats, mv, rstd, std_wanted, std_done, signal=None):
    for t in range(NT):
        own.mark(own.eng.bn_stats(stats[0:rows, t, :], src[0:rows, t, :]))
    own.settle()
    for t in range(NT):
        own.mark(own.eng.bn_aggr(mv[0:rows, t, :], stats[0:rows, t, :]))
    own.settle()
    own.eng.tensor_scalar(rstd[0:rows, 0, :], mv[0:rows, :, 1], EPS_LN, None, ALU.add).then_inc(std_wanted, 1)
    own.eng.wait_ge(std_done[0], std_done[1])
    own.link(own.eng.reciprocal(rstd[0:rows, 1, :], rstd[0:rows, 0, :]))
    for t in range(NT):
        ins = own.eng.tensor_scalar(dst[0:rows, t, :], src[0:rows, t, :], mv[0:rows, t, 0:1],
                                    rstd[0:rows, 1, t:t + 1], ALU.subtract, ALU.mult)
        if signal is None:
            own.mark(ins)
        else:
            ins.then_inc(signal, 1)
    if signal is None:
        own.settle()


def self_attention(nc, psum, wt, ct, x1, xq_split, prep, ins):
    x_rows, x_cols, wpack, cpack = ins
    W = lambda n: wt[:, W_AT[n][0]:W_AT[n][1]]
    C = lambda n: ct[:, C_AT[n][0]:C_AT[n][1]]
    ident = C("ident")
    NQK = D + NKV * HD
    NHK = NH + NKV
    with ExitStack() as ctx:
        k = Core(nc, ctx)
        xT = k.sb("a_xT", [128, N])
        xr = k.sb("a_xr", [TP, NT, D])
        qk = k.sb("a_qk", [TP, NT, NQK])
        t1 = k.sb("a_t1", [TP, NT, NQK])
        t2 = k.sb("a_t2", [TP, NT, NQK])
        nrm = k.sb("a_nrm", [TP, 3, NT * NHK])
        qr = k.sb("a_qr", [TP, NT, D])
        kr = k.sb("a_kr", [TP, NT, D])
        vx = k.sb("a_vx", [T, B, NKV, 32])
        qT = k.sb("a_qT", [128, N])
        kT = k.sb("a_kT", [128, N])
        qbd = k.sb("a_qbd", [128, 2, NH, T])
        prob = k.sb("a_prob", [T, 3, HQ])
        oT = qT
        oAll = k.sb("a_o", [128, NKV, N])
        mv = k.sb("a_mv", [TP, NT, 2])
        stats = k.sb("a_stats", [TP, NT, 6])
        rstd = k.sb("a_rstd", [TP, 2, NT])

        got_x, got_w, got_r = k.sem("a_got_x"), k.sem("a_got_w"), k.sem("a_got_r")
        qk_made, v_made, qk_out = k.sem("a_qk_made"), k.sem("a_v_made"), k.sem("a_qk_out")
        own_v, own_a = k.sem("a_own_v"), k.sem("a_own_a")
        nrm_in, nrm_out = k.sem("a_nrm_in"), k.sem("a_nrm_out")
        qk_rot, qkT_made, qT_out, kT_out = (k.sem("a_qk_rot"), k.sem("a_qkT_made"), k.sem("a_qT_out"),
                                            k.sem("a_kT_out"))
        spread_v, spread_p = k.sem("a_spread_v"), k.sem("a_spread_p")
        s_made, e_made, masked, o_made, o_out = (k.sem("a_s_made"), k.sem("a_e_made"), k.sem("a_masked"),
                                                 k.sem("a_o_made"), k.sem("a_o_out"))
        oT_made, y_out, yT_made, yT_out, pr_made = (k.sem("a_oT_made"), k.sem("a_y_out"), k.sem("a_yT_made"),
                                                    k.sem("a_yT_out"), k.sem("a_pr_made"))
        std_in, std_out = k.sem("a_std_in"), k.sem("a_std_out")
        xn_made, xnT_made, xnT_out, q_made, q_split = (k.sem("a_xn_made"), k.sem("a_xnT_made"),
                                                       k.sem("a_xnT_out"), k.sem("a_q_made"), k.sem("a_q_split"))
        w_fold, bias_made, bias_out, q_stored = (k.sem("a_w_fold"), k.sem("a_bias_made"), k.sem("a_bias_out"),
                                                 k.sem("a_q_stored"))
        block = ctx.enter_context(nc.Block())

        yT, xnT = kT, xT
        y, res = t1, t2
        QK_BANK = 3

        @block.sync
        def _(sp):
            sp.dma_start(xT[:], x_cols).then_inc(got_x, 16)
            sp.dma_start(wt[:], wpack).then_inc(got_w, 16)
            sp.dma_start(ct[:], cpack).then_inc(got_w, 16)
            sp.dma_start(xr[:], x_rows.rearrange("(t p) d -> p t d", p=TP)).then_inc(got_r, 16)
            sp.wait_ge(q_split, 2)
            sp.dma_start(xq_split[0], kT[:].bitcast(F32)).then_inc(q_stored, 16)
            sp.dma_start(xq_split[1], oAll[:, 1, :].bitcast(F32)).then_inc(q_stored, 16)
            sp.wait_ge(q_stored, 32)

        @block.tensor
        def _(pe):
            pe.wait_ge(got_x, 16)
            pe.wait_ge(got_w, 32)
            for t in range(NT):
                mm = pe.matmul(psum[0:TP, t // QK_BANK, (t % QK_BANK) * NQK:(t % QK_BANK + 1) * NQK],
                               xT[:, t * TP:(t + 1) * TP], W("qk"), start=True, stop=True)
                if t % QK_BANK == QK_BANK - 1 or t == NT - 1:
                    mm.then_inc(qk_made, 1)
            for b in range(B):
                mm = pe.matmul(psum[0:T, 6 + b // 16, (b % 16) * 32:(b % 16) * 32 + 32],
                               xT[:, b * T:(b + 1) * T], W("v"), start=True, stop=True)
                if b % 16 == 15:
                    mm.then_inc(v_made, 1)
            pe.wait_ge(qk_out, 6)
            for n, name in enumerate(("xq", "xqp", "xk", "xkp")):
                pe.matmul(psum[:, 0, n:n + 1], W(name), W("beta"), start=True, stop=True)
            pe.wait_ge(w_fold, 1)
            pe.matmul(psum[0:TP, 1, 0:D], prep["beta_cols"][:, 0:TP], W("xv"), start=True, stop=True)\
              .then_inc(bias_made, 1)
            pe.wait_ge(qk_rot, 2)
            pe.wait_ge(bias_out, 2)
            for n, src in enumerate((qr, kr)):
                for t in range(NT):
                    mm = pe.transpose(psum[:, 4 * n + t // 4, (t % 4) * TP:(t % 4 + 1) * TP], src[:, t, :],
                                      ident[0:TP, 0:TP])
                    if t % 4 == 3:
                        mm.then_inc(qkT_made, 1)
            pe.wait_ge(kT_out, 4)
            pe.wait_ge(qT_out, 4)
            for b in range(B + 1):
                if b < B:
                    pe.wait_ge(spread_v if b % 2 == 0 else spread_p, b // 2 + 1)
                    if b >= 2:
                        pe.wait_ge(e_made, b - 1)
                    for h in range(2):
                        mm = pe.matmul(psum[0:T, 2 * (b % 2) + h, 0:HALF], kT[:, b * T:(b + 1) * T],
                                       qbd[:, b % 2, h * 8:(h + 1) * 8, :], start=True, stop=True)
                    mm.then_inc(s_made, 1)
                if b >= 1:
                    pe.wait_ge(masked, b)
                    if b >= 3:
                        pe.wait_ge(o_out, b - 2)
                    for g in range(NKV):
                        mm = pe.matmul(psum[32 * g:32 * g + 32, 4 + (b - 1) % 2, 0:GC], vx[:, b - 1, g, :],
                                       prob[:, (b - 1) % 3, g * GC:(g + 1) * GC], start=True, stop=True)
                    mm.then_inc(o_made, 1)
            pe.wait_ge(o_out, B)
            for t in range(NT):
                if t >= 4:
                    pe.wait_ge(y_out, t - 3)
                for l in range(GH):
                    mm = pe.transpose(psum[0:TP, t % 4, l * 128:(l + 1) * 128], oAll[:, l, t * TP:(t + 1) * TP],
                                      ident)
                mm.then_inc(oT_made, 1)
            for t in range(NT):
                pe.wait_ge(y_out, t + 1)
                mm = pe.transpose(psum[:, 4 + t // 4, (t % 4) * TP:(t % 4 + 1) * TP], y[:, t, 0:D],
                                  ident[0:TP, 0:TP])
                if t % 4 == 3:
                    mm.then_inc(yT_made, 1)
            for t in range(NT):
                pe.wait_ge(yT_out, t // 4 + 1)
                mm = pe.matmul(psum[0:TP, t // 4, (t % 4) * 128:(t % 4 + 1) * 128], yT[:, t * TP:(t + 1) * TP],
                               W("proj"), start=True, stop=True)
                if t % 4 == 3:
                    mm.then_inc(pr_made, 1)
            for t in range(NT):
                pe.wait_ge(xn_made, t + 1)
                mm = pe.transpose(psum[:, 4 + t // 4, (t % 4) * TP:(t % 4 + 1) * TP], y[:, t, 0:D],
                                  ident[0:TP, 0:TP])
                if t % 4 == 3:
                    mm.then_inc(xnT_made, 1)
            for n in range(4):
                pe.wait_ge(xnT_out, 4 if n == 0 else n + 1)
                pe.matmul(psum[:, n, 0:448], prep["xq"][:], xnT[:, n * 448:(n + 1) * 448], start=True, stop=True)
                pe.matmul(psum[:, 4 + n, 0:448], prep["xqp"][:], xnT[:, n * 448:(n + 1) * 448],
                          start=True, stop=True).then_inc(q_made, 1)

        @block.scalar
        def _(act):
            for n in range(6):
                act.wait_ge(qk_made, n + 1)
                m = min(QK_BANK, NT - QK_BANK * n)
                act.copy(qk[:, QK_BANK * n:QK_BANK * n + m, :],
                         psum[0:TP, n, 0:m * NQK].rearrange("p (t c) -> p t c", c=NQK)).then_inc(qk_out, 1)
            act.wait_ge(nrm_in, 1)
            act.activation(nrm[:, 1, :], nrm[:, 0, :], ACT.Sqrt).then_inc(nrm_out, 1)
            for n in range(4):
                act.wait_ge(qkT_made, n + 1)
                act.copy(qT[:, n * 448:(n + 1) * 448], psum[:, n, 0:448]).then_inc(qT_out, 1)
            for b in range(B + 1):
                if b < B:
                    act.wait_ge(s_made, b + 1)
                    if b >= 3:
                        act.wait_ge(o_made, b - 2)
                    act.activation(prob[:, b % 3, :].rearrange("p (a c) -> p a c", a=2),
                                   psum[0:T, 2 * (b % 2):2 * (b % 2) + 2, 0:HALF], ACT.Exp,
                                   scale=HD ** -0.5).then_inc(e_made, 1)
                if b >= 1:
                    act.wait_ge(o_made, b)
                    act.copy(oAll[:, :, (b - 1) * T:b * T],
                             psum[:, 4 + (b - 1) % 2, 0:GC].rearrange("p (l q) -> p l q", l=GH)).then_inc(o_out, 1)
            for n in range(4):
                act.wait_ge(yT_made, n + 1)
                act.copy(yT[:, n * 448:(n + 1) * 448], psum[:, 4 + n, 0:448]).then_inc(yT_out, 1)
            for n in range(2):
                act.wait_ge(std_in, n + 1)
                act.activation(rstd[:, 0, :], rstd[:, 0, :], ACT.Sqrt).then_inc(std_out, 1)
            for n in range(4):
                act.wait_ge(xnT_made, n + 1)
                act.copy(xnT[:, n * 448:(n + 1) * 448], psum[:, 4 + n, 0:448]).then_inc(xnT_out, 1)

        @block.vector
        def _(dve):
            own = Own(dve, own_v)
            own.mark(dve.memset(vx[:], 0.0))
            own.settle()
            own.link(dve.memset(vx[:, :, :, HD:HD + 1], 1.0))
            for n in range(2):
                dve.wait_ge(v_made, n + 1)
                own.mark(dve.tensor_copy(vx[:, 16 * n:16 * n + 16, :, 0:HD],
                                         psum[0:T, 6 + n, 0:512].rearrange("p (b g d) -> p b g d", b=16, g=NKV)))
            own.mark(dve.memset(prep["beta_cols"][:], 0.0))
            own.settle()
            dve.tensor_scalar(prep["beta_cols"][:], prep["beta_cols"][:], W("beta"), None, ALU.add)\
               .then_inc(w_fold, 1)
            for name in ("xq", "xqp", "xk", "xkp", "xv"):
                own.mark(dve.tensor_scalar(prep[name][:], W(name), W("gamma"), None, ALU.mult))
            dve.wait_ge(bias_made, 1)
            dve.tensor_copy(prep["off"][:], psum[:, 0, 0:4]).then_inc(bias_out, 1)
            dve.tensor_copy(prep["off_v"][:], psum[0:TP, 1, 0:D]).then_inc(bias_out, 1)
            dve.wait_ge(qk_out, 6)
            flat = lambda a: a[:].rearrange("p t c -> p (t c)")
            own.link(dve.tensor_tensor(flat(t1), flat(qk), flat(qk), ALU.mult))
            dve.tensor_reduce(nrm[:, 0, :], flat(t1).rearrange("p (h d) -> p h d", d=HD), AX.X, ALU.add)\
               .then_inc(nrm_in, 1)
            dve.wait_ge(nrm_out, 1)
            own.link(dve.tensor_scalar(nrm[:, 2, :], nrm[:, 1, :], EPS_NORM, None, ALU.add))
            own.link(dve.reciprocal(nrm[:, 0, :], nrm[:, 2, :]))
            own.link(dve.tensor_tensor(flat(qk).rearrange("p (h d) -> p h d", d=HD),
                                       flat(qk).rearrange("p (h d) -> p h d", d=HD),
                                       strided(nrm[:, 0, :], [[1, NT * NHK], [0, HD]]), ALU.mult))
            cosa, sina = C("cosa")[0:TP], C("sina")[0:TP]
            heads = lambda a: flat(a).rearrange("p (h d) -> p h d", d=HD)
            own.mark(dve.tensor_tensor(heads(t1), heads(qk), strided(cosa, [[0, NT * NHK], [1, HD]]), ALU.mult))
            for a in range(2):
                lo, hi = 4 * a, 4 - 4 * a
                own.mark(dve.tensor_tensor(heads(t2)[:, :, lo:lo + 4], heads(qk)[:, :, hi:hi + 4],
                                           strided(sina, [[0, NT * NHK], [1, 4]], lo), ALU.mult))
            own.settle()
            dve.tensor_tensor(qr[:], t1[:, :, 0:D], t2[:, :, 0:D], ALU.add).then_inc(qk_rot, 1)
            for g in range(NKV):
                lo = D + HD * g
                last = dve.tensor_tensor(
                    kr[:, :, 32 * g:32 * g + 32].rearrange("p t (r d) -> p t r d", r=GH),
                    strided(t1[:, :, lo:lo + HD], [[NQK, NT], [0, GH], [1, HD]]),
                    strided(t2[:, :, lo:lo + HD], [[NQK, NT], [0, GH], [1, HD]]), ALU.add)
            last.then_inc(qk_rot, 1)
            for n in range(4):
                dve.wait_ge(qkT_made, 4 + n + 1)
                dve.tensor_copy(kT[:, n * 448:(n + 1) * 448], psum[:, 4 + n, 0:448]).then_inc(kT_out, 1)
            dve.wait_ge(qT_out, 4)

            def mask(b):
                dve.wait_ge(e_made, b + 1)
                p = prob[:, b % 3, :].rearrange("p (h q) -> p h q", h=NH)
                dve.tensor_tensor(p, p, strided(C("causal")[0:T], [[0, NH], [1, T]]), ALU.mult).then_inc(masked, 1)

            for b in range(B + 1):
                if b < B and b % 2 == 0:
                    if b >= 2:
                        dve.wait_ge(s_made, b - 1)
                    dve.tensor_tensor(qbd[:, 0, :, :], strided(qT[:, b * T:(b + 1) * T], [[0, NH], [1, T]]),
                                      strided(C("mask16"), [[1, NH], [0, T]]), ALU.mult).then_inc(spread_v, 1)
                if b >= 1:
                    mask(b - 1)
            for t in range(NT):
                dve.wait_ge(oT_made, t + 1)
                o4 = psum[0:TP, t % 4, 0:512].rearrange("p (l g c) -> p l g c", l=GH, g=NKV)
                own.link(dve.reciprocal(nrm[:, t % 3, 0:16].rearrange("p (l g) -> p l g", l=GH), o4[:, :, :, HD]))
                dve.tensor_tensor(y[:, t, 0:D].rearrange("p (g l d) -> p l g d", g=NKV, l=GH), o4[:, :, :, 0:HD],
                                  strided(nrm[:, t % 3, 0:16], [[4, GH], [1, NKV], [0, HD]]), ALU.mult)\
                   .then_inc(y_out, 1)
            dve.wait_ge(got_r, 16)
            for n in range(4):
                dve.wait_ge(pr_made, n + 1)
                own.mark(dve.tensor_tensor(res[:, 4 * n:4 * n + 4, 0:D],
                                           psum[0:TP, n, 0:512].rearrange("p (t d) -> p t d", t=4),
                                           xr[:, 4 * n:4 * n + 4, :], ALU.add))
            own.settle()
            layernorm_dve(own, TP, res[:, :, 0:D], x1, stats, mv, rstd, std_in, (std_out, 1))
            dve.wait_ge(yT_made, 4)
            layernorm_dve(own, TP, x1, y[:, :, 0:D], stats, mv, rstd, std_in, (std_out, 2), xn_made)
            q = oAll[:, 0, :]
            for n in range(4):
                dve.wait_ge(q_made, n + 1)
                for m, tab in ((0, "cosq"), (1, "sinq")):
                    own.mark(dve.scalar_tensor_tensor(
                        out=oAll[:, 2 + m, n * 448:(n + 1) * 448].rearrange("p (b q) -> p b q", q=T),
                        in0=psum[:, 4 * m + n, 0:448].rearrange("p (b q) -> p b q", q=T),
                        scalar=prep["off"][:, m:m + 1], in1=strided(C(tab), [[0, 8], [1, T]]),
                        op0=ALU.add, op1=ALU.mult))
            own.settle()
            own.link(dve.tensor_tensor(q, oAll[:, 2, :], oAll[:, 3, :], ALU.add))
            hi = kT[:].bitcast(F32R)
            lo = oAll[:, 1, :].bitcast(F32R)
            dve.tensor_copy(hi, q).then_inc(q_split, 1)
            dve.wait_ge(q_split, 1)
            dve.tensor_tensor(lo, q, hi.bitcast(F32), ALU.subtract).then_inc(q_split, 1)

        @block.gpsimd
        def _(pool):
            pool.wait_ge(qT_out, 4)
            for b in range(1, B, 2):
                if b >= 3:
                    pool.wait_ge(s_made, b - 1)
                pool.tensor_tensor(qbd[:, 1, :, :], strided(qT[:, b * T:(b + 1) * T], [[0, NH], [1, T]]),
                                   strided(C("mask16"), [[1, NH], [0, T]]), ALU.mult).then_inc(spread_p, 1)


def cross_attention(nc, psum, wt, ct, xq_split, o_dram, prep, ins):
    ctx_in, rope, hats, nodes = ins
    C = lambda n: ct[:, C_AT[n][0]:C_AT[n][1]]
    ident = C("ident")
    VW = HD + 1
    VROW = NH * VW + 14
    NVG = NH // VH
    OC = VH * T
    with ExitStack() as ctx:
        k = Core(nc, ctx)
        xin = k.sb("b_xin", [CH, 2, NC, D])
        eps = k.sb("b_eps", [CH, 1])
        stats = k.sb("b_stats", [CH, NC, 6])
        mv = k.sb("b_mv", [CH, NC, 2])
        std = k.sb("b_std", [CH, NC])
        rstd = k.sb("b_rstd", [CH, NC])
        xT = k.sb("b_xT", [128, 2, S])
        tab = k.sb("b_tab", [128, 2, S])
        kt = k.sb("b_kt", [128, 2, 2, KB])
        k32 = k.sb("b_k32", [128, KB])
        khi = k.sb("b_khi", [128, 2, S], F32R)
        klo = k.sb("b_klo", [128, 2, S], F32R)
        stack = k.sb("b_stack", [128, 2, NG, S], F32R)
        hat = k.sb("b_hat", [128, S], F32R)
        node = k.sb("b_node", [128, NC, T], F32R)
        vx = k.sb("b_vx", [CH, 2, NC, VROW])
        qs = k.sb("b_qs", [96, 2, NG, T])
        qh = k.sb("b_qh", [128, 2, T])
        qstack = k.sb("b_qstack", [97, 2, NG, GC], F32R)
        qmax = k.sb("b_qmax", [128, 2, NH, T], F32R)
        prob = k.sb("b_prob", [CH, 3, HQ])
        mx = k.sb("b_mx", [128, NMX, NB])
        mx1 = k.sb("b_mx1", [128, NMX])
        mneg = k.sb("b_mneg", [NMX, 128], F32R)
        o_sb = k.sb("b_o", [128, 2, 2 * OC])

        ctx_got = [k.sem("b_ctx_even"), k.sem("b_ctx_odd")]
        q_got = [k.sem("b_q_even"), k.sem("b_q_odd")]
        stack_got = [k.sem("b_stack_even"), k.sem("b_stack_odd")]
        m_got = [k.sem("b_m_even"), k.sem("b_m_odd")]
        o_put = [k.sem("b_o_even"), k.sem("b_o_odd")]
        tab_got, hat_got, consts = k.sem("b_tab_got"), k.sem("b_hat_got"), k.sem("b_consts")
        stats_made, var_made, std_made, rstd_made, xn_made = (
            k.sem("b_stats_made"), k.sem("b_var"), k.sem("b_std_made"), k.sem("b_rstd_made"), k.sem("b_xn"))
        xT_made, xT_out, k_made, k_rot, k_sum, k_hi, k_split = (
            k.sem("b_xT_made"), k.sem("b_xT_out"), k.sem("b_k_made"), k.sem("b_k_rot"), k.sem("b_k_sum"),
            k.sem("b_k_hi"), k.sem("b_k_split"))
        v_made, v_out = k.sem("b_v_made"), k.sem("b_v_out")
        qm_made, qk_made = k.sem("b_qm_made"), k.sem("b_qk_made")
        g_made, g_red, g_max, gT_made, m_made = (k.sem("b_g_made"), k.sem("b_g_red"), k.sem("b_g_max"),
                                                 k.sem("b_gT_made"), k.sem("b_m_made"))
        s_made, e_made, pv_made, o_out = k.sem("b_s_made"), k.sem("b_e_made"), k.sem("b_pv_made"), k.sem("b_o_out")
        block = ctx.enter_context(nc.Block())

        BX, BK = 5, (6, 7)
        FIRST, LAST = 2, 27

        def periods(eng, period):
            for p in range(-3, FIRST):
                period(0, p)
            with eng.Fori(FIRST // 2, (LAST + 1) // 2) as i:
                period(i, 0)
                period(i, 1)
            for p in range(LAST + 1, B):
                period(0, p)

        def live(i, n):
            return not isinstance(i, int) or 0 <= n < B

        def seq(i, n):
            return 2 * i + n

        def pair(i, n):
            return i + n // 2

        @block.sync
        def _(sp):
            sp.dma_start(tab[:], rope).then_inc(tab_got, 16)
            sp.dma_start(xT[:, 0, :], hats).then_inc(hat_got, 16)
            sp.dma_start(xT[:, 1, 0:NC * T], nodes).then_inc(hat_got, 16)

            def period(i, p):
                n = p + 3
                if live(i, n):
                    positive(sp, xT_made, NB * (seq(i, n) - 1))
                    sp.dma_start(xin[:, n % 2, :, :], ctx_in[seq(i, n)].rearrange("(c p) d -> p c d", p=CH))\
                      .then_inc(ctx_got[n % 2], 16)
                n = p + 2
                if live(i, n):
                    positive(sp, qk_made, seq(i, n) - 1)
                    positive(sp, qm_made, seq(i, n) - 1)
                    src = xq_split.rearrange("s (g r) (b t) -> s r b g t", g=NG, t=T)
                    for row, part in ((0, 0), (1, 1), (2, 0)):
                        sp.dma_start(qs[32 * row:32 * row + 32, n % 2, :, :], src[part, :, seq(i, n)])\
                          .then_inc(q_got[n % 2], 16)
                    sp.dma_start(qh[:, n % 2, :], xq_split.rearrange("s r (b t) -> s b r t", t=T)[0, seq(i, n)])\
                      .then_inc(q_got[n % 2], 16)
                n = p + 1
                if live(i, n):
                    sp.wait_ge(consts, 5)
                    sp.wait_ge(k_split, NB * (seq(i, n) + 1))
                    positive(sp, s_made, NC * (seq(i, n) - 1))
                    for g in range(NG):
                        for row, part in ((0, khi), (1, khi), (2, klo)):
                            sp.dma_start(stack[32 * row:32 * row + 32, n % 2, g, :].bitcast(F32),
                                         part[32 * g:32 * g + 32, n % 2, :].bitcast(F32)).then_inc(stack_got[n % 2], 16)
                    sp.wait_ge(m_made, seq(i, n) + 1)
                    sp.dma_start(qstack[96:97, n % 2, :, :].rearrange("p g c -> p (g c)").bitcast(F32),
                                 mneg[:].bitcast(F32))\
                      .then_inc(m_got[n % 2], 16)
                n = p - 1
                if live(i, n):
                    sp.wait_ge(o_out, seq(i, n) + 1)
                    sp.dma_start(o_dram[pair(i, n), :, :, n % 2, :], o_sb[:, n % 2, :].rearrange("p (c t) -> p c t", t=T)).then_inc(o_put[n % 2], 16)

            periods(sp, period)
            sp.wait_ge(o_out, B)
            sp.dma_start(o_dram[NT - 1, :, :, 1, :], o_sb[:, 1, :].rearrange("p (c t) -> p c t", t=T)).then_inc(o_put[(B - 1) % 2], 16)
            for s in o_put:
                sp.wait_ge(s, 16 * B // 2)

        @block.tensor
        def _(pe):
            pe.wait_ge(consts, 5)

            def values(i, n, c):
                positive(pe, e_made, NC * seq(i, n) + c + 1)
                if c == 0:
                    pe.wait_ge(v_out, NB * (seq(i, n) + 1))
                    positive(pe, o_out, seq(i, n))
                for g in range(NVG):
                    j, cols = g % 4, OC
                    mm = pe.matmul(psum[32 * j:32 * j + 32, 4, (g // 4) * OC:(g // 4) * OC + cols],
                                   vx[:, n % 2, c, VH * VW * g:VH * VW * g + 32],
                                   prob[:, c % 3, OC * g:OC * g + cols],
                                   start=(c == 0 and g < 4), stop=(c == NC - 1), skip_group_check=True)
                mm.then_inc(pv_made, 1)

            def scores(i, n, c):
                if c == 0:
                    pe.wait_ge(stack_got[n % 2], 16 * 3 * NG * (pair(i, n) + 1))
                    pe.wait_ge(qk_made, seq(i, n) + 1)
                    pe.wait_ge(m_got[n % 2], 16 * (pair(i, n) + 1))
                positive(pe, e_made, NC * seq(i, n) + c - 1)
                for h in range(2):
                    bank = 2 * (c % 2) + h
                    pe.matmul(psum[0:CH, bank, 0:HALF], hat[:, c * CH:(c + 1) * CH],
                              strided(node[:, c, :], [[0, NH // 2], [1, T]]), start=True, stop=False,
                              skip_group_check=True)
                    for g in (2 * h, 2 * h + 1):
                        mm = pe.matmul(psum[0:CH, bank, GC * (g % 2):GC * (g % 2 + 1)],
                                       stack[0:97, n % 2, g, c * CH:(c + 1) * CH], qstack[0:97, n % 2, g, :],
                                       start=False, stop=True, skip_group_check=True)
                mm.then_inc(s_made, 1)

            def turn(i, n, r):
                if r == 0:
                    pe.wait_ge(xn_made, 2 * (seq(i, n) + 1))
                    positive(pe, v_out, NB * (seq(i, n) - 1))
                    positive(pe, m_made, seq(i, n) - 1)
                positive(pe, xT_out, NB * seq(i, n) + r)
                for c in range(4):
                    mm = pe.transpose(psum[:, BX, c * CH:(c + 1) * CH], xin[:, n % 2, 4 * r + c, :],
                                      ident[0:CH, 0:CH])
                mm.then_inc(xT_made, 1)

            def keys(i, n, r):
                pe.wait_ge(xT_out, NB * seq(i, n) + r + 1)
                if r == 0:
                    positive(pe, g_max, seq(i, n))
                positive(pe, k_rot, NB * seq(i, n) + r)
                for m, name in ((0, "xk"), (1, "xkp")):
                    mm = pe.matmul(psum[:, BK[m], 0:KB], prep[name][:], xT[:, n % 2, r * KB:(r + 1) * KB],
                                   start=True, stop=True)
                mm.then_inc(k_made, 1)

            def vals(i, n, r):
                if r == 0:
                    positive(pe, xT_out, NB * min(seq(i, n) + 2, B) if isinstance(i, int) else NB * (seq(i, n) + 2))
                positive(pe, v_out, NB * seq(i, n) + r)
                for c in range(4):
                    at = (4 * r + c) * CH
                    mm = pe.matmul(psum[0:CH, BX, c * D:(c + 1) * D], xT[:, n % 2, at:at + CH], prep["xv"][:],
                                   start=True, stop=True)
                mm.then_inc(v_made, 1)

            def maxima(i, n, j):
                r, m = divmod(j, NMX)
                if j == 0:
                    pe.wait_ge(qm_made, seq(i, n) + 1)
                    positive(pe, k_rot, NB * (seq(i, n) + 1))
                if m == 0:
                    pe.wait_ge(k_hi, NB * seq(i, n) + r + 1)
                positive(pe, g_red, NB * NMX * seq(i, n) + j - 1)
                pe.matmul(psum[:, BK[j % 2], 0:KB],
                          qmax[:, n % 2, :, :].rearrange("p h q -> p (h q)")[:, m * 128:(m + 1) * 128],
                          khi[:, n % 2, r * KB:(r + 1) * KB], start=True, stop=True).then_inc(g_made, 1)

            def period(i, p):
                for c in range(NC):
                    if live(i, p):
                        scores(i, p, c)
                    if c == 0 and live(i, p - 1):
                        values(i, p - 1, NC - 1)
                    if c > 0 and live(i, p):
                        values(i, p, c - 1)
                    if live(i, p + 1):
                        for j in range(c * NB * NMX // 9, min((c + 1) * NB * NMX // 9, NB * NMX)):
                            maxima(i, p + 1, j)
                        if 6 <= c < 9:
                            vals(i, p + 1, c - 6)
                        if c == 9:
                            pe.wait_ge(v_out, NB * (seq(i, p + 1) + 1))
                            pe.wait_ge(g_max, seq(i, p + 1) + 1)
                            pe.transpose(psum[0:NMX, BX, 0:128], mx1[:], ident).then_inc(gT_made, 1)
                    if live(i, p + 2):
                        if 3 <= c < 6:
                            turn(i, p + 2, c - 3)
                        if c >= 9:
                            keys(i, p + 2, c - 9)

            periods(pe, period)
            values(0, B - 1, NC - 1)

        @block.scalar
        def _(act):
            def out(i, n):
                act.wait_ge(pv_made, NC * (seq(i, n) + 1))
                positive(act, o_put[n % 2], 16 * pair(i, n))
                act.copy(o_sb[:, n % 2, :], psum[:, 4, 0:2 * OC]).then_inc(o_out, 1)

            def period(i, p):
                for c in range(NC):
                    if live(i, p):
                        act.wait_ge(s_made, NC * seq(i, p) + c + 1)
                        positive(act, pv_made, NC * seq(i, p) + c - 2)
                        act.activation(prob[:, c % 3, :].rearrange("p (a c) -> p a c", a=2),
                                       psum[0:CH, 2 * (c % 2):2 * (c % 2) + 2, 0:HALF], ACT.Exp).then_inc(e_made, 1)
                    if c == 0 and live(i, p - 1):
                        out(i, p - 1)
                    if c == 8 and live(i, p + 3):
                        act.wait_ge(var_made, NC * (seq(i, p + 3) + 1))
                        positive(act, rstd_made, seq(i, p + 3))
                        act.activation(std[:], mv[:, :, 1], ACT.Sqrt, bias=eps[:]).then_inc(std_made, 1)
                    if live(i, p + 2) and 3 <= c < 6:
                        r, n = c - 3, p + 2
                        act.wait_ge(xT_made, NB * seq(i, n) + r + 1)
                        act.copy(xT[:, n % 2, r * KB:(r + 1) * KB], psum[:, BX, 0:KB]).then_inc(xT_out, 1)
                    if live(i, p + 1) and 6 <= c < 9:
                        r, n = c - 6, p + 1
                        act.wait_ge(v_made, NB * seq(i, n) + r + 1)
                        act.copy(vx[:, n % 2, 4 * r:4 * r + 4, 0:NH * VW]
                                 .rearrange("p c (h d) -> p c h d", h=NH)[:, :, :, 0:HD],
                                 psum[0:CH, BX, 0:512].rearrange("p (c h d) -> p c h d", c=4, h=NH))\
                           .then_inc(v_out, 1)

            act.wait_ge(consts, 5)
            periods(act, period)
            out(0, B - 1)

        @block.vector
        def _(dve):
            dve.memset(vx[:], 1.0).then_inc(consts, 1)
            dve.memset(eps[:], EPS_LN).then_inc(consts, 1)
            dve.wait_ge(hat_got, 32)
            dve.tensor_copy(hat[:], xT[:, 0, :]).then_inc(consts, 1)
            dve.tensor_copy(node[:].rearrange("p c t -> p (c t)"), xT[:, 1, 0:NC * T])\
               .then_inc(consts, 1)
            dve.wait_ge(consts, 4)
            dve.memset(stack[96:97].bitcast(F32), 1.0).then_inc(consts, 1)

            def period(i, p):
                for j in range(NB * NMX):
                    n = p + 3
                    step = j // 2 if j % 2 and j // 2 <= NC // 2 and live(i, n) else None
                    if step == 0:
                        dve.wait_ge(ctx_got[n % 2], 16 * (pair(i, n) + 1))
                    elif step is not None:
                        dve.wait_ge(stats_made, NC * seq(i, n) + 2 * step)
                    if live(i, p + 1):
                        m = p + 1
                        dve.wait_ge(g_made, NB * NMX * seq(i, m) + j + 1)
                        dve.tensor_reduce(mx[:, j % NMX, j // NMX:j // NMX + 1], psum[:, BK[j % 2], 0:KB], AX.X,
                                          ALU.max).then_inc(g_red, 1)
                    if step == 0:
                        positive(dve, std_made, seq(i, n))
                        positive(dve, xn_made, 2 * seq(i, n))
                    if step is not None and step < NC // 2:
                        for c in (2 * step, 2 * step + 1):
                            dve.bn_stats(stats[:, c, :], xin[:, n % 2, c, :]).then_inc(stats_made, 1)
                    if step:
                        for c in (2 * step - 2, 2 * step - 1):
                            dve.bn_aggr(mv[:, c, :], stats[:, c, :]).then_inc(var_made, 1)
                n = p + 1
                if live(i, n):
                    dve.wait_ge(g_red, NB * NMX * (seq(i, n) + 1))
                    dve.tensor_reduce(mx1[:], mx[:], AX.X, ALU.max).then_inc(g_max, 1)
                n = p + 3
                if live(i, n):
                    dve.wait_ge(std_made, seq(i, n) + 1)
                    dve.reciprocal(rstd[:], std[:]).then_inc(rstd_made, 1)
                n = p + 1
                if live(i, n):
                    dve.wait_ge(gT_made, seq(i, n) + 1)
                    positive(dve, m_got[(n - 1) % 2], 16 * (pair(i, n - 1) + 1))
                    dve.tensor_scalar(mneg[:], psum[0:NMX, BX, 0:128], -1.0, None, ALU.mult).then_inc(m_made, 1)
                for r in range(NB):
                    n = p + 2
                    if live(i, n):
                        dve.wait_ge(k_made, NB * seq(i, n) + r + 1)
                        positive(dve, k_sum, NB * seq(i, n) + r - 1)
                        for m in range(2):
                            last = dve.scalar_tensor_tensor(
                                out=kt[:, (n * NB + r) % 2, m, :], in0=psum[:, BK[m], 0:KB],
                                scalar=prep["off"][:, 2 + m:3 + m], in1=tab[:, m, r * KB:(r + 1) * KB],
                                op0=ALU.add, op1=ALU.mult)
                        last.then_inc(k_rot, 1)
                    n = p + 3
                    if live(i, n) and r < 2:
                        dve.wait_ge(rstd_made, seq(i, n) + 1)
                        for c in range(r * NC // 2, (r + 1) * NC // 2):
                            last = dve.tensor_scalar(xin[:, n % 2, c, :], xin[:, n % 2, c, :], mv[:, c, 0:1],
                                                     rstd[:, c:c + 1], ALU.subtract, ALU.mult)
                        last.then_inc(xn_made, 1)

            dve.wait_ge(tab_got, 16)
            periods(dve, period)

        @block.gpsimd
        def _(pool):
            mask4 = C("mask4")
            pool.wait_ge(consts, 5)

            def spread_max(i, n):
                pool.wait_ge(q_got[n % 2], 64 * (pair(i, n) + 1))
                positive(pool, g_made, NB * NMX * (seq(i, n) - 1))
                pool.tensor_tensor(qmax[:, n % 2, :, :], strided(qh[:, n % 2, :], [[0, NH], [1, T]]),
                                   strided(C("mask16"), [[1, NH], [0, T]]), ALU.mult).then_inc(qm_made, 1)

            def period(i, p):
                n = p + 1
                if live(i, n):
                    positive(pool, s_made, NC * (seq(i, n) - 1))
                    pool.wait_ge(q_got[n % 2], 64 * (pair(i, n) + 1))
                    pool.tensor_tensor(qstack[0:96, n % 2, :, :].rearrange("p g (h q) -> p g h q", h=GH),
                                       strided(qs[:, n % 2, :, :], [[T, NG], [0, GH], [1, T]]),
                                       strided(mask4[0:96], [[0, NG], [1, GH], [0, T]]), ALU.mult)\
                        .then_inc(qk_made, 1)
                if live(i, p + 2):
                    spread_max(i, p + 2)
                n = p + 2
                if live(i, n):
                    for r in range(NB):
                        cols = slice(r * KB, (r + 1) * KB)
                        t = kt[:, (n * NB + r) % 2, :, :]
                        pool.wait_ge(k_rot, NB * seq(i, n) + r + 1)
                        if r == 0:
                            positive(pool, stack_got[n % 2], 16 * 3 * NG * pair(i, n))
                            positive(pool, g_made, NB * NMX * (seq(i, n) - 1))
                        positive(pool, k_split, NB * seq(i, n) + r)
                        pool.tensor_tensor(khi[:, n % 2, cols], t[:, 0, :], t[:, 1, :], ALU.add).then_inc(k_hi, 1)
                        pool.tensor_tensor(k32[:], t[:, 0, :], t[:, 1, :], ALU.add).then_inc(k_sum, 1)
                        pool.wait_ge(k_hi, NB * seq(i, n) + r + 1)
                        pool.wait_ge(k_sum, NB * seq(i, n) + r + 1)
                        pool.tensor_tensor(klo[:, n % 2, cols], k32[:], khi[:, n % 2, cols].bitcast(F32),
                                           ALU.subtract).then_inc(k_split, 1)

            periods(pool, period)


def mix_and_experts(nc, psum, wt, ct, x1, o_dram, prep, ins, out):
    w1, b1, w2, b2 = ins
    W = lambda n: wt[:, W_AT[n][0]:W_AT[n][1]]
    C = lambda n: ct[:, C_AT[n][0]:C_AT[n][1]]
    ident = C("ident")
    OC = VH * T
    VW = HD + 1
    SEG = N // 4
    TS = SEG // TP
    with ExitStack() as ctx:
        k = Core(nc, ctx)
        o = k.sb("c_o", [128, NT // 2, 2 * VH, TP])
        att = k.sb("c_att", [TP, NT, D])
        gated = k.sb("c_gated", [TP, NT, D])
        x2 = k.sb("c_x2", [TP, NT, D])
        cT = k.sb("c_cT", [128, N])
        x2T = k.sb("c_x2T", [128, N])
        rden = k.sb("c_rden", [TP, 2, NH])
        mv = k.sb("c_mv", [TP, NT, 2])
        stats = k.sb("c_stats", [TP, NT, 6])
        rstd = k.sb("c_rstd", [TP, 2, NT])
        rt = k.sb("c_rt", [TP, 6, NT, E])
        col = k.sb("c_col", [TP, 2, NT])
        top = k.sb("c_top", [TP, NT, 8])
        topi = k.sb("c_topi", [TP, NT, 8], U32)
        topf = k.sb("c_topf", [TP, NT, 8])
        wT = k.sb("c_wT", [E, NT, TP])
        w1s = k.sb("c_w1", [128, E, F])
        w2s = k.sb("c_w2", [128, E, FT, D])
        b1s = k.sb("c_b1", [128, E, FT])
        b2s = k.sb("c_b2", [E, D])
        hid = k.sb("c_hid", [128, 2, FT, SEG])
        y = att

        got_o, got_f = k.sem("c_got_o"), k.sem("c_got_f")
        own_v = k.sem("c_own_v")
        oT_made, att_out, aT_made, aT_out, w_made, a_out, cT_made, cT_out, g_made, g_out, sig_out = (
            k.sem("c_oT_made"), k.sem("c_att_out"), k.sem("c_aT_made"), k.sem("c_aT_out"), k.sem("c_w_made"),
            k.sem("c_a_out"), k.sem("c_cT_made"), k.sem("c_cT_out"), k.sem("c_g_made"), k.sem("c_g_out"),
            k.sem("c_sig_out"))
        std_in, std_out, x2_made, x2T_made, x2T_out, l_made = (
            k.sem("c_std_in"), k.sem("c_std_out"), k.sem("c_x2_made"), k.sem("c_x2T_made"), k.sem("c_x2T_out"),
            k.sem("c_l_made"))
        e_in, e_out, sel_made, p_made, rw_made, rT_made, rT_out, b_made, y_in = (
            k.sem("c_e_in"), k.sem("c_e_out"), k.sem("c_sel"), k.sem("c_p_made"), k.sem("c_rw"),
            k.sem("c_rT_made"), k.sem("c_rT_out"), k.sem("c_b_made"), k.sem("c_y_in"))
        h_made, h_out, y_made, y_out, fin, stored = (k.sem("c_h_made"), k.sem("c_h_out"), k.sem("c_y_made"),
                                                     k.sem("c_y_out"), k.sem("c_fin"), k.sem("c_stored"))
        block = ctx.enter_context(nc.Block())

        STEPS = [(e, s) for e in range(E) for s in range(4)]

        @block.sync
        def _(sp):
            for half in range(2):
                if half:
                    sp.wait_ge(oT_made, NT // 2)
                sp.dma_start(o[:].rearrange("p b c t -> p b (c t)"),
                             o_dram[half * (NT // 2):(half + 1) * (NT // 2)].rearrange("b p c s t -> p b (c s t)"))\
                  .then_inc(got_o, 16)
                if half == 0:
                    sp.dma_start(w1s[:], w1).then_inc(got_f, 16)
                    sp.dma_start(w2s[:], w2).then_inc(got_f, 16)
                    sp.dma_start(b1s[:], b1).then_inc(got_f, 16)
                    sp.dma_start(b2s[:], b2).then_inc(got_f, 16)
            sp.wait_ge(fin, NT)
            sp.dma_start(out.rearrange("(t p) d -> p t d", p=TP), gated[:]).then_inc(stored, 16)
            sp.wait_ge(stored, 16)

        def turn(pe, made, waited, src, rows, bank):
            for t in range(NT):
                pe.wait_ge(waited, t + 1)
                mm = pe.transpose(psum[:, bank + t // 4, (t % 4) * TP:(t % 4 + 1) * TP], src[:, t, :],
                                  ident[0:rows, 0:rows])
                if t % 4 == 3:
                    mm.then_inc(made, 1)

        def product(pe, made, ready, src, weights, bank):
            for t in range(NT):
                if t % 4 == 0:
                    pe.wait_ge(ready, t // 4 + 1)
                mm = pe.matmul(psum[0:TP, bank + t // 4, (t % 4) * D:(t % 4 + 1) * D], src[:, t * TP:(t + 1) * TP],
                               weights, start=True, stop=True)
                if t % 4 == 3:
                    mm.then_inc(made, 1)

        @block.tensor
        def _(pe):
            for t in range(NT):
                pe.wait_ge(got_o, 16 * (t // (NT // 2) + 1))
                if t >= 2:
                    pe.wait_ge(att_out, t - 1)
                b = t % (NT // 2)
                for l in range(2 * VH):
                    mm = pe.transpose(psum[0:TP, t % 2, l * 128:(l + 1) * 128], o[:, b, l, :], ident)
                mm.then_inc(oT_made, 1)
            turn(pe, aT_made, att_out, att, TP, 4)
            product(pe, w_made, aT_out, cT, W("out"), 0)
            turn(pe, cT_made, a_out, gated, TP, 4)
            product(pe, g_made, cT_out, cT, W("gate"), 0)
            turn(pe, x2T_made, x2_made, x2, TP, 4)
            pe.wait_ge(g_out, 4)
            for t in range(NT):
                pe.wait_ge(x2T_out, t // 4 + 1)
                mm = pe.matmul(psum[0:TP, 0, t * E:(t + 1) * E], x2T[:, t * TP:(t + 1) * TP], W("router"),
                               start=True, stop=True)
            mm.then_inc(l_made, 1)
            pe.wait_ge(sel_made, 1)
            pe.matmul(psum[0:TP, 1, 0:NT * E], C("before")[0:TP], rt[:, 2, :, :], start=True, stop=True)
            pe.matmul(psum[0:TP, 2, 0:NT * E], C("ones")[0:TP], rt[:, 2, :, :], start=True, stop=True)\
              .then_inc(p_made, 1)
            pe.wait_ge(rw_made, 1)
            for t in range(NT):
                mm = pe.transpose(psum[0:E, 3 + t // 4, (t % 4) * TP:(t % 4 + 1) * TP], rt[:, 5, t, :],
                                  ident[0:TP, 0:TP])
            mm.then_inc(rT_made, 1)
            pe.wait_ge(rT_out, 1)
            pe.wait_ge(got_f, 64)
            for t in range(NT):
                mm = pe.matmul(psum[0:TP, t // 4, (t % 4) * D:(t % 4 + 1) * D], wT[:, t, :], b2s[:],
                               start=True, stop=True)
            mm.then_inc(b_made, 1)
            pe.wait_ge(y_in, 1)
            for n in range(len(STEPS) + 1):
                if n < len(STEPS):
                    e, s = STEPS[n]
                    for f in range(FT):
                        if n >= 1:
                            pe.wait_ge(h_out, FT * (n - 1) + f + 1)
                        pe.matmul(psum[:, f, 0:SEG], w1s[:, e, f * 128:(f + 1) * 128], x2T[:, s * SEG:(s + 1) * SEG],
                                  start=True, stop=True).then_inc(h_made, 1)
                if n >= 1:
                    e, s = STEPS[n - 1]
                    pe.wait_ge(h_out, FT * n)
                    if n >= 3:
                        pe.wait_ge(y_out, TS * (n - 2))
                    for t in range(TS):
                        for f in range(FT):
                            mm = pe.matmul(psum[0:TP, 4 + n % 2, t * D:(t + 1) * D],
                                           hid[:, (n - 1) % 2, f, t * TP:(t + 1) * TP], w2s[:, e, f, :],
                                           start=(f == 0), stop=(f == FT - 1))
                    mm.then_inc(y_made, 1)

        @block.scalar
        def _(act):
            def evacuate(made, out_sem, dst):
                for n in range(4):
                    act.wait_ge(made, n + 1)
                    act.copy(dst[:, n * SEG:(n + 1) * SEG], psum[:, 4 + n, 0:SEG]).then_inc(out_sem, 1)

            evacuate(aT_made, aT_out, cT)
            act.wait_ge(w_made, 4)
            evacuate(cT_made, cT_out, cT)
            act.wait_ge(g_out, 4)
            act.activation(x2[:], x2[:], ACT.Sigmoid).then_inc(sig_out, 1)
            act.wait_ge(std_in, 1)
            act.activation(rstd[:, 0, :], rstd[:, 0, :], ACT.Sqrt).then_inc(std_out, 1)
            evacuate(x2T_made, x2T_out, x2T)
            act.wait_ge(e_in, 1)
            act.activation(rt[:, 1, :, :], rt[:, 0, :, :], ACT.Exp).then_inc(e_out, 1)
            act.wait_ge(rT_made, 1)
            act.copy(wT[:].rearrange("p (a t) c -> p a t c", a=4),
                     psum[0:E, 3:7, 0:SEG].rearrange("p a (t c) -> p a t c", c=TP)).then_inc(rT_out, 1)
            act.wait_ge(got_f, 64)
            for n, (e, s) in enumerate(STEPS):
                for f in range(FT):
                    act.wait_ge(h_made, FT * n + f + 1)
                    if n >= 2:
                        act.wait_ge(y_made, n - 1)
                    act.activation(hid[:, n % 2, f, :], psum[:, f, 0:SEG], ACT.Gelu, bias=b1s[:, e, f:f + 1])\
                       .then_inc(h_out, 1)
            act.wait_ge(std_in, 2)
            act.activation(rstd[:, 0, :], rstd[:, 0, :], ACT.Sqrt).then_inc(std_out, 1)

        @block.vector
        def _(dve):
            own = Own(dve, own_v)
            for t in range(NT):
                dve.wait_ge(oT_made, t + 1)
                for half in range(2):
                    p, at, first = psum[0:TP, t % 2, :], 256 * half, 8 * half
                    heads, spots = [[1, VH], [VH, 4]], [[128 + VW, VH], [32, 4]]
                    own.link(dve.reciprocal(strided(rden[:, t % 2, :], heads, first), strided(p, spots, at + HD)))
                    own.mark(dve.tensor_tensor(strided(att[:, t, :], [[HD, VH], [VH * HD, 4], [1, HD]], first * HD),
                                               strided(p, spots + [[1, HD]], at),
                                               strided(rden[:, t % 2, :], heads + [[0, HD]], first), ALU.mult))
                own.settle()
                dve.tensor_tensor(att[:, t, :], att[:, t, :], prep["off_v"][:], ALU.add).then_inc(att_out, 1)
            four = lambda a, n: a[:, 4 * n:4 * n + 4, :]
            rows = lambda name: strided(W(name)[0:TP], [[0, 4], [1, D]])
            bank4 = lambda n: psum[0:TP, n, 0:512].rearrange("p (t d) -> p t d", t=4)
            for n in range(4):
                dve.wait_ge(w_made, n + 1)
                dve.tensor_tensor(four(gated, n), bank4(n), rows("b_out"), ALU.add).then_inc(a_out, 4)
            for n in range(4):
                dve.wait_ge(g_made, n + 1)
                dve.tensor_tensor(four(x2, n), bank4(n), rows("b_gate"), ALU.add).then_inc(g_out, 1)
            own.mark(dve.tensor_tensor(gated[:], gated[:], x1[:], ALU.subtract))
            dve.wait_ge(sig_out, 1)
            own.settle()
            own.link(dve.tensor_tensor(gated[:], gated[:], x2[:], ALU.mult))
            own.link(dve.scalar_tensor_tensor(out=gated[:], in0=x1[:], scalar=2.0, in1=gated[:],
                                              op0=ALU.mult, op1=ALU.add))
            layernorm_dve(own, TP, gated, x2, stats, mv, rstd, std_in, (std_out, 1), x2_made)
            dve.wait_ge(l_made, 1)
            own.link(dve.tensor_tensor(rt[:, 3, :, :], psum[0:TP, 0, 0:NT * E].rearrange("p (t e) -> p t e", e=E),
                                       strided(W("b_router")[0:TP], [[0, NT], [1, E]]), ALU.add))
            own.link(dve.tensor_reduce(col[:, 0, :], rt[:, 3, :, :], AX.X, ALU.max))
            spread = lambda n: strided(col[:, n, :], [[1, NT], [0, E]])
            dve.tensor_tensor(rt[:, 0, :, :], rt[:, 3, :, :], spread(0), ALU.subtract).then_inc(e_in, 1)
            dve.wait_ge(e_out, 1)
            own.link(dve.tensor_reduce(col[:, 0, :], rt[:, 1, :, :], AX.X, ALU.add))
            own.link(dve.reciprocal(col[:, 1, :], col[:, 0, :]))
            own.link(dve.tensor_tensor(rt[:, 1, :, :], rt[:, 1, :, :], spread(1), ALU.mult))
            for t in range(NT):
                own.mark(dve.max(top[:, t, :], rt[:, 1, t, :]))
            own.settle()
            for t in range(NT):
                own.mark(dve.max_index(topi[:, t, :], top[:, t, :], rt[:, 1, t, :]))
            own.settle()
            own.link(dve.tensor_copy(topf[:], topi[:]))
            iota = strided(C("iota")[0:TP], [[0, NT], [1, E]])
            for n in range(TOPK):
                own.mark(dve.tensor_tensor(rt[:, 3 + n, :, :], iota, strided(topf[:, :, n:n + 1], [[8, NT], [0, E]]),
                                           ALU.is_equal))
            own.settle()
            dve.tensor_tensor(rt[:, 2, :, :], rt[:, 3, :, :], rt[:, 4, :, :], ALU.add).then_inc(sel_made, 1)
            dve.wait_ge(p_made, 1)
            own.link(dve.memset(rt[:, 3, 0, :], 0.0))
            own.link(dve.tensor_copy(rt[:, 4, :, :], psum[0:TP, 2, 0:NT * E].rearrange("p (t e) -> p t e", e=E)))
            for t in range(1, NT):
                own.link(dve.tensor_tensor(rt[:, 3, t, :], rt[:, 3, t - 1, :], rt[:, 4, t - 1, :], ALU.add))
            own.link(dve.tensor_tensor(rt[:, 4, :, :], psum[0:TP, 1, 0:NT * E].rearrange("p (t e) -> p t e", e=E),
                                       rt[:, 3, :, :], ALU.add))
            own.link(dve.scalar_tensor_tensor(out=rt[:, 3, :, :], in0=rt[:, 4, :, :], scalar=float(CAP),
                                              in1=rt[:, 2, :, :], op0=ALU.is_lt, op1=ALU.mult))
            own.link(dve.tensor_tensor(rt[:, 4, :, :], rt[:, 3, :, :], rt[:, 1, :, :], ALU.mult))
            own.link(dve.tensor_reduce(col[:, 0, :], rt[:, 4, :, :], AX.X, ALU.add))
            own.link(dve.tensor_scalar(col[:, 1, :], col[:, 0, :], 1e-6, None, ALU.max))
            own.link(dve.reciprocal(col[:, 0, :], col[:, 1, :]))
            dve.tensor_tensor(rt[:, 5, :, :], rt[:, 4, :, :], spread(0), ALU.mult).then_inc(rw_made, 1)
            dve.wait_ge(b_made, 1)
            for n in range(4):
                last = dve.tensor_tensor(four(y, n), bank4(n), four(x2, n), ALU.add)
            last.then_inc(y_in, 1)
            dve.wait_ge(y_in, 1)
            for n, (e, s) in enumerate(STEPS):
                dve.wait_ge(y_made, n + 1)
                if n >= 4:
                    dve.wait_ge(y_out, TS * (n - 3))
                for t in range(TS):
                    at = TS * s + t
                    dve.scalar_tensor_tensor(out=y[:, at, :], in0=psum[0:TP, 4 + (n + 1) % 2, t * D:(t + 1) * D],
                                             scalar=rt[:, 5, at, e:e + 1], in1=y[:, at, :],
                                             op0=ALU.mult, op1=ALU.add).then_inc(y_out, 1)
            dve.wait_ge(y_out, TS * len(STEPS))
            layernorm_dve(own, TP, y, gated, stats, mv, rstd, std_in, (std_out, 2), fin)


def decoder_layer(nc, x_rows, x_cols, ctx_in, wpack, cpack, rope, hats, nodes, w1, b1, w2, b2, out):
    xq_split = nc.dram_tensor("xq_split", [2, 128, N], F32, kind="Internal").ap()
    o_dram = nc.dram_tensor("o_sums", [NT, 128, 2 * VH, 2, T], F32, kind="Internal").ap()
    with ExitStack() as ctx:
        k = Core(nc, ctx)
        psum = ctx.enter_context(nc.psum_tensor("psum", [128, 8, 512], F32))
        wt = k.sb("wt", [128, W_N])
        ct = k.sb("ct", [128, C_N])
        x1 = k.sb("x1", [TP, NT, D])
        prep = {n: k.sb("w_" + n, [128, D]) for n in ("xq", "xqp", "xk", "xkp", "xv")}
        prep["beta_cols"] = k.sb("beta_cols", [128, TP])
        prep["off"] = k.sb("off", [128, 4])
        prep["off_v"] = k.sb("off_v", [TP, D])
        self_attention(nc, psum, wt, ct, x1, xq_split, prep, (x_rows, x_cols, wpack, cpack))
        cross_attention(nc, psum, wt, ct, xq_split, o_dram, prep, (ctx_in, rope, hats, nodes))
        mix_and_experts(nc, psum, wt, ct, x1, o_dram, prep, (w1, b1, w2, b2), out)


def resize_weights(n_in, n_out):
    step = n_in / n_out
    at = (np.arange(n_out) + 0.5) * step - 0.5
    w = np.maximum(0.0, 1.0 - np.abs(at[None, :] - np.arange(n_in)[:, None]) / max(step, 1.0))
    return w / w.sum(0, keepdims=True)


def rotary(positions, width):
    half = width // 2
    inv = (np.float32(1.0) / np.float32(10000.0) ** (np.arange(0, width, 2, dtype=np.float32) / np.float32(width)))
    ang = (np.arange(positions, dtype=np.float32)[:, None] * inv[None, :].astype(np.float32)).astype(np.float32)
    cos, sin = np.cos(ang.astype(np.float64)), np.sin(ang.astype(np.float64))
    return np.concatenate([cos, cos], 1), np.concatenate([-sin, sin], 1), half


def half_precision_pair(a):
    a = a.astype(np.float32)
    bits = a.view(np.uint32).astype(np.uint64)
    hi = ((bits + 0x800) & 0xFFFFF000).astype(np.uint32).view(np.float32)
    return hi, (a - hi).astype(np.float32)


def constants():
    c = np.zeros((128, C_N), np.float32)

    def put(name, a):
        lo, _ = C_AT[name]
        c[:a.shape[0], lo:lo + a.shape[1]] = a

    p = np.arange(128)
    put("ident", np.eye(128))
    put("mask16", (p[:, None] // HD == np.arange(NH)[None, :]) * 1.0)
    put("mask4", ((p[:, None] % 32) // HD == np.arange(GH)[None, :]) * 1.0)
    cq, sq, _ = rotary(T, HD)
    put("cosq", cq[:, p % HD].T * HD ** -0.5)
    put("sinq", sq[:, p % HD].T * HD ** -0.5)
    t = np.arange(T)
    put("causal", (t[:, None] <= t[None, :]) * 1.0)
    put("cosa", cq[np.arange(TP) % T])
    put("sina", sq[np.arange(TP) % T])
    put("before", (np.arange(TP)[:, None] < np.arange(TP)[None, :]) * 1.0)
    put("ones", np.ones((TP, TP)))
    put("iota", np.tile(np.arange(E), (128, 1)))
    ck, sk, _ = rotary(S, HD)
    rope = np.stack([ck[:, p % HD].T, sk[:, p % HD].T], 1).astype(np.float32)

    pos = np.arange(BIAS_LEN, dtype=np.float32)
    dist = np.abs(pos[None, :] - pos[:, None])
    bias = np.exp(-dist * np.float32(0.1)) - dist * np.float32(0.05)
    whole = 2 * S // 4
    hat = np.rint(resize_weights(BIAS_LEN, S) * whole)
    base = (bias.astype(np.float64) @ resize_weights(BIAS_LEN, T)) / whole
    hi, lo = half_precision_pair(base)
    hats = np.zeros((128, S), np.float32)
    nodes = np.zeros((128, NC, T), np.float32)
    for n in range(NC):
        cols = slice(n * CH, (n + 1) * CH)
        touched = np.nonzero(hat[:, cols].sum(1))[0]
        assert len(touched) <= HAT
        for r, j in enumerate(touched):
            for off, part in ((0, hi), (HAT, lo)):
                hats[off + r, cols] = hat[j, cols]
                nodes[off + r, n, :] = part[j]
    return c, rope, hats, nodes.reshape(128, NC * T)


def kernel(x, ctx_1024, L0_attn_Wq, L0_attn_Wkv, L0_attn_Wproj, L0_xattn_Wqkv, L0_xattn_Wout, L0_xattn_b_out,
           L0_xattn_Wgate, L0_xattn_b_gate, L0_xattn_gamma, L0_xattn_beta, L0_ffn_w_router, L0_ffn_b_router,
           L0_ffn_w1, L0_ffn_b1, L0_ffn_w2, L0_ffn_b2):
    import concourse.bacc as bacc
    from concourse.bass_utils import run_bass_kernel_spmd

    a = {n: np.asarray(v) for n, v in locals().items() if n[0] in "xcL" and not n.startswith("concourse")}
    x = a["x"].reshape(N, D)
    wqkv = a["L0_xattn_Wqkv"]
    partner = np.arange(D) // HD * HD + (np.arange(D) % HD + HD // 2) % HD
    wq, wk, wv = wqkv[:D], wqkv[D:2 * D], wqkv[2 * D:]
    rows = lambda v: np.broadcast_to(v[None, :], (128, v.shape[0]))
    wpack = np.concatenate(
        [a["L0_attn_Wq"].T, a["L0_attn_Wkv"].T, a["L0_attn_Wproj"].T, wq.T, wq[partner].T, wk.T, wk[partner].T,
         wv.T, a["L0_xattn_Wout"].T, a["L0_xattn_Wgate"].T, a["L0_xattn_gamma"][:, None],
         a["L0_xattn_beta"][:, None], rows(a["L0_xattn_b_out"]), rows(a["L0_xattn_b_gate"]),
         a["L0_ffn_w_router"], rows(a["L0_ffn_b_router"])], axis=1)
    cpack, rope, hats, nodes = constants()
    arrays = {
        "x_rows": x, "x_cols": x.T, "ctx_in": a["ctx_1024"], "wpack": wpack, "cpack": cpack, "rope": rope,
        "hats": hats, "nodes": nodes,
        "w1": a["L0_ffn_w1"].transpose(1, 0, 2),
        "b1": a["L0_ffn_b1"].reshape(E, FT, 128).transpose(2, 0, 1),
        "w2": a["L0_ffn_w2"].reshape(E, FT, 128, D).transpose(2, 0, 1, 3),
        "b2": a["L0_ffn_b2"],
    }
    arrays = {n: np.ascontiguousarray(v) for n, v in arrays.items()}
    nc = bacc.Bacc("TRN2", target_bir_lowering=False, num_devices=1)
    args = [nc.dram_tensor(n, v.shape, F32, kind="ExternalInput").ap() for n, v in arrays.items()]
    out = nc.dram_tensor("out", (N, D), F32, kind="ExternalOutput").ap()
    decoder_layer(nc, *args, out)
    r = run_bass_kernel_spmd(nc, [arrays], core_ids=[0])
    return r.results[0]["out"].reshape(B, T, D)
```

```python
from contextlib import ExitStack

import numpy as np

import concourse.bass as bass
from concourse import mybir

F32 = mybir.dt.float32
F32R = mybir.dt.float32r
U32 = mybir.dt.uint32
ALU = mybir.AluOpType
ACT = mybir.ActivationFunctionType
AX = mybir.AxisListType

B, T, D = 32, 56, 128
S = 1500
NH, HD = 16, 8
NKV = 4
N = B * T
TP = 2 * T
NT = N // TP
CH = 125
NC = S // CH
KB = 500
NB = S // KB
HQ = NH * T
HALF = HQ // 2
GH = 4
NG = NH // GH
GC = GH * T
VH = 2
NMX = HQ // 128
E, F, TOPK = 8, 512, 2
CAP = max(1, int(1.25 * N / E))
SLOTS = E * CAP
NQ = SLOTS // TP
FAR = 2 * SLOTS
FT = F // 128
EPS_LN = 1e-5
EPS_NORM = 1e-6
BIAS_LEN = 128
HAT = 13
QC = 3
CQ = NC // QC
BQ = NC // 4

W_COLS = [("qk", D + NKV * HD), ("v", NKV * HD), ("proj", D), ("xq", D), ("xqp", D), ("xk", D), ("xkp", D),
          ("xv", D), ("out", D), ("gate", D), ("gamma", 1), ("beta", 1), ("b_out", D), ("b_gate", D),
          ("router", E), ("b_router", E)]
C_COLS = [("ident", 128), ("mask16", NH), ("mask4", GH), ("cosq", T), ("sinq", T), ("causal", T),
          ("cosa", HD), ("sina", HD), ("before", TP), ("ones", TP), ("iota", E), ("slot", E)]


def columns(cols):
    at, out = 0, {}
    for name, n in cols:
        out[name] = (at, at + n)
        at += n
    return out, at


W_AT, W_N = columns(W_COLS)
C_AT, C_N = columns(C_COLS)


def strided(ap, dims, off=0):
    return bass.AP(ap.tensor, ap.offset + off, [list(ap.ap[0])] + [list(d) for d in dims])


def positive(eng, sem, value):
    if not isinstance(value, int) or value > 0:
        eng.wait_ge(sem, value)


class Own:

    def __init__(self, eng, sem):
        self.eng, self.sem, self.n = eng, sem, 0

    def mark(self, ins):
        ins.then_inc(self.sem, 1)
        self.n += 1

    def settle(self):
        self.eng.wait_ge(self.sem, self.n)

    def link(self, ins):
        self.mark(ins)
        self.settle()


class Core:

    def __init__(self, nc, ctx):
        self.nc, self.ctx = nc, ctx

    def sb(self, name, shape, dt=F32):
        return self.ctx.enter_context(self.nc.sbuf_tensor(name, shape, dt))

    def sem(self, name):
        return self.ctx.enter_context(self.nc.semaphore(name))


def layernorm_dve(own, rows, src, dst, stats, mv, rstd, std_wanted, std_done, signal=None):
    for t in range(NT):
        own.mark(own.eng.bn_stats(stats[0:rows, t, :], src[0:rows, t, :]))
    own.settle()
    for t in range(NT):
        own.mark(own.eng.bn_aggr(mv[0:rows, t, :], stats[0:rows, t, :]))
    own.settle()
    own.eng.tensor_scalar(rstd[0:rows, 0, :], mv[0:rows, :, 1], EPS_LN, None, ALU.add).then_inc(std_wanted, 1)
    own.eng.wait_ge(std_done[0], std_done[1])
    own.link(own.eng.reciprocal(rstd[0:rows, 1, :], rstd[0:rows, 0, :]))
    for t in range(NT):
        ins = own.eng.tensor_scalar(dst[0:rows, t, :], src[0:rows, t, :], mv[0:rows, t, 0:1],
                                    rstd[0:rows, 1, t:t + 1], ALU.subtract, ALU.mult)
        if signal is None:
            own.mark(ins)
        else:
            ins.then_inc(signal, 1)
    if signal is None:
        own.settle()


def self_attention(nc, psum, wt, ct, x1, xq_split, prep, ins):
    x_rows, x_cols, wpack, cpack = ins
    W = lambda n: wt[:, W_AT[n][0]:W_AT[n][1]]
    C = lambda n: ct[:, C_AT[n][0]:C_AT[n][1]]
    ident = C("ident")
    NQK = D + NKV * HD
    NHK = NH + NKV
    with ExitStack() as ctx:
        k = Core(nc, ctx)
        xT = k.sb("a_xT", [128, N])
        xr = k.sb("a_xr", [TP, NT, D])
        qk = k.sb("a_qk", [TP, NT, NQK])
        t1 = k.sb("a_t1", [TP, NT, NQK])
        t2 = k.sb("a_t2", [TP, NT, NQK])
        nrm = k.sb("a_nrm", [TP, 3, NT * NHK])
        qr = k.sb("a_qr", [TP, NT, D])
        kr = k.sb("a_kr", [TP, NT, D])
        vx = k.sb("a_vx", [T, B, NKV, 32])
        qT = k.sb("a_qT", [128, N])
        kT = k.sb("a_kT", [128, N])
        qbd = k.sb("a_qbd", [128, 2, NH, T])
        prob = k.sb("a_prob", [T, 3, HQ])
        oT = qT
        oAll = k.sb("a_o", [128, NKV, N])
        mv = k.sb("a_mv", [TP, NT, 2])
        stats = k.sb("a_stats", [TP, NT, 6])
        rstd = k.sb("a_rstd", [TP, 2, NT])

        got_x, got_w, got_r = k.sem("a_got_x"), k.sem("a_got_w"), k.sem("a_got_r")
        qk_made, v_made, qk_out = k.sem("a_qk_made"), k.sem("a_v_made"), k.sem("a_qk_out")
        own_v, own_a = k.sem("a_own_v"), k.sem("a_own_a")
        nrm_in, nrm_out = k.sem("a_nrm_in"), k.sem("a_nrm_out")
        qk_rot, qkT_made, qT_out, kT_out = (k.sem("a_qk_rot"), k.sem("a_qkT_made"), k.sem("a_qT_out"),
                                            k.sem("a_kT_out"))
        spread_v, spread_p = k.sem("a_spread_v"), k.sem("a_spread_p")
        s_made, e_made, masked, o_made, o_out = (k.sem("a_s_made"), k.sem("a_e_made"), k.sem("a_masked"),
                                                 k.sem("a_o_made"), k.sem("a_o_out"))
        oT_made, y_out, yT_made, yT_out, pr_made = (k.sem("a_oT_made"), k.sem("a_y_out"), k.sem("a_yT_made"),
                                                    k.sem("a_yT_out"), k.sem("a_pr_made"))
        std_in, std_out = k.sem("a_std_in"), k.sem("a_std_out")
        xn_made, xnT_made, xnT_out, q_made, q_split = (k.sem("a_xn_made"), k.sem("a_xnT_made"),
                                                       k.sem("a_xnT_out"), k.sem("a_q_made"), k.sem("a_q_split"))
        w_fold, bias_made, bias_out, q_stored = (k.sem("a_w_fold"), k.sem("a_bias_made"), k.sem("a_bias_out"),
                                                 k.sem("a_q_stored"))
        block = ctx.enter_context(nc.Block())

        yT, xnT = kT, xT
        y, res = t1, t2
        QK_BANK = 3

        @block.sync
        def _(sp):
            sp.dma_start(xT[:], x_cols).then_inc(got_x, 16)
            sp.dma_start(wt[:], wpack).then_inc(got_w, 16)
            sp.dma_start(ct[:], cpack).then_inc(got_w, 16)
            sp.dma_start(xr[:], x_rows.rearrange("(t p) d -> p t d", p=TP)).then_inc(got_r, 16)
            sp.wait_ge(q_split, 2)
            sp.dma_start(xq_split[0], kT[:].bitcast(F32)).then_inc(q_stored, 16)
            sp.dma_start(xq_split[1], oAll[:, 1, :].bitcast(F32)).then_inc(q_stored, 16)
            sp.wait_ge(q_stored, 32)

        @block.tensor
        def _(pe):
            pe.wait_ge(got_x, 16)
            pe.wait_ge(got_w, 32)
            for t in range(NT):
                mm = pe.matmul(psum[0:TP, t // QK_BANK, (t % QK_BANK) * NQK:(t % QK_BANK + 1) * NQK],
                               xT[:, t * TP:(t + 1) * TP], W("qk"), start=True, stop=True)
                if t % QK_BANK == QK_BANK - 1 or t == NT - 1:
                    mm.then_inc(qk_made, 1)
            for b in range(B):
                mm = pe.matmul(psum[0:T, 6 + b // 16, (b % 16) * 32:(b % 16) * 32 + 32],
                               xT[:, b * T:(b + 1) * T], W("v"), start=True, stop=True)
                if b % 16 == 15:
                    mm.then_inc(v_made, 1)
            pe.wait_ge(qk_out, 6)
            for n, name in enumerate(("xq", "xqp", "xk", "xkp")):
                pe.matmul(psum[:, 0, n:n + 1], W(name), W("beta"), start=True, stop=True)
            pe.wait_ge(w_fold, 1)
            pe.matmul(psum[0:TP, 1, 0:D], prep["beta_cols"][:, 0:TP], W("xv"), start=True, stop=True)\
              .then_inc(bias_made, 1)
            pe.wait_ge(qk_rot, 2)
            pe.wait_ge(bias_out, 2)
            for n, src in enumerate((qr, kr)):
                for t in range(NT):
                    mm = pe.transpose(psum[:, 4 * n + t // 4, (t % 4) * TP:(t % 4 + 1) * TP], src[:, t, :],
                                      ident[0:TP, 0:TP])
                    if t % 4 == 3:
                        mm.then_inc(qkT_made, 1)
            pe.wait_ge(kT_out, 4)
            pe.wait_ge(qT_out, 4)
            for b in range(B + 1):
                if b < B:
                    pe.wait_ge(spread_v if b % 2 == 0 else spread_p, b // 2 + 1)
                    if b >= 2:
                        pe.wait_ge(e_made, b - 1)
                    for h in range(2):
                        mm = pe.matmul(psum[0:T, 2 * (b % 2) + h, 0:HALF], kT[:, b * T:(b + 1) * T],
                                       qbd[:, b % 2, h * 8:(h + 1) * 8, :], start=True, stop=True)
                    mm.then_inc(s_made, 1)
                if b >= 1:
                    pe.wait_ge(masked, b)
                    if b >= 3:
                        pe.wait_ge(o_out, b - 2)
                    for g in range(NKV):
                        mm = pe.matmul(psum[32 * g:32 * g + 32, 4 + (b - 1) % 2, 0:GC], vx[:, b - 1, g, :],
                                       prob[:, (b - 1) % 3, g * GC:(g + 1) * GC], start=True, stop=True)
                    mm.then_inc(o_made, 1)
            pe.wait_ge(o_out, B)
            for t in range(NT):
                if t >= 4:
                    pe.wait_ge(y_out, t - 3)
                for l in range(GH):
                    mm = pe.transpose(psum[0:TP, t % 4, l * 128:(l + 1) * 128], oAll[:, l, t * TP:(t + 1) * TP],
                                      ident)
                mm.then_inc(oT_made, 1)
            for t in range(NT):
                pe.wait_ge(y_out, t + 1)
                mm = pe.transpose(psum[:, 4 + t // 4, (t % 4) * TP:(t % 4 + 1) * TP], y[:, t, 0:D],
                                  ident[0:TP, 0:TP])
                if t % 4 == 3:
                    mm.then_inc(yT_made, 1)
            for t in range(NT):
                pe.wait_ge(yT_out, t // 4 + 1)
                mm = pe.matmul(psum[0:TP, t // 4, (t % 4) * 128:(t % 4 + 1) * 128], yT[:, t * TP:(t + 1) * TP],
                               W("proj"), start=True, stop=True)
                if t % 4 == 3:
                    mm.then_inc(pr_made, 1)
            for t in range(NT):
                pe.wait_ge(xn_made, t + 1)
                mm = pe.transpose(psum[:, 4 + t // 4, (t % 4) * TP:(t % 4 + 1) * TP], y[:, t, 0:D],
                                  ident[0:TP, 0:TP])
                if t % 4 == 3:
                    mm.then_inc(xnT_made, 1)
            for n in range(4):
                pe.wait_ge(xnT_out, 4 if n == 0 else n + 1)
                pe.matmul(psum[:, n, 0:448], prep["xq"][:], xnT[:, n * 448:(n + 1) * 448], start=True, stop=True)
                pe.matmul(psum[:, 4 + n, 0:448], prep["xqp"][:], xnT[:, n * 448:(n + 1) * 448],
                          start=True, stop=True).then_inc(q_made, 1)

        @block.scalar
        def _(act):
            for n in range(6):
                act.wait_ge(qk_made, n + 1)
                m = min(QK_BANK, NT - QK_BANK * n)
                act.copy(qk[:, QK_BANK * n:QK_BANK * n + m, :],
                         psum[0:TP, n, 0:m * NQK].rearrange("p (t c) -> p t c", c=NQK)).then_inc(qk_out, 1)
            act.wait_ge(nrm_in, 1)
            act.activation(nrm[:, 1, :], nrm[:, 0, :], ACT.Sqrt).then_inc(nrm_out, 1)
            for n in range(4):
                act.wait_ge(qkT_made, n + 1)
                act.copy(qT[:, n * 448:(n + 1) * 448], psum[:, n, 0:448]).then_inc(qT_out, 1)
            for b in range(B + 1):
                if b < B:
                    act.wait_ge(s_made, b + 1)
                    if b >= 3:
                        act.wait_ge(o_made, b - 2)
                    act.activation(prob[:, b % 3, :].rearrange("p (a c) -> p a c", a=2),
                                   psum[0:T, 2 * (b % 2):2 * (b % 2) + 2, 0:HALF], ACT.Exp,
                                   scale=HD ** -0.5).then_inc(e_made, 1)
                if b >= 1:
                    act.wait_ge(o_made, b)
                    act.copy(oAll[:, :, (b - 1) * T:b * T],
                             psum[:, 4 + (b - 1) % 2, 0:GC].rearrange("p (l q) -> p l q", l=GH)).then_inc(o_out, 1)
            for n in range(4):
                act.wait_ge(yT_made, n + 1)
                act.copy(yT[:, n * 448:(n + 1) * 448], psum[:, 4 + n, 0:448]).then_inc(yT_out, 1)
            for n in range(2):
                act.wait_ge(std_in, n + 1)
                act.activation(rstd[:, 0, :], rstd[:, 0, :], ACT.Sqrt).then_inc(std_out, 1)
            for n in range(4):
                act.wait_ge(xnT_made, n + 1)
                act.copy(xnT[:, n * 448:(n + 1) * 448], psum[:, 4 + n, 0:448]).then_inc(xnT_out, 1)

        @block.vector
        def _(dve):
            own = Own(dve, own_v)
            own.mark(dve.memset(vx[:], 0.0))
            own.settle()
            own.link(dve.memset(vx[:, :, :, HD:HD + 1], 1.0))
            for n in range(2):
                dve.wait_ge(v_made, n + 1)
                own.mark(dve.tensor_copy(vx[:, 16 * n:16 * n + 16, :, 0:HD],
                                         psum[0:T, 6 + n, 0:512].rearrange("p (b g d) -> p b g d", b=16, g=NKV)))
            own.mark(dve.memset(prep["beta_cols"][:], 0.0))
            own.settle()
            dve.tensor_scalar(prep["beta_cols"][:], prep["beta_cols"][:], W("beta"), None, ALU.add)\
               .then_inc(w_fold, 1)
            for name in ("xq", "xqp", "xk", "xkp", "xv"):
                own.mark(dve.tensor_scalar(prep[name][:], W(name), W("gamma"), None, ALU.mult))
            dve.wait_ge(bias_made, 1)
            dve.tensor_copy(prep["off"][:], psum[:, 0, 0:4]).then_inc(bias_out, 1)
            dve.tensor_copy(prep["off_v"][:], psum[0:TP, 1, 0:D]).then_inc(bias_out, 1)
            dve.wait_ge(qk_out, 6)
            flat = lambda a: a[:].rearrange("p t c -> p (t c)")
            own.link(dve.tensor_tensor(flat(t1), flat(qk), flat(qk), ALU.mult))
            dve.tensor_reduce(nrm[:, 0, :], flat(t1).rearrange("p (h d) -> p h d", d=HD), AX.X, ALU.add)\
               .then_inc(nrm_in, 1)
            dve.wait_ge(nrm_out, 1)
            own.link(dve.tensor_scalar(nrm[:, 2, :], nrm[:, 1, :], EPS_NORM, None, ALU.add))
            own.link(dve.reciprocal(nrm[:, 0, :], nrm[:, 2, :]))
            own.link(dve.tensor_tensor(flat(qk).rearrange("p (h d) -> p h d", d=HD),
                                       flat(qk).rearrange("p (h d) -> p h d", d=HD),
                                       strided(nrm[:, 0, :], [[1, NT * NHK], [0, HD]]), ALU.mult))
            cosa, sina = C("cosa")[0:TP], C("sina")[0:TP]
            heads = lambda a: flat(a).rearrange("p (h d) -> p h d", d=HD)
            own.mark(dve.tensor_tensor(heads(t1), heads(qk), strided(cosa, [[0, NT * NHK], [1, HD]]), ALU.mult))
            for a in range(2):
                lo, hi = 4 * a, 4 - 4 * a
                own.mark(dve.tensor_tensor(heads(t2)[:, :, lo:lo + 4], heads(qk)[:, :, hi:hi + 4],
                                           strided(sina, [[0, NT * NHK], [1, 4]], lo), ALU.mult))
            own.settle()
            dve.tensor_tensor(qr[:], t1[:, :, 0:D], t2[:, :, 0:D], ALU.add).then_inc(qk_rot, 1)
            for g in range(NKV):
                lo = D + HD * g
                last = dve.tensor_tensor(
                    kr[:, :, 32 * g:32 * g + 32].rearrange("p t (r d) -> p t r d", r=GH),
                    strided(t1[:, :, lo:lo + HD], [[NQK, NT], [0, GH], [1, HD]]),
                    strided(t2[:, :, lo:lo + HD], [[NQK, NT], [0, GH], [1, HD]]), ALU.add)
            last.then_inc(qk_rot, 1)
            for n in range(4):
                dve.wait_ge(qkT_made, 4 + n + 1)
                dve.tensor_copy(kT[:, n * 448:(n + 1) * 448], psum[:, 4 + n, 0:448]).then_inc(kT_out, 1)
            dve.wait_ge(qT_out, 4)

            def mask(b):
                dve.wait_ge(e_made, b + 1)
                p = prob[:, b % 3, :].rearrange("p (h q) -> p h q", h=NH)
                dve.tensor_tensor(p, p, strided(C("causal")[0:T], [[0, NH], [1, T]]), ALU.mult).then_inc(masked, 1)

            for b in range(B + 1):
                if b < B and b % 2 == 0:
                    if b >= 2:
                        dve.wait_ge(s_made, b - 1)
                    dve.tensor_tensor(qbd[:, 0, :, :], strided(qT[:, b * T:(b + 1) * T], [[0, NH], [1, T]]),
                                      strided(C("mask16"), [[1, NH], [0, T]]), ALU.mult).then_inc(spread_v, 1)
                if b >= 1:
                    mask(b - 1)
            for t in range(NT):
                dve.wait_ge(oT_made, t + 1)
                o4 = psum[0:TP, t % 4, 0:512].rearrange("p (l g c) -> p l g c", l=GH, g=NKV)
                own.link(dve.reciprocal(nrm[:, t % 3, 0:16].rearrange("p (l g) -> p l g", l=GH), o4[:, :, :, HD]))
                dve.tensor_tensor(y[:, t, 0:D].rearrange("p (g l d) -> p l g d", g=NKV, l=GH), o4[:, :, :, 0:HD],
                                  strided(nrm[:, t % 3, 0:16], [[4, GH], [1, NKV], [0, HD]]), ALU.mult)\
                   .then_inc(y_out, 1)
            dve.wait_ge(got_r, 16)
            for n in range(4):
                dve.wait_ge(pr_made, n + 1)
                own.mark(dve.tensor_tensor(res[:, 4 * n:4 * n + 4, 0:D],
                                           psum[0:TP, n, 0:512].rearrange("p (t d) -> p t d", t=4),
                                           xr[:, 4 * n:4 * n + 4, :], ALU.add))
            own.settle()
            layernorm_dve(own, TP, res[:, :, 0:D], x1, stats, mv, rstd, std_in, (std_out, 1))
            dve.wait_ge(yT_made, 4)
            layernorm_dve(own, TP, x1, y[:, :, 0:D], stats, mv, rstd, std_in, (std_out, 2), xn_made)
            q = oAll[:, 0, :]
            for n in range(4):
                dve.wait_ge(q_made, n + 1)
                for m, tab in ((0, "cosq"), (1, "sinq")):
                    own.mark(dve.scalar_tensor_tensor(
                        out=oAll[:, 2 + m, n * 448:(n + 1) * 448].rearrange("p (b q) -> p b q", q=T),
                        in0=psum[:, 4 * m + n, 0:448].rearrange("p (b q) -> p b q", q=T),
                        scalar=prep["off"][:, m:m + 1], in1=strided(C(tab), [[0, 8], [1, T]]),
                        op0=ALU.add, op1=ALU.mult))
            own.settle()
            own.link(dve.tensor_tensor(q, oAll[:, 2, :], oAll[:, 3, :], ALU.add))
            hi = kT[:].bitcast(F32R)
            lo = oAll[:, 1, :].bitcast(F32R)
            dve.tensor_copy(hi, q).then_inc(q_split, 1)
            dve.wait_ge(q_split, 1)
            dve.tensor_tensor(lo, q, hi.bitcast(F32), ALU.subtract).then_inc(q_split, 1)

        @block.gpsimd
        def _(pool):
            pool.wait_ge(qT_out, 4)
            for b in range(1, B, 2):
                if b >= 3:
                    pool.wait_ge(s_made, b - 1)
                pool.tensor_tensor(qbd[:, 1, :, :], strided(qT[:, b * T:(b + 1) * T], [[0, NH], [1, T]]),
                                   strided(C("mask16"), [[1, NH], [0, T]]), ALU.mult).then_inc(spread_p, 1)


def cross_attention(nc, psum, wt, ct, xq_split, node_dram, o_dram, prep, ins):
    ctx_in, rope, hats, nodes = ins
    C = lambda n: ct[:, C_AT[n][0]:C_AT[n][1]]
    ident = C("ident")
    VW = HD + 1
    VROW = NH * VW + 14
    NVG = NH // VH
    OC = VH * T
    with ExitStack() as ctx:
        k = Core(nc, ctx)
        xin = k.sb("b_xin", [CH, 2, NC, D])
        eps = k.sb("b_eps", [CH, 1])
        stats = k.sb("b_stats", [CH, NC, 6])
        mv = k.sb("b_mv", [CH, NC, 2])
        std = k.sb("b_std", [CH, NC])
        rstd = k.sb("b_rstd", [CH, NC])
        shift = k.sb("b_shift", [CH, NC])
        xT = k.sb("b_xT", [128, 2, S])
        tab = k.sb("b_tab", [128, 2, S])
        kt = k.sb("b_kt", [128, 2, 2, KB])
        k32 = k.sb("b_k32", [128, KB])
        khi = k.sb("b_khi", [128, 2, S], F32R)
        klo = k.sb("b_klo", [128, 2, S], F32R)
        stack = k.sb("b_stack", [128, 2, NG, S], F32R)
        vx = k.sb("b_vx", [CH, 2, NC, VROW])
        qs = k.sb("b_qs", [96, 2, NG, T])
        qh = k.sb("b_qh", [128, 2, T])
        qstack = k.sb("b_qstack", [97 + 2 * HAT, 2, QC, NG, GC], F32R)
        qmax = k.sb("b_qmax", [128, 2, NH, T], F32R)
        prob = k.sb("b_prob", [CH, 3, HQ])
        mx = k.sb("b_mx", [128, NMX, NB])
        mx1 = k.sb("b_mx1", [128, NMX])
        mneg = k.sb("b_mneg", [NMX, 128], F32R)
        o_sb = k.sb("b_o", [128, 2, 2 * OC])

        ctx_got = [k.sem("b_ctx_even"), k.sem("b_ctx_odd")]
        q_got = [k.sem("b_q_even"), k.sem("b_q_odd")]
        stack_got = [k.sem("b_stack_even"), k.sem("b_stack_odd")]
        m_got = [k.sem("b_m_even"), k.sem("b_m_odd")]
        o_put = [k.sem("b_o_even"), k.sem("b_o_odd")]
        bias_got = [[k.sem(f"b_bias_{b}_{j}") for j in range(QC)] for b in ("even", "odd")]
        tab_got, hat_got, consts = k.sem("b_tab_got"), k.sem("b_hat_got"), k.sem("b_consts")
        hat_put, node_put = k.sem("b_hat_put"), k.sem("b_node_put")
        stats_made, var_made, std_made, rstd_made, xn_made = (
            k.sem("b_stats_made"), k.sem("b_var"), k.sem("b_std_made"), k.sem("b_rstd_made"), k.sem("b_xn"))
        xT_made, xT_out, k_made, k_rot, k_sum, k_hi, k_split = (
            k.sem("b_xT_made"), k.sem("b_xT_out"), k.sem("b_k_made"), k.sem("b_k_rot"), k.sem("b_k_sum"),
            k.sem("b_k_hi"), k.sem("b_k_split"))
        v_made, v_out = k.sem("b_v_made"), k.sem("b_v_out")
        qm_made, qk_made = k.sem("b_qm_made"), k.sem("b_qk_made")
        g_made, g_red, g_max, gT_made, m_made = (k.sem("b_g_made"), k.sem("b_g_red"), k.sem("b_g_max"),
                                                 k.sem("b_gT_made"), k.sem("b_m_made"))
        s_made, e_made, pv_made, o_out = k.sem("b_s_made"), k.sem("b_e_made"), k.sem("b_pv_made"), k.sem("b_o_out")
        block = ctx.enter_context(nc.Block())

        BX, BK = 5, (6, 7)
        FIRST, LAST = 2, 27

        def periods(eng, period):
            for p in range(-3, FIRST):
                period(0, p)
            with eng.Fori(FIRST // 2, (LAST + 1) // 2) as i:
                period(i, 0)
                period(i, 1)
            for p in range(LAST + 1, B):
                period(0, p)

        def live(i, n):
            return not isinstance(i, int) or 0 <= n < B

        def seq(i, n):
            return 2 * i + n

        def pair(i, n):
            return i + n // 2

        @block.sync
        def _(sp):
            sp.dma_start(tab[:], rope).then_inc(tab_got, 16)
            sp.dma_start(xT[0:2 * HAT, 0, :], hats).then_inc(hat_got, 16)
            sp.dma_start(xT[:, 1, 0:BQ * T], nodes).then_inc(hat_got, 16)
            sp.wait_ge(consts, 4)
            sp.dma_start(node_dram, stack[:, 1, 0:2, :].rearrange("p g s -> p (g s)")[:, 0:BQ * HQ].bitcast(F32))\
              .then_inc(node_put, 16)
            sp.wait_ge(node_put, 16)
            for b in range(2):
                for g in range(NG):
                    sp.dma_start(stack[97:97 + 2 * HAT, b, g, :].bitcast(F32), khi[0:2 * HAT, 0, :].bitcast(F32))\
                      .then_inc(hat_put, 16)

            def bias(n, c):
                row = 32 * (c // BQ)
                sp.dma_start(qstack[97:97 + 2 * HAT, n % 2, c % QC, :, :].rearrange("p g c -> p (g c)").bitcast(F32),
                             node_dram[row:row + 2 * HAT, (c % BQ) * HQ:(c % BQ + 1) * HQ])\
                  .then_inc(bias_got[n % 2][c % QC], 16)

            for n in range(2):
                for c in range(QC):
                    bias(n, c)

            def next_context(i, n):
                positive(sp, xT_made, NB * (seq(i, n) - 1))
                sp.dma_start(xin[:, n % 2, :, :], ctx_in[seq(i, n)].rearrange("(c p) d -> p c d", p=CH))\
                  .then_inc(ctx_got[n % 2], 16)

            def next_queries(i, n):
                positive(sp, qk_made, QC * (seq(i, n) - 1))
                positive(sp, qm_made, seq(i, n) - 1)
                src = xq_split.rearrange("s (g r) (b t) -> s r b g t", g=NG, t=T)
                for row, part in ((0, 0), (1, 1), (2, 0)):
                    sp.dma_start(qs[32 * row:32 * row + 32, n % 2, :, :], src[part, :, seq(i, n)])\
                      .then_inc(q_got[n % 2], 16)
                sp.dma_start(qh[:, n % 2, :], xq_split.rearrange("s r (b t) -> s b r t", t=T)[0, seq(i, n)])\
                  .then_inc(q_got[n % 2], 16)

            def stack_keys(i, n, g):
                if g == 0:
                    sp.wait_ge(k_split, NB * (seq(i, n) + 1))
                    positive(sp, s_made, NC * (seq(i, n) - 1))
                for row, part in ((0, khi), (1, khi), (2, klo)):
                    sp.dma_start(stack[32 * row:32 * row + 32, n % 2, g, :].bitcast(F32),
                                 part[32 * g:32 * g + 32, n % 2, :].bitcast(F32)).then_inc(stack_got[n % 2], 16)

            def negated_maxima(i, n):
                sp.wait_ge(m_made, seq(i, n) + 1)
                for j in range(QC):
                    sp.dma_start(qstack[96:97, n % 2, j, :, :].rearrange("p g c -> p (g c)").bitcast(F32),
                                 mneg[:].bitcast(F32)).then_inc(m_got[n % 2], 16)

            def sums(i, n):
                sp.wait_ge(o_out, seq(i, n) + 1)
                sp.dma_start(o_dram[pair(i, n), :, :, n % 2, :],
                             o_sb[:, n % 2, :].rearrange("p (c t) -> p c t", t=T)).then_inc(o_put[n % 2], 16)

            def period(i, p):
                for c in range(NC):
                    if c == 1 and live(i, p + 2):
                        next_queries(i, p + 2)
                    if c == 2 and live(i, p - 1):
                        sums(i, p - 1)
                    if c == 8 and live(i, p + 4):
                        next_context(i, p + 4)
                    if c == NC - 1 and live(i, p + 1):
                        negated_maxima(i, p + 1)
                    if live(i, p) and (c + QC < NC or live(i, p + 2)):
                        sp.wait_ge(s_made, NC * seq(i, p) + c + 1)
                        bias(p, (c + QC) % NC)
                    if 4 <= c < 4 + NG and live(i, p + 1):
                        stack_keys(i, p + 1, c - 4)

            next_context(0, 0)
            periods(sp, period)
            sums(0, B - 1)
            for s in o_put:
                sp.wait_ge(s, 16 * B // 2)

        @block.tensor
        def _(pe):
            pe.wait_ge(consts, 5)
            pe.wait_ge(hat_put, 16 * 2 * NG)

            def values(i, n, c):
                positive(pe, e_made, NC * seq(i, n) + c + 1)
                if c == 0:
                    pe.wait_ge(v_out, NB * (seq(i, n) + 1))
                    positive(pe, o_out, seq(i, n))
                for g in range(NVG):
                    j, cols = g % 4, OC
                    mm = pe.matmul(psum[32 * j:32 * j + 32, 4, (g // 4) * OC:(g // 4) * OC + cols],
                                   vx[:, n % 2, c, VH * VW * g:VH * VW * g + 32],
                                   prob[:, c % 3, OC * g:OC * g + cols],
                                   start=(c == 0 and g < 4), stop=(c == NC - 1), skip_group_check=True)
                mm.then_inc(pv_made, 1)

            def scores(i, n, c):
                if c == 0:
                    pe.wait_ge(stack_got[n % 2], 16 * 3 * NG * (pair(i, n) + 1))
                    pe.wait_ge(qk_made, QC * (seq(i, n) + 1))
                    pe.wait_ge(m_got[n % 2], 16 * QC * (pair(i, n) + 1))
                pe.wait_ge(bias_got[n % 2][c % QC], 16 * (CQ * pair(i, n) + c // QC + 1))
                positive(pe, e_made, NC * seq(i, n) + c - 1)
                for g in range(NG):
                    mm = pe.matmul(psum[0:CH, 2 * (c % 2) + g // 2, GC * (g % 2):GC * (g % 2 + 1)],
                                   stack[0:97 + 2 * HAT, n % 2, g, c * CH:(c + 1) * CH],
                                   qstack[:, n % 2, c % QC, g, :], start=True, stop=True)
                mm.then_inc(s_made, 1)

            def turn(i, n, r):
                if r == 0:
                    pe.wait_ge(xn_made, NC * (seq(i, n) + 1))
                    positive(pe, v_out, NB * (seq(i, n) - 1))
                    positive(pe, m_made, seq(i, n) - 1)
                positive(pe, xT_out, NB * seq(i, n) + r)
                for c in range(4):
                    mm = pe.transpose(psum[:, BX, c * CH:(c + 1) * CH], xin[:, n % 2, 4 * r + c, :],
                                      ident[0:CH, 0:CH])
                mm.then_inc(xT_made, 1)

            def keys(i, n, r, m):
                if m == 0:
                    pe.wait_ge(xT_out, NB * seq(i, n) + r + 1)
                    if r == 0:
                        positive(pe, g_max, seq(i, n))
                positive(pe, k_rot, 2 * (NB * seq(i, n) + r) + m - 1)
                pe.matmul(psum[:, BK[m], 0:KB], prep["xk" if m == 0 else "xkp"][:],
                          xT[:, n % 2, r * KB:(r + 1) * KB], start=True, stop=True).then_inc(k_made, 1)

            def vals(i, n, r):
                if r == 0:
                    positive(pe, xT_out, NB * min(seq(i, n) + 2, B) if isinstance(i, int) else NB * (seq(i, n) + 2))
                positive(pe, v_out, NB * seq(i, n) + r)
                for c in range(4):
                    at = (4 * r + c) * CH
                    mm = pe.matmul(psum[0:CH, BX, c * D:(c + 1) * D], xT[:, n % 2, at:at + CH], prep["xv"][:],
                                   start=True, stop=True)
                mm.then_inc(v_made, 1)

            def maxima(i, n, j):
                r, m = divmod(j, NMX)
                if j == 0:
                    pe.wait_ge(qm_made, seq(i, n) + 1)
                    positive(pe, k_rot, 2 * NB * (seq(i, n) + 1))
                if m == 0:
                    pe.wait_ge(k_hi, NB * seq(i, n) + r + 1)
                positive(pe, g_red, NB * NMX * seq(i, n) + j - 1)
                pe.matmul(psum[:, BK[j % 2], 0:KB],
                          qmax[:, n % 2, :, :].rearrange("p h q -> p (h q)")[:, m * 128:(m + 1) * 128],
                          khi[:, n % 2, r * KB:(r + 1) * KB], start=True, stop=True).then_inc(g_made, 1)

            def period(i, p):
                for c in range(NC):
                    js = range(min(c * NB * NMX // 9, NB * NMX), min((c + 1) * NB * NMX // 9, NB * NMX))
                    some = [lambda j=j: maxima(i, p + 1, j) for j in js] if live(i, p + 1) else []
                    if live(i, p):
                        scores(i, p, c)
                    if c >= 9 and live(i, p + 2):
                        keys(i, p + 2, c - 9, 0)
                    for m in some[:1]:
                        m()
                    if c == 0 and live(i, p - 1):
                        values(i, p - 1, NC - 1)
                    if c > 0 and live(i, p):
                        values(i, p, c - 1)
                    for m in some[1:2]:
                        m()
                    if live(i, p + 1):
                        if 6 <= c < 9:
                            vals(i, p + 1, c - 6)
                        if c == 9:
                            pe.wait_ge(v_out, NB * (seq(i, p + 1) + 1))
                            pe.wait_ge(g_max, seq(i, p + 1) + 1)
                            pe.transpose(psum[0:NMX, BX, 0:128], mx1[:], ident).then_inc(gT_made, 1)
                    if live(i, p + 2):
                        if 3 <= c < 6:
                            turn(i, p + 2, c - 3)
                        if c >= 9:
                            keys(i, p + 2, c - 9, 1)
                    for m in some[2:]:
                        m()

            periods(pe, period)
            values(0, B - 1, NC - 1)

        @block.scalar
        def _(act):
            def out(i, n):
                act.wait_ge(pv_made, NC * (seq(i, n) + 1))
                positive(act, o_put[n % 2], 16 * pair(i, n))
                act.copy(o_sb[:, n % 2, :], psum[:, 4, 0:2 * OC]).then_inc(o_out, 1)

            def period(i, p):
                for c in range(NC):
                    if live(i, p):
                        act.wait_ge(s_made, NC * seq(i, p) + c + 1)
                        positive(act, pv_made, NC * seq(i, p) + c - 2)
                        act.activation(prob[:, c % 3, :].rearrange("p (a c) -> p a c", a=2),
                                       psum[0:CH, 2 * (c % 2):2 * (c % 2) + 2, 0:HALF], ACT.Exp).then_inc(e_made, 1)
                    if c == 0 and live(i, p - 1):
                        out(i, p - 1)
                    if c == 8 and live(i, p + 3):
                        act.wait_ge(var_made, NC * (seq(i, p + 3) + 1))
                        positive(act, rstd_made, 2 * seq(i, p + 3))
                        act.activation(std[:], mv[:, :, 1], ACT.Sqrt, bias=eps[:]).then_inc(std_made, 1)
                    if c >= 9 and live(i, p + 3):
                        act.wait_ge(rstd_made, 2 * (seq(i, p + 3) + 1))
                        for t in range(4 * (c - 9), 4 * (c - 8)):
                            at = xin[:, (p + 3) % 2, t, :]
                            act.activation(at, at, ACT.Identity, bias=shift[:, t:t + 1], scale=rstd[:, t:t + 1])\
                               .then_inc(xn_made, 1)
                    if live(i, p + 2) and 3 <= c < 6:
                        r, n = c - 3, p + 2
                        act.wait_ge(xT_made, NB * seq(i, n) + r + 1)
                        act.copy(xT[:, n % 2, r * KB:(r + 1) * KB], psum[:, BX, 0:KB]).then_inc(xT_out, 1)
                    if live(i, p + 1) and 6 <= c < 9:
                        r, n = c - 6, p + 1
                        act.wait_ge(v_made, NB * seq(i, n) + r + 1)
                        act.copy(vx[:, n % 2, 4 * r:4 * r + 4, 0:NH * VW]
                                 .rearrange("p c (h d) -> p c h d", h=NH)[:, :, :, 0:HD],
                                 psum[0:CH, BX, 0:512].rearrange("p (c h d) -> p c h d", c=4, h=NH))\
                           .then_inc(v_out, 1)

            act.wait_ge(consts, 5)
            periods(act, period)
            out(0, B - 1)

        @block.vector
        def _(dve):
            dve.memset(vx[:], 1.0).then_inc(consts, 1)
            dve.memset(eps[:], EPS_LN).then_inc(consts, 1)
            dve.wait_ge(hat_got, 32)
            dve.tensor_copy(khi[0:2 * HAT, 0, :], xT[0:2 * HAT, 0, :]).then_inc(consts, 1)
            dve.tensor_copy(stack[:, 1, 0:2, :].rearrange("p g s -> p (g s)")[:, 0:BQ * HQ]
                            .rearrange("p (c h t) -> p c h t", c=BQ, h=NH),
                            strided(xT[:, 1, :], [[T, BQ], [0, NH], [1, T]])).then_inc(consts, 1)
            dve.wait_ge(node_put, 16)
            dve.memset(stack[96:97].bitcast(F32), 1.0).then_inc(consts, 1)

            def period(i, p):
                for j in range(NB * NMX):
                    n = p + 3
                    step = j // 2 if j % 2 and j // 2 <= NC // 2 and live(i, n) else None
                    if step == 0:
                        dve.wait_ge(ctx_got[n % 2], 16 * (pair(i, n) + 1))
                    elif step is not None:
                        dve.wait_ge(stats_made, NC * seq(i, n) + 2 * step)
                    if live(i, p + 1):
                        m = p + 1
                        dve.wait_ge(g_made, NB * NMX * seq(i, m) + j + 1)
                        dve.tensor_reduce(mx[:, j % NMX, j // NMX:j // NMX + 1], psum[:, BK[j % 2], 0:KB], AX.X,
                                          ALU.max).then_inc(g_red, 1)
                    if step == 0:
                        positive(dve, std_made, seq(i, n))
                        positive(dve, xn_made, NC * seq(i, n))
                    if step is not None and step < NC // 2:
                        for c in (2 * step, 2 * step + 1):
                            dve.bn_stats(stats[:, c, :], xin[:, n % 2, c, :]).then_inc(stats_made, 1)
                    if step:
                        for c in (2 * step - 2, 2 * step - 1):
                            dve.bn_aggr(mv[:, c, :], stats[:, c, :]).then_inc(var_made, 1)
                n = p + 1
                if live(i, n):
                    dve.wait_ge(g_red, NB * NMX * (seq(i, n) + 1))
                    dve.tensor_reduce(mx1[:], mx[:], AX.X, ALU.max).then_inc(g_max, 1)
                n = p + 3
                if live(i, n):
                    dve.wait_ge(std_made, seq(i, n) + 1)
                    dve.reciprocal(rstd[:], std[:]).then_inc(rstd_made, 1)
                    dve.wait_ge(rstd_made, 2 * seq(i, n) + 1)
                    dve.scalar_tensor_tensor(out=shift[:], in0=mv[:, :, 0], scalar=-1.0, in1=rstd[:],
                                             op0=ALU.mult, op1=ALU.mult).then_inc(rstd_made, 1)
                for r in range(NB):
                    n = p + 2
                    if live(i, n):
                        positive(dve, k_sum, NB * seq(i, n) + r - 1)
                        for m in range(2):
                            dve.wait_ge(k_made, 2 * (NB * seq(i, n) + r) + m + 1)
                            dve.scalar_tensor_tensor(
                                out=kt[:, (n * NB + r) % 2, m, :], in0=psum[:, BK[m], 0:KB],
                                scalar=prep["off"][:, 2 + m:3 + m], in1=tab[:, m, r * KB:(r + 1) * KB],
                                op0=ALU.add, op1=ALU.mult).then_inc(k_rot, 1)
                    n = p + 1
                    if live(i, n) and r == 0:
                        dve.wait_ge(gT_made, seq(i, n) + 1)
                        positive(dve, m_got[(n - 1) % 2], 16 * QC * (pair(i, n - 1) + 1))
                        dve.tensor_scalar(mneg[:], psum[0:NMX, BX, 0:128], -1.0, None, ALU.mult).then_inc(m_made, 1)

            dve.wait_ge(tab_got, 16)
            periods(dve, period)

        @block.gpsimd
        def _(pool):
            mask4 = C("mask4")
            pool.wait_ge(consts, 5)
            pool.wait_ge(hat_put, 16 * 2 * NG)

            def spread_max(i, n):
                pool.wait_ge(q_got[n % 2], 64 * (pair(i, n) + 1))
                positive(pool, g_made, NB * NMX * (seq(i, n) - 1))
                pool.tensor_tensor(qmax[:, n % 2, :, :], strided(qh[:, n % 2, :], [[0, NH], [1, T]]),
                                   strided(C("mask16"), [[1, NH], [0, T]]), ALU.mult).then_inc(qm_made, 1)

            def period(i, p):
                n = p + 1
                if live(i, n):
                    positive(pool, s_made, NC * (seq(i, n) - 1))
                    pool.wait_ge(q_got[n % 2], 64 * (pair(i, n) + 1))
                    for j in range(QC):
                        pool.tensor_tensor(qstack[0:96, n % 2, j, :, :].rearrange("p g (h q) -> p g h q", h=GH),
                                           strided(qs[:, n % 2, :, :], [[T, NG], [0, GH], [1, T]]),
                                           strided(mask4[0:96], [[0, NG], [1, GH], [0, T]]), ALU.mult)\
                            .then_inc(qk_made, 1)
                if live(i, p + 2):
                    spread_max(i, p + 2)
                n = p + 2
                if live(i, n):
                    for r in range(NB):
                        cols = slice(r * KB, (r + 1) * KB)
                        t = kt[:, (n * NB + r) % 2, :, :]
                        pool.wait_ge(k_rot, 2 * (NB * seq(i, n) + r + 1))
                        if r == 0:
                            positive(pool, stack_got[n % 2], 16 * 3 * NG * pair(i, n))
                            positive(pool, g_made, NB * NMX * (seq(i, n) - 1))
                        positive(pool, k_split, NB * seq(i, n) + r)
                        pool.tensor_tensor(khi[:, n % 2, cols], t[:, 0, :], t[:, 1, :], ALU.add).then_inc(k_hi, 1)
                        pool.tensor_tensor(k32[:], t[:, 0, :], t[:, 1, :], ALU.add).then_inc(k_sum, 1)
                        pool.wait_ge(k_hi, NB * seq(i, n) + r + 1)
                        pool.wait_ge(k_sum, NB * seq(i, n) + r + 1)
                        pool.tensor_tensor(klo[:, n % 2, cols], k32[:], khi[:, n % 2, cols].bitcast(F32),
                                           ALU.subtract).then_inc(k_split, 1)

            periods(pool, period)


def mix_and_experts(nc, psum, wt, ct, x1, o_dram, queue, made, prep, ins, out):
    w1, b1, w2, b2 = ins
    queue_rows, made_rows = (a.rearrange("(j p) d -> p j d", p=TP) for a in (queue, made))
    W = lambda n: wt[:, W_AT[n][0]:W_AT[n][1]]
    C = lambda n: ct[:, C_AT[n][0]:C_AT[n][1]]
    ident = C("ident")
    OC = VH * T
    VW = HD + 1
    SEG = N // 4
    with ExitStack() as ctx:
        k = Core(nc, ctx)
        o = k.sb("c_o", [128, NT // 2, 2 * VH, TP])
        att = k.sb("c_att", [TP, NT, D])
        gated = k.sb("c_gated", [TP, NT, D])
        x2 = k.sb("c_x2", [TP, NT, D])
        cT = k.sb("c_cT", [128, N])
        x2T = cT
        rden = k.sb("c_rden", [TP, 2, NH])
        mv = k.sb("c_mv", [TP, NT, 2])
        stats = k.sb("c_stats", [TP, NT, 6])
        rstd = k.sb("c_rstd", [TP, 2, NT])
        rt = k.sb("c_rt", [TP, 8, NT, E])
        col = k.sb("c_col", [TP, 2, NT])
        top = k.sb("c_top", [TP, NT, 8])
        topi = k.sb("c_topi", [TP, NT, 8], U32)
        topf = k.sb("c_topf", [TP, NT, 8])
        rowf = k.sb("c_rowf", [TP, TOPK, NT])
        row = k.sb("c_row", [TP, 2, TOPK, NT], U32)
        wk = k.sb("c_wk", [TP, TOPK, NT])
        w1s = k.sb("c_w1", [128, E, F])
        w2s = k.sb("c_w2", [128, E, FT, D])
        b1s = k.sb("c_b1", [128, E, FT])
        b2s = k.sb("c_b2", [128, E])
        hid = k.sb("c_hid", [128, 2, FT, CAP])
        xb = k.sb("c_xb", [TP, NQ, D])
        xbT = k.sb("c_xbT", [128, SLOTS])
        obT = k.sb("c_obT", [128, SLOTS])
        ob = xb
        picked = k.sb("c_picked", [TP, TOPK, NT, D])
        y = att

        got_o, got_f = k.sem("c_got_o"), k.sem("c_got_f")
        own_v = k.sem("c_own_v")
        oT_made, att_out, aT_made, aT_out, w_made, a_out, cT_made, cT_out, g_made, g_out, sig_out = (
            k.sem("c_oT_made"), k.sem("c_att_out"), k.sem("c_aT_made"), k.sem("c_aT_out"), k.sem("c_w_made"),
            k.sem("c_a_out"), k.sem("c_cT_made"), k.sem("c_cT_out"), k.sem("c_g_made"), k.sem("c_g_out"),
            k.sem("c_sig_out"))
        std_in, std_out, x2_made, x2T_made, x2T_out, l_made = (
            k.sem("c_std_in"), k.sem("c_std_out"), k.sem("c_x2_made"), k.sem("c_x2T_made"), k.sem("c_x2T_out"),
            k.sem("c_l_made"))
        e_in, e_out, sel_made, p_made, rows_made = (
            k.sem("c_e_in"), k.sem("c_e_out"), k.sem("c_sel"), k.sem("c_p_made"), k.sem("c_rows"))
        cleared, zeroed, sent = k.sem("c_cleared"), k.sem("c_zeroed"), k.sem("c_sent")
        queued = [k.sem(f"c_queued_{n}") for n in range(NQ // 4)]
        bT_made, bT_out, h_made, h_out, z_made, z_out = (k.sem("c_bT_made"), k.sem("c_bT_out"), k.sem("c_h_made"),
                                                         k.sem("c_h_out"), k.sem("c_z_made"), k.sem("c_z_out"))
        zT_made, zT_out, kept = k.sem("c_zT_made"), k.sem("c_zT_out"), k.sem("c_kept")
        got = [k.sem(f"c_got_{t}") for t in range(NT)]
        y_out, fin, stored = k.sem("c_y_out"), k.sem("c_fin"), k.sem("c_stored")
        block = ctx.enter_context(nc.Block())

        @block.sync
        def _(sp):
            for half in range(2):
                if half:
                    sp.wait_ge(oT_made, NT // 2)
                sp.dma_start(o[:].rearrange("p b c t -> p b (c t)"),
                             o_dram[half * (NT // 2):(half + 1) * (NT // 2)].rearrange("b p c s t -> p b (c s t)"))\
                  .then_inc(got_o, 16)
                if half == 0:
                    sp.dma_start(w1s[:], w1).then_inc(got_f, 16)
                    sp.dma_start(w2s[:], w2).then_inc(got_f, 16)
                    sp.dma_start(b1s[:], b1).then_inc(got_f, 16)
                    sp.dma_start(b2s[:], b2).then_inc(got_f, 16)
                    sp.wait_ge(cleared, 1)
                    sp.dma_start(queue_rows, xb[:]).then_inc(zeroed, 16)
            sp.wait_ge(sent, 16 * TOPK * NT)
            for n in range(NQ // 4):
                sp.dma_start(xb[:, 4 * n:4 * n + 4, :], queue_rows[:, 4 * n:4 * n + 4, :]).then_inc(queued[n], 16)
            for n in range(NQ // 4):
                sp.wait_ge(zT_out, n + 1)
                sp.dma_start(made_rows[:, 4 * n:4 * n + 4, :], ob[:, 4 * n:4 * n + 4, :]).then_inc(kept, 16)
            out_rows = out.rearrange("(t p) d -> p t d", p=TP)
            for n in range(4):
                sp.wait_ge(fin, 4 * n + 4)
                sp.dma_start(out_rows[:, 4 * n:4 * n + 4, :], gated[:, 4 * n:4 * n + 4, :]).then_inc(stored, 16)
            sp.wait_ge(zeroed, 16)
            sp.wait_ge(kept, 16 * NQ // 4)
            sp.wait_ge(stored, 64)

        @block.gpsimd
        def _(pool):
            pool.wait_ge(rows_made, 2)
            pool.wait_ge(zeroed, 16)
            for t in range(NT):
                for n in range(TOPK):
                    pool.indirect_dma_start(
                        out=queue, out_offset=bass.IndirectOffsetOnAxis(ap=row[:, 0, n, t:t + 1], axis=0),
                        in_=x2[:, t, :], in_offset=None, bounds_check=SLOTS - 1, oob_is_err=False)\
                        .then_inc(sent, 16)
            pool.wait_ge(kept, 16 * NQ // 4)
            for t in range(NT):
                for n in range(TOPK):
                    pool.indirect_dma_start(
                        out=picked[:, n, t, :], out_offset=None, in_=made,
                        in_offset=bass.IndirectOffsetOnAxis(ap=row[:, 1, n, t:t + 1], axis=0),
                        bounds_check=SLOTS - 1, oob_is_err=False).then_inc(got[t], 16)

        def turn(pe, made, waited, src, rows, bank):
            for t in range(NT):
                pe.wait_ge(waited, t + 1)
                mm = pe.transpose(psum[:, bank + t // 4, (t % 4) * TP:(t % 4 + 1) * TP], src[:, t, :],
                                  ident[0:rows, 0:rows])
                if t % 4 == 3:
                    mm.then_inc(made, 1)

        def product(pe, made, ready, src, weights, bank):
            for t in range(NT):
                if t % 4 == 0:
                    pe.wait_ge(ready, t // 4 + 1)
                mm = pe.matmul(psum[0:TP, bank + t // 4, (t % 4) * D:(t % 4 + 1) * D], src[:, t * TP:(t + 1) * TP],
                               weights, start=True, stop=True)
                if t % 4 == 3:
                    mm.then_inc(made, 1)

        @block.tensor
        def _(pe):
            for t in range(NT):
                pe.wait_ge(got_o, 16 * (t // (NT // 2) + 1))
                if t >= 2:
                    pe.wait_ge(att_out, t - 1)
                b = t % (NT // 2)
                for l in range(2 * VH):
                    mm = pe.transpose(psum[0:TP, t % 2, l * 128:(l + 1) * 128], o[:, b, l, :], ident)
                mm.then_inc(oT_made, 1)
            turn(pe, aT_made, att_out, att, TP, 4)
            product(pe, w_made, aT_out, cT, W("out"), 0)
            turn(pe, cT_made, a_out, gated, TP, 4)
            product(pe, g_made, cT_out, cT, W("gate"), 0)
            turn(pe, x2T_made, x2_made, x2, TP, 4)
            pe.wait_ge(g_out, 4)
            for t in range(NT):
                pe.wait_ge(x2T_out, t // 4 + 1)
                mm = pe.matmul(psum[0:TP, 0, t * E:(t + 1) * E], x2T[:, t * TP:(t + 1) * TP], W("router"),
                               start=True, stop=True)
            mm.then_inc(l_made, 1)
            pe.wait_ge(sel_made, 1)
            pe.matmul(psum[0:TP, 1, 0:NT * E], C("before")[0:TP], rt[:, 2, :, :], start=True, stop=True)
            pe.matmul(psum[0:TP, 2, 0:NT * E], C("ones")[0:TP], rt[:, 2, :, :], start=True, stop=True)\
              .then_inc(p_made, 1)
            for j in range(NQ):
                if j % 4 == 0:
                    pe.wait_ge(queued[j // 4], 16)
                mm = pe.transpose(psum[:, 3 + j // 4, (j % 4) * TP:(j % 4 + 1) * TP], xb[:, j, :], ident[0:TP, 0:TP])
                if j % 4 == 3:
                    mm.then_inc(bT_made, 1)
            pe.wait_ge(got_f, 64)
            pe.wait_ge(bT_out, NQ // 4)

            def hidden(e):
                for f in range(FT):
                    if e >= 1:
                        pe.wait_ge(h_out, FT * (e - 1) + f + 1)
                    pe.matmul(psum[:, f, 0:CAP], w1s[:, e, f * 128:(f + 1) * 128], xbT[:, e * CAP:(e + 1) * CAP],
                              start=True, stop=True).then_inc(h_made, 1)

            def outcome(e):
                if e >= 2:
                    pe.wait_ge(z_out, e - 1)
                for f in range(FT):
                    pe.wait_ge(h_out, FT * e + f + 1)
                    mm = pe.matmul(psum[:, 4 + e % 2, 0:CAP], w2s[:, e, f, :], hid[:, e % 2, f, :],
                                   start=(f == 0), stop=(f == FT - 1))
                mm.then_inc(z_made, 1)

            turned = 0
            for e in range(E + 1):
                if e < E:
                    hidden(e)
                if e >= 1:
                    outcome(e - 1)
                whole = e - 1 if e < E else E
                if e == E:
                    pe.wait_ge(z_out, E)
                elif whole > 0:
                    pe.wait_ge(z_out, whole)
                while whole > 0 and turned < NQ and (turned // 4 + 1) * 4 * TP <= whole * CAP:
                    n = turned // 4
                    if n >= 2:
                        pe.wait_ge(zT_out, n - 1)
                    for j in range(4):
                        mm = pe.transpose(psum[0:TP, 6 + n % 2, j * D:(j + 1) * D],
                                          obT[:, (turned + j) * TP:(turned + j + 1) * TP], ident)
                    mm.then_inc(zT_made, 1)
                    turned += 4

        @block.scalar
        def _(act):
            def evacuate(made, out_sem, dst):
                for n in range(4):
                    act.wait_ge(made, n + 1)
                    act.copy(dst[:, n * SEG:(n + 1) * SEG], psum[:, 4 + n, 0:SEG]).then_inc(out_sem, 1)

            evacuate(aT_made, aT_out, cT)
            act.wait_ge(w_made, 4)
            evacuate(cT_made, cT_out, cT)
            act.wait_ge(g_out, 4)
            act.activation(x2[:], x2[:], ACT.Sigmoid).then_inc(sig_out, 1)
            act.wait_ge(std_in, 1)
            act.activation(rstd[:, 0, :], rstd[:, 0, :], ACT.Sqrt).then_inc(std_out, 1)
            evacuate(x2T_made, x2T_out, x2T)
            act.wait_ge(e_in, 1)
            act.activation(rt[:, 1, :, :], rt[:, 0, :, :], ACT.Exp).then_inc(e_out, 1)
            for n in range(NQ // 4):
                act.wait_ge(bT_made, n + 1)
                act.copy(xbT[:, n * SEG:(n + 1) * SEG], psum[:, 3 + n, 0:SEG]).then_inc(bT_out, 1)
            act.wait_ge(got_f, 64)
            for e in range(E):
                for f in range(FT):
                    act.wait_ge(h_made, FT * e + f + 1)
                    if e >= 2:
                        act.wait_ge(z_made, e - 1)
                    act.activation(hid[:, e % 2, f, :], psum[:, f, 0:CAP], ACT.Gelu, bias=b1s[:, e, f:f + 1])\
                       .then_inc(h_out, 1)
            act.wait_ge(std_in, 2)
            act.activation(rstd[:, 0, :], rstd[:, 0, :], ACT.Sqrt).then_inc(std_out, 1)

        @block.vector
        def _(dve):
            own = Own(dve, own_v)
            dve.memset(xb[:], 0.0).then_inc(cleared, 1)
            for t in range(NT):
                dve.wait_ge(oT_made, t + 1)
                for half in range(2):
                    p, at, first = psum[0:TP, t % 2, :], 256 * half, 8 * half
                    heads, spots = [[1, VH], [VH, 4]], [[128 + VW, VH], [32, 4]]
                    own.link(dve.reciprocal(strided(rden[:, t % 2, :], heads, first), strided(p, spots, at + HD)))
                    own.mark(dve.tensor_tensor(strided(att[:, t, :], [[HD, VH], [VH * HD, 4], [1, HD]], first * HD),
                                               strided(p, spots + [[1, HD]], at),
                                               strided(rden[:, t % 2, :], heads + [[0, HD]], first), ALU.mult))
                own.settle()
                dve.tensor_tensor(att[:, t, :], att[:, t, :], prep["off_v"][:], ALU.add).then_inc(att_out, 1)
            four = lambda a, n: a[:, 4 * n:4 * n + 4, :]
            rows = lambda name: strided(W(name)[0:TP], [[0, 4], [1, D]])
            bank4 = lambda n: psum[0:TP, n, 0:512].rearrange("p (t d) -> p t d", t=4)
            for n in range(4):
                dve.wait_ge(w_made, n + 1)
                dve.tensor_tensor(four(gated, n), bank4(n), rows("b_out"), ALU.add).then_inc(a_out, 4)
            for n in range(4):
                dve.wait_ge(g_made, n + 1)
                dve.tensor_tensor(four(x2, n), bank4(n), rows("b_gate"), ALU.add).then_inc(g_out, 1)
            own.mark(dve.tensor_tensor(gated[:], gated[:], x1[:], ALU.subtract))
            dve.wait_ge(sig_out, 1)
            own.settle()
            own.link(dve.tensor_tensor(gated[:], gated[:], x2[:], ALU.mult))
            own.link(dve.scalar_tensor_tensor(out=gated[:], in0=x1[:], scalar=2.0, in1=gated[:],
                                              op0=ALU.mult, op1=ALU.add))
            layernorm_dve(own, TP, gated, x2, stats, mv, rstd, std_in, (std_out, 1), x2_made)
            dve.wait_ge(l_made, 1)
            own.link(dve.tensor_tensor(rt[:, 3, :, :], psum[0:TP, 0, 0:NT * E].rearrange("p (t e) -> p t e", e=E),
                                       strided(W("b_router")[0:TP], [[0, NT], [1, E]]), ALU.add))
            own.link(dve.tensor_reduce(col[:, 0, :], rt[:, 3, :, :], AX.X, ALU.max))
            spread = lambda n: strided(col[:, n, :], [[1, NT], [0, E]])
            dve.tensor_tensor(rt[:, 0, :, :], rt[:, 3, :, :], spread(0), ALU.subtract).then_inc(e_in, 1)
            dve.wait_ge(e_out, 1)
            own.link(dve.tensor_reduce(col[:, 0, :], rt[:, 1, :, :], AX.X, ALU.add))
            own.link(dve.reciprocal(col[:, 1, :], col[:, 0, :]))
            own.link(dve.tensor_tensor(rt[:, 1, :, :], rt[:, 1, :, :], spread(1), ALU.mult))
            for t in range(NT):
                own.mark(dve.max(top[:, t, :], rt[:, 1, t, :]))
            own.settle()
            for t in range(NT):
                own.mark(dve.max_index(topi[:, t, :], top[:, t, :], rt[:, 1, t, :]))
            own.settle()
            own.link(dve.tensor_copy(topf[:], topi[:]))
            iota = strided(C("iota")[0:TP], [[0, NT], [1, E]])
            for n in range(TOPK):
                own.mark(dve.tensor_tensor(rt[:, 6 + n, :, :], iota, strided(topf[:, :, n:n + 1], [[8, NT], [0, E]]),
                                           ALU.is_equal))
            own.settle()
            dve.tensor_tensor(rt[:, 2, :, :], rt[:, 6, :, :], rt[:, 7, :, :], ALU.add).then_inc(sel_made, 1)
            dve.wait_ge(p_made, 1)
            own.link(dve.memset(rt[:, 3, 0, :], 0.0))
            own.link(dve.tensor_copy(rt[:, 4, :, :], psum[0:TP, 2, 0:NT * E].rearrange("p (t e) -> p t e", e=E)))
            for t in range(1, NT):
                own.link(dve.tensor_tensor(rt[:, 3, t, :], rt[:, 3, t - 1, :], rt[:, 4, t - 1, :], ALU.add))
            own.link(dve.tensor_tensor(rt[:, 4, :, :], psum[0:TP, 1, 0:NT * E].rearrange("p (t e) -> p t e", e=E),
                                       rt[:, 3, :, :], ALU.add))
            own.link(dve.tensor_scalar(rt[:, 0, :, :], rt[:, 4, :, :], float(CAP), float(FAR), ALU.is_ge, ALU.mult))
            own.link(dve.tensor_tensor(rt[:, 0, :, :], rt[:, 0, :, :], rt[:, 4, :, :], ALU.add))
            own.link(dve.tensor_tensor(rt[:, 0, :, :], rt[:, 0, :, :], strided(C("slot")[0:TP], [[0, NT], [1, E]]),
                                       ALU.add))
            for n in range(TOPK):
                own.mark(dve.tensor_tensor(rt[:, 2 + n, :, :], rt[:, 0, :, :], rt[:, 6 + n, :, :], ALU.mult))
            own.settle()
            own.link(dve.tensor_reduce(rowf[:], rt[:, 2:4, :, :], AX.X, ALU.add))
            dve.tensor_copy(row[:, 0, :, :], rowf[:]).then_inc(rows_made, 1)
            dve.tensor_scalar(row[:, 1, :, :], rowf[:], float(SLOTS - 1), None, ALU.min).then_inc(rows_made, 1)
            own.link(dve.scalar_tensor_tensor(out=rt[:, 4, :, :], in0=rt[:, 4, :, :], scalar=float(CAP),
                                              in1=rt[:, 1, :, :], op0=ALU.is_lt, op1=ALU.mult))
            for n in range(TOPK):
                own.mark(dve.tensor_tensor(rt[:, 2 + n, :, :], rt[:, 4, :, :], rt[:, 6 + n, :, :], ALU.mult))
            own.settle()
            own.link(dve.tensor_reduce(wk[:], rt[:, 2:4, :, :], AX.X, ALU.add))
            own.link(dve.tensor_tensor(col[:, 0, :], wk[:, 0, :], wk[:, 1, :], ALU.add))
            own.link(dve.tensor_scalar(col[:, 1, :], col[:, 0, :], 1e-6, None, ALU.max))
            own.link(dve.reciprocal(col[:, 0, :], col[:, 1, :]))
            own.link(dve.tensor_tensor(wk[:], wk[:], strided(col[:, 0, :], [[0, TOPK], [1, NT]]), ALU.mult))

            def expert_out(e):
                dve.wait_ge(z_made, e + 1)
                dve.tensor_scalar(obT[:, e * CAP:(e + 1) * CAP], psum[:, 4 + e % 2, 0:CAP], b2s[:, e:e + 1], None,
                                  ALU.add).then_inc(z_out, 1)

            def rows_out(n):
                dve.wait_ge(zT_made, n + 1)
                dve.tensor_copy(ob[:, 4 * n:4 * n + 4, :],
                                psum[0:TP, 6 + n % 2, 0:512].rearrange("p (t d) -> p t d", t=4)).then_inc(zT_out, 1)

            dve.wait_ge(bT_made, NQ // 4)
            done = 0
            for e in range(E):
                expert_out(e)
                while done < NQ // 4 and (done + 1) * 4 * TP <= (e - 1) * CAP:
                    rows_out(done)
                    done += 1
            for n in range(done, NQ // 4):
                rows_out(n)
            for t in range(NT):
                dve.wait_ge(got[t], 32)
                own.link(dve.scalar_tensor_tensor(out=y[:, t, :], in0=picked[:, 0, t, :], scalar=wk[:, 0, t:t + 1],
                                                  in1=x2[:, t, :], op0=ALU.mult, op1=ALU.add))
                own.link(dve.scalar_tensor_tensor(out=y[:, t, :], in0=picked[:, 1, t, :], scalar=wk[:, 1, t:t + 1],
                                                  in1=y[:, t, :], op0=ALU.mult, op1=ALU.add))
                own.link(dve.bn_stats(stats[:, t, :], y[:, t, :]))
                own.mark(dve.bn_aggr(mv[:, t, :], stats[:, t, :]))
            own.settle()
            dve.tensor_scalar(rstd[:, 0, :], mv[:, :, 1], EPS_LN, None, ALU.add).then_inc(std_in, 1)
            dve.wait_ge(std_out, 2)
            own.link(dve.reciprocal(rstd[:, 1, :], rstd[:, 0, :]))
            for t in range(NT):
                dve.tensor_scalar(gated[:, t, :], y[:, t, :], mv[:, t, 0:1], rstd[:, 1, t:t + 1],
                                  ALU.subtract, ALU.mult).then_inc(fin, 1)


def decoder_layer(nc, x_rows, x_cols, ctx_in, wpack, cpack, rope, hats, nodes, w1, b1, w2, b2, out):
    xq_split = nc.dram_tensor("xq_split", [2, 128, N], F32, kind="Internal").ap()
    node_dram = nc.dram_tensor("bias_nodes", [128, BQ * HQ], F32, kind="Internal").ap()
    o_dram = nc.dram_tensor("o_sums", [NT, 128, 2 * VH, 2, T], F32, kind="Internal").ap()
    queue = nc.dram_tensor("queue", [SLOTS, D], F32, kind="Internal").ap()
    made = nc.dram_tensor("made", [SLOTS, D], F32, kind="Internal").ap()
    with ExitStack() as ctx:
        k = Core(nc, ctx)
        psum = ctx.enter_context(nc.psum_tensor("psum", [128, 8, 512], F32))
        wt = k.sb("wt", [128, W_N])
        ct = k.sb("ct", [128, C_N])
        x1 = k.sb("x1", [TP, NT, D])
        prep = {n: k.sb("w_" + n, [128, D]) for n in ("xq", "xqp", "xk", "xkp", "xv")}
        prep["beta_cols"] = k.sb("beta_cols", [128, TP])
        prep["off"] = k.sb("off", [128, 4])
        prep["off_v"] = k.sb("off_v", [TP, D])
        self_attention(nc, psum, wt, ct, x1, xq_split, prep, (x_rows, x_cols, wpack, cpack))
        cross_attention(nc, psum, wt, ct, xq_split, node_dram, o_dram, prep, (ctx_in, rope, hats, nodes))
        mix_and_experts(nc, psum, wt, ct, x1, o_dram, queue, made, prep, (w1, b1, w2, b2), out)


def resize_weights(n_in, n_out):
    step = n_in / n_out
    at = (np.arange(n_out) + 0.5) * step - 0.5
    w = np.maximum(0.0, 1.0 - np.abs(at[None, :] - np.arange(n_in)[:, None]) / max(step, 1.0))
    return w / w.sum(0, keepdims=True)


def rotary(positions, width):
    half = width // 2
    inv = (np.float32(1.0) / np.float32(10000.0) ** (np.arange(0, width, 2, dtype=np.float32) / np.float32(width)))
    ang = (np.arange(positions, dtype=np.float32)[:, None] * inv[None, :].astype(np.float32)).astype(np.float32)
    cos, sin = np.cos(ang.astype(np.float64)), np.sin(ang.astype(np.float64))
    return np.concatenate([cos, cos], 1), np.concatenate([-sin, sin], 1), half


def half_precision_pair(a):
    a = a.astype(np.float32)
    bits = a.view(np.uint32).astype(np.uint64)
    hi = ((bits + 0x800) & 0xFFFFF000).astype(np.uint32).view(np.float32)
    return hi, (a - hi).astype(np.float32)


def constants():
    c = np.zeros((128, C_N), np.float32)

    def put(name, a):
        lo, _ = C_AT[name]
        c[:a.shape[0], lo:lo + a.shape[1]] = a

    p = np.arange(128)
    put("ident", np.eye(128))
    put("mask16", (p[:, None] // HD == np.arange(NH)[None, :]) * 1.0)
    put("mask4", ((p[:, None] % 32) // HD == np.arange(GH)[None, :]) * 1.0)
    cq, sq, _ = rotary(T, HD)
    put("cosq", cq[:, p % HD].T * HD ** -0.5)
    put("sinq", sq[:, p % HD].T * HD ** -0.5)
    t = np.arange(T)
    put("causal", (t[:, None] <= t[None, :]) * 1.0)
    put("cosa", cq[np.arange(TP) % T])
    put("sina", sq[np.arange(TP) % T])
    put("before", (np.arange(TP)[:, None] < np.arange(TP)[None, :]) * 1.0)
    put("ones", np.ones((TP, TP)))
    put("iota", np.tile(np.arange(E), (128, 1)))
    put("slot", np.tile(np.arange(E) * CAP, (128, 1)))
    ck, sk, _ = rotary(S, HD)
    rope = np.stack([ck[:, p % HD].T, sk[:, p % HD].T], 1).astype(np.float32)

    pos = np.arange(BIAS_LEN, dtype=np.float32)
    dist = np.abs(pos[None, :] - pos[:, None])
    bias = np.exp(-dist * np.float32(0.1)) - dist * np.float32(0.05)
    whole = 2 * S // 4
    hat = np.rint(resize_weights(BIAS_LEN, S) * whole)
    base = (bias.astype(np.float64) @ resize_weights(BIAS_LEN, T)) / whole
    hi, lo = half_precision_pair(base)
    hats = np.zeros((2 * HAT, S), np.float32)
    nodes = np.zeros((4, 32, BQ, T), np.float32)
    for n in range(NC):
        cols = slice(n * CH, (n + 1) * CH)
        touched = np.nonzero(hat[:, cols].sum(1))[0]
        assert len(touched) <= HAT
        for r, j in enumerate(touched):
            for off, part in ((0, hi), (HAT, lo)):
                hats[off + r, cols] = hat[j, cols]
                nodes[n // BQ, off + r, n % BQ, :] = part[j]
    return c, rope, hats, nodes.reshape(128, BQ * T)


def kernel(x, ctx_1024, L0_attn_Wq, L0_attn_Wkv, L0_attn_Wproj, L0_xattn_Wqkv, L0_xattn_Wout, L0_xattn_b_out,
           L0_xattn_Wgate, L0_xattn_b_gate, L0_xattn_gamma, L0_xattn_beta, L0_ffn_w_router, L0_ffn_b_router,
           L0_ffn_w1, L0_ffn_b1, L0_ffn_w2, L0_ffn_b2):
    import concourse.bacc as bacc
    from concourse.bass_utils import run_bass_kernel_spmd

    a = {n: np.asarray(v) for n, v in locals().items() if n[0] in "xcL" and not n.startswith("concourse")}
    x = a["x"].reshape(N, D)
    wqkv = a["L0_xattn_Wqkv"]
    partner = np.arange(D) // HD * HD + (np.arange(D) % HD + HD // 2) % HD
    wq, wk, wv = wqkv[:D], wqkv[D:2 * D], wqkv[2 * D:]
    rows = lambda v: np.broadcast_to(v[None, :], (128, v.shape[0]))
    wpack = np.concatenate(
        [a["L0_attn_Wq"].T, a["L0_attn_Wkv"].T, a["L0_attn_Wproj"].T, wq.T, wq[partner].T, wk.T, wk[partner].T,
         wv.T, a["L0_xattn_Wout"].T, a["L0_xattn_Wgate"].T, a["L0_xattn_gamma"][:, None],
         a["L0_xattn_beta"][:, None], rows(a["L0_xattn_b_out"]), rows(a["L0_xattn_b_gate"]),
         a["L0_ffn_w_router"], rows(a["L0_ffn_b_router"])], axis=1)
    cpack, rope, hats, nodes = constants()
    arrays = {
        "x_rows": x, "x_cols": x.T, "ctx_in": a["ctx_1024"], "wpack": wpack, "cpack": cpack, "rope": rope,
        "hats": hats, "nodes": nodes,
        "w1": a["L0_ffn_w1"].transpose(1, 0, 2),
        "b1": a["L0_ffn_b1"].reshape(E, FT, 128).transpose(2, 0, 1),
        "w2": a["L0_ffn_w2"].reshape(E, FT, 128, D).transpose(2, 0, 1, 3),
        "b2": a["L0_ffn_b2"].T,
    }
    arrays = {n: np.ascontiguousarray(v) for n, v in arrays.items()}
    nc = bacc.Bacc("TRN2", target_bir_lowering=False, num_devices=1)
    args = [nc.dram_tensor(n, v.shape, F32, kind="ExternalInput").ap() for n, v in arrays.items()]
    out = nc.dram_tensor("out", (N, D), F32, kind="ExternalOutput").ap()
    decoder_layer(nc, *args, out)
    r = run_bass_kernel_spmd(nc, [arrays], core_ids=[0])
    return r.results[0]["out"].reshape(B, T, D)
```

```python
from contextlib import ExitStack

import numpy as np

import concourse.bass as bass
from concourse import mybir

F32 = mybir.dt.float32
F32R = mybir.dt.float32r
U32 = mybir.dt.uint32
I32 = mybir.dt.int32
ALU = mybir.AluOpType
ACT = mybir.ActivationFunctionType
AX = mybir.AxisListType

B, T, D = 32, 56, 128
S = 1500
NH, HD = 16, 8
NKV = 4
N = B * T
TP = 2 * T
NT = N // TP
CH = 125
NC = S // CH
KB = 500
NB = S // KB
HQ = NH * T
NP = B // 2
HALF = HQ // 2
GH = 4
NG = NH // GH
GC = GH * T
VH = 2
NMX = HQ // 128
E, F, TOPK = 8, 512, 2
CAP = max(1, int(1.25 * N / E))
SLOTS = E * CAP
NQ = SLOTS // TP
FAR = 2 * SLOTS
FT = F // 128
EPS_LN = 1e-5
EPS_NORM = 1e-6
VW = HD + 1
VROW = NH * VW + 14
NEWTON = 3
RSTD_STEPS = 4 * NEWTON + 2
BIAS_LEN = 128
HAT = 13
QC = 3
CQ = NC // QC
BQ = NC // 4

W_COLS = [("qk", D + NKV * HD), ("v", NKV * HD), ("proj", D), ("xq", D), ("xqp", D), ("xk", D), ("xkp", D),
          ("xv", D), ("out", D), ("gate", D), ("gamma", 1), ("beta", 1), ("b_out", D), ("b_gate", D),
          ("router", E), ("b_router", E)]
C_COLS = [("ident", 128), ("mask16", NH), ("mask4", GH), ("cosq", T), ("sinq", T), ("causal", T),
          ("cosa", HD), ("sina", HD), ("before", TP), ("ones", TP), ("iota", E), ("slot", E),
          ("dest", TOPK * NT)]


def columns(cols):
    at, out = 0, {}
    for name, n in cols:
        out[name] = (at, at + n)
        at += n
    return out, at


W_AT, W_N = columns(W_COLS)
C_AT, C_N = columns(C_COLS)


def strided(ap, dims, off=0):
    return bass.AP(ap.tensor, ap.offset + off, [list(ap.ap[0])] + [list(d) for d in dims])


def positive(eng, sem, value):
    if not isinstance(value, int) or value > 0:
        eng.wait_ge(sem, value)


class Own:

    def __init__(self, eng, sem):
        self.eng, self.sem, self.n = eng, sem, 0

    def mark(self, ins):
        ins.then_inc(self.sem, 1)
        self.n += 1

    def settle(self):
        self.eng.wait_ge(self.sem, self.n)

    def link(self, ins):
        self.mark(ins)
        self.settle()


class Core:

    def __init__(self, nc, ctx):
        self.nc, self.ctx = nc, ctx

    def sb(self, name, shape, dt=F32):
        return self.ctx.enter_context(self.nc.sbuf_tensor(name, shape, dt))

    def sem(self, name):
        return self.ctx.enter_context(self.nc.semaphore(name))


def layernorm_dve(own, rows, src, dst, stats, mv, rstd, std_wanted, std_done, signal=None):
    for t in range(NT):
        own.mark(own.eng.bn_stats(stats[0:rows, t, :], src[0:rows, t, :]))
    own.settle()
    for t in range(NT):
        own.mark(own.eng.bn_aggr(mv[0:rows, t, :], stats[0:rows, t, :]))
    own.settle()
    own.eng.tensor_scalar(rstd[0:rows, 0, :], mv[0:rows, :, 1], EPS_LN, None, ALU.add).then_inc(std_wanted, 1)
    own.eng.wait_ge(std_done[0], std_done[1])
    own.link(own.eng.reciprocal(rstd[0:rows, 1, :], rstd[0:rows, 0, :]))
    for t in range(NT):
        ins = own.eng.tensor_scalar(dst[0:rows, t, :], src[0:rows, t, :], mv[0:rows, t, 0:1],
                                    rstd[0:rows, 1, t:t + 1], ALU.subtract, ALU.mult)
        if signal is None:
            own.mark(ins)
        else:
            ins.then_inc(signal, 1)
    if signal is None:
        own.settle()


CONTEXT_ARRAYS = ("stats", "mv", "half", "bits", "newton", "rstd", "shift")
CONTEXT_SIGNALS = ("stats_made", "var_made", "guess_made", "rstd_made", "xn_made")


def guess(dve, at, n, step):
    half, bits = at["half"][:], at["bits"][:]
    if step == 0:
        dve.tensor_scalar(half, at["mv"][:, :, 1], EPS_LN, 0.5, ALU.add, ALU.mult).then_inc(at["guess_made"], 1)
        return
    dve.wait_ge(at["guess_made"], 3 * n + step)
    if step == 1:
        dve.tensor_scalar(bits, half.bitcast(I32), 1, None, ALU.logical_shift_right).then_inc(at["guess_made"], 1)
    else:
        dve.tensor_scalar(at["rstd"][:].bitcast(I32), bits, -1.0, float(0x5ef759df), ALU.mult, ALU.add)\
           .then_inc(at["guess_made"], 1)


def inverse_deviation(pool, at, n):
    y, a, shift, half = at["rstd"][:], at["newton"][:], at["shift"][:], at["half"][:]
    zero, one_half = at["whole"][:, 0, :], at["whole"][:, 1, :]
    pool.wait_ge(at["guess_made"], 3 * (n + 1))
    for step in range(RSTD_STEPS):
        if step:
            pool.wait_ge(at["rstd_made"], RSTD_STEPS * n + step)
        out, in0, in1, op = {
            0: (a, y, y, ALU.mult), 1: (a, a, half, ALU.mult), 2: (a, one_half, a, ALU.subtract),
            3: (y, y, a, ALU.mult)}[step % 4] if step < 4 * NEWTON else {
            0: (a, at["mv"][:, :, 0], y, ALU.mult), 1: (shift, zero, a, ALU.subtract)}[step - 4 * NEWTON]
        pool.tensor_tensor(out, in0, in1, op).then_inc(at["rstd_made"], 1)


def self_attention(nc, psum, wt, ct, x1, xq_split, prep, start, tables, ins):
    x_rows, x_cols, wpack, cpack, ctx_in, rope, hats, nodes = ins
    hat_dram, node_dram = tables
    W = lambda n: wt[:, W_AT[n][0]:W_AT[n][1]]
    C = lambda n: ct[:, C_AT[n][0]:C_AT[n][1]]
    ident = C("ident")
    NQK = D + NKV * HD
    NHK = NH + NKV
    with ExitStack() as ctx:
        k = Core(nc, ctx)
        xT = k.sb("a_xT", [128, N])
        xr = k.sb("a_xr", [TP, NT, D])
        qk = k.sb("a_qk", [TP, NT, NQK])
        t1 = k.sb("a_t1", [TP, NT, NQK])
        t2 = k.sb("a_t2", [TP, NT, NQK])
        nrm = k.sb("a_nrm", [TP, 3, NT * NHK])
        qr = k.sb("a_qr", [TP, NT, D])
        kr = k.sb("a_kr", [TP, NT, D])
        vx = k.sb("a_vx", [128, NP, NKV, 32])
        qT = k.sb("a_qT", [128, N])
        kT = k.sb("a_kT", [128, N + 64 - T])
        qbd = k.sb("a_qbd", [128, 2, 2, NH, T])
        prob = k.sb("a_prob", [128, 3, HQ])
        oT = qT
        oAll = k.sb("a_o", [128, NKV, N])
        mv = k.sb("a_mv", [TP, NT, 2])
        stats = k.sb("a_stats", [TP, NT, 6])
        rstd = k.sb("a_rstd", [TP, 2, NT])

        got_x, got_w, got_r = k.sem("a_got_x"), k.sem("a_got_w"), k.sem("a_got_r")
        qk_made, v_made, qk_out = k.sem("a_qk_made"), k.sem("a_v_made"), k.sem("a_qk_out")
        own_v = k.sem("a_own_v")
        nrm_in, nrm_out = k.sem("a_nrm_in"), k.sem("a_nrm_out")
        qk_rot, qkT_made, qT_out, kT_out = (k.sem("a_qk_rot"), k.sem("a_qkT_made"), k.sem("a_qT_out"),
                                            k.sem("a_kT_out"))
        spread_v, spread_p = k.sem("a_spread_v"), k.sem("a_spread_p")
        s_made, e_made, masked, o_made, o_out = (k.sem("a_s_made"), k.sem("a_e_made"), k.sem("a_masked"),
                                                 k.sem("a_o_made"), k.sem("a_o_out"))
        oT_made, y_out, yT_made, yT_out, pr_made = (k.sem("a_oT_made"), k.sem("a_y_out"), k.sem("a_yT_made"),
                                                    k.sem("a_yT_out"), k.sem("a_pr_made"))
        padded, std_in, std_out = k.sem("a_padded"), k.sem("a_std_in"), k.sem("a_std_out")
        xn_made, xnT_made, xnT_out, q_made, q_split = (k.sem("a_xn_made"), k.sem("a_xnT_made"),
                                                       k.sem("a_xnT_out"), k.sem("a_q_made"), k.sem("a_q_split"))
        w_fold, bias_made, bias_out, q_stored = (k.sem("a_w_fold"), k.sem("a_bias_made"), k.sem("a_bias_out"),
                                                 k.sem("a_q_stored"))
        block = ctx.enter_context(nc.Block())

        node32 = k.sb("a_node32", [128, BQ * T])
        spare = qbd[0:1 + 2 * HAT].rearrange("p a b h t -> p (a b h t)")
        hat32, hatr = spare[:, 0:S], spare[:, S:2 * S].bitcast(F32R)
        table_got, table_made, table_put = k.sem("a_table_got"), k.sem("a_table_made"), k.sem("a_table_put")
        flat = lambda a: a[:].rearrange("p t c -> p (t c)")
        heads = lambda a: flat(a).rearrange("p (h d) -> p h d", d=HD)
        sq = oAll[0:TP].rearrange("p l n -> p (l n)")[:, 0:NT * NQK]
        sq_made, sin_made, whole_made = k.sem("a_sq_made"), k.sem("a_sin_made"), k.sem("a_whole_made")
        yT, xnT = kT, xT
        y, res = t1, t2
        QK_BANK = 3

        @block.sync
        def _(sp):
            sp.dma_start(xT[:], x_cols).then_inc(got_x, 16)
            sp.dma_start(wt[:], wpack).then_inc(got_w, 16)
            sp.dma_start(ct[:], cpack).then_inc(got_w, 16)
            sp.dma_start(node32[:], nodes).then_inc(table_got, 16)
            sp.dma_start(hat32, hats).then_inc(table_got, 16)
            sp.dma_start(xr[:], x_rows.rearrange("(t p) d -> p t d", p=TP)).then_inc(got_r, 16)
            for n in range(2):
                sp.dma_start(start["xin"][:, n, :, :], ctx_in[n].rearrange("(c p) d -> p c d", p=CH))\
                  .then_inc(start["ctx_got"][n], 16)
            sp.dma_start(start["tab"][:], rope).then_inc(start["tab_got"], 16)
            sp.wait_ge(table_made, 2)
            sp.dma_start(hat_dram, hatr.bitcast(F32)).then_inc(table_put, 16)
            sp.dma_start(node_dram, prob[:].rearrange("p c n -> p (c n)")).then_inc(table_put, 16)
            for n in range(4):
                cols = slice(n * 448, (n + 1) * 448)
                sp.wait_ge(q_split, 2 * n + 2)
                sp.dma_start(xq_split[0][:, cols], kT[:, cols].bitcast(F32)).then_inc(q_stored, 16)
                sp.dma_start(xq_split[1][:, cols], oAll[:, 1, cols].bitcast(F32)).then_inc(q_stored, 16)
            sp.wait_ge(q_stored, 128)
            sp.wait_ge(table_put, 32)

        @block.tensor
        def _(pe):
            pe.wait_ge(got_x, 16)
            pe.wait_ge(got_w, 32)
            for t in range(NT):
                mm = pe.matmul(psum[0:TP, t // QK_BANK, (t % QK_BANK) * NQK:(t % QK_BANK + 1) * NQK],
                               xT[:, t * TP:(t + 1) * TP], W("qk"), start=True, stop=True)
                if t % QK_BANK == QK_BANK - 1 or t == NT - 1:
                    mm.then_inc(qk_made, 1)
            for b in range(B):
                at = 64 * (b % 2)
                mm = pe.matmul(psum[at:at + T, 6, (b // 2) * 32:(b // 2) * 32 + 32],
                               xT[:, b * T:(b + 1) * T], W("v"), start=True, stop=True)
            mm.then_inc(v_made, 1)
            pe.wait_ge(qk_out, 6)
            pe.wait_ge(sq_made, 6)
            for n, name in enumerate(("xq", "xqp", "xk", "xkp", "xv")):
                mm = pe.matmul(psum[:, 0, n:n + 1], W(name), W("beta"), start=True, stop=True)
            mm.then_inc(bias_made, 1)
            pe.wait_ge(w_fold, 1)
            pe.matmul(psum[0:TP, 1, 0:D], prep["off_cols"][:, 0:TP], W("out"), start=True, stop=True)\
              .then_inc(bias_made, 1)
            pe.wait_ge(qk_rot, 2)
            pe.wait_ge(bias_out, 2)
            for n, src in enumerate((qr, kr)):
                for t in range(NT):
                    mm = pe.transpose(psum[:, 4 * n + t // 4, (t % 4) * TP:(t % 4 + 1) * TP], src[:, t, :],
                                      ident[0:TP, 0:TP])
                    if t % 4 == 3:
                        mm.then_inc(qkT_made, 1)
            pe.wait_ge(kT_out, 4)
            pe.wait_ge(qT_out, 4)
            for n in range(NP + 1):
                if n < NP:
                    pe.wait_ge(spread_v, n + 1)
                    pe.wait_ge(spread_p, n + 1)
                    if n == 0:
                        pe.wait_ge(padded, 1)
                    if n >= 2:
                        pe.wait_ge(e_made, n - 1)
                    for h in range(2):
                        for r in range(2):
                            b = 2 * n + r
                            mm = pe.matmul(psum[64 * r:64 * r + 64, 2 * (n % 2) + h, 0:HALF],
                                           kT[:, b * T:b * T + 64], qbd[:, n % 2, r, h * 8:(h + 1) * 8, :],
                                           start=True, stop=True)
                    mm.then_inc(s_made, 1)
                if n >= 1:
                    m = n - 1
                    pe.wait_ge(masked, n)
                    if n >= 3:
                        pe.wait_ge(o_out, n - 2)
                    for r in range(2):
                        for g in range(NKV):
                            mm = pe.matmul(psum[32 * g:32 * g + 32, 4 + 2 * (m % 2) + r, 0:GC],
                                           vx[64 * r:64 * r + T, m, g, :],
                                           prob[64 * r:64 * r + T, m % 3, g * GC:(g + 1) * GC],
                                           start=True, stop=True)
                    mm.then_inc(o_made, 1)
            pe.wait_ge(o_out, NP)
            for t in range(NT):
                if t >= 4:
                    pe.wait_ge(y_out, t - 3)
                for l in range(GH):
                    mm = pe.transpose(psum[0:TP, t % 4, l * 128:(l + 1) * 128], oAll[:, l, t * TP:(t + 1) * TP],
                                      ident)
                mm.then_inc(oT_made, 1)
            for t in range(NT):
                pe.wait_ge(y_out, t + 1)
                mm = pe.transpose(psum[:, 4 + t // 4, (t % 4) * TP:(t % 4 + 1) * TP], y[:, t, 0:D],
                                  ident[0:TP, 0:TP])
                if t % 4 == 3:
                    mm.then_inc(yT_made, 1)
            for t in range(NT):
                pe.wait_ge(yT_out, t // 4 + 1)
                mm = pe.matmul(psum[0:TP, t // 4, (t % 4) * 128:(t % 4 + 1) * 128], yT[:, t * TP:(t + 1) * TP],
                               W("proj"), start=True, stop=True)
                if t % 4 == 3:
                    mm.then_inc(pr_made, 1)
            for t in range(NT):
                pe.wait_ge(xn_made, t + 1)
                mm = pe.transpose(psum[:, 4 + t // 4, (t % 4) * TP:(t % 4 + 1) * TP], y[:, t, 0:D],
                                  ident[0:TP, 0:TP])
                if t % 4 == 3:
                    mm.then_inc(xnT_made, 1)
            for n in range(4):
                pe.wait_ge(xnT_out, 4 if n == 0 else n + 1)
                pe.matmul(psum[:, n, 0:448], prep["xq"][:], xnT[:, n * 448:(n + 1) * 448], start=True, stop=True)
                pe.matmul(psum[:, 4 + n, 0:448], prep["xqp"][:], xnT[:, n * 448:(n + 1) * 448],
                          start=True, stop=True).then_inc(q_made, 1)

        @block.scalar
        def _(act):
            for n in range(6):
                act.wait_ge(qk_made, n + 1)
                m = min(QK_BANK, NT - QK_BANK * n)
                act.copy(qk[:, QK_BANK * n:QK_BANK * n + m, :],
                         psum[0:TP, n, 0:m * NQK].rearrange("p (t c) -> p t c", c=NQK)).then_inc(qk_out, 1)
                act.activation(sq[:, QK_BANK * n * NQK:(QK_BANK * n + m) * NQK], psum[0:TP, n, 0:m * NQK],
                               ACT.Square).then_inc(sq_made, 1)
            act.wait_ge(table_got, 32)
            act.copy(hatr, hat32).then_inc(table_made, 1)
            act.wait_ge(nrm_in, 1)
            act.activation(nrm[:, 1, :], nrm[:, 0, :], ACT.Sqrt).then_inc(nrm_out, 1)
            act.copy(prob[:].rearrange("p c (h t) -> p c h t", h=NH).bitcast(F32R),
                     strided(node32[:], [[T, BQ], [0, NH], [1, T]])).then_inc(table_made, 1)
            for n in range(4):
                act.wait_ge(qkT_made, n + 1)
                act.copy(qT[:, n * 448:(n + 1) * 448], psum[:, n, 0:448]).then_inc(qT_out, 1)
            for n in range(NP + 1):
                if n < NP:
                    if n == 0:
                        act.wait_ge(table_put, 32)
                    act.wait_ge(s_made, n + 1)
                    if n >= 3:
                        act.wait_ge(o_made, n - 2)
                    act.activation(prob[:, n % 3, :].rearrange("p (a c) -> p a c", a=2),
                                   psum[:, 2 * (n % 2):2 * (n % 2) + 2, 0:HALF], ACT.Exp,
                                   scale=HD ** -0.5).then_inc(e_made, 1)
                if n >= 1:
                    act.wait_ge(o_made, n)
                    m = n - 1
                    act.copy(oAll[:, :, m * TP:(m + 1) * TP].rearrange("p l (r q) -> p r l q", r=2),
                             psum[:, 4 + 2 * (m % 2):6 + 2 * (m % 2), 0:GC].rearrange("p r (l q) -> p r l q", l=GH))\
                       .then_inc(o_out, 1)
            for n in range(4):
                act.wait_ge(yT_made, n + 1)
                act.copy(yT[:, n * 448:(n + 1) * 448], psum[:, 4 + n, 0:448]).then_inc(yT_out, 1)
            act.wait_ge(start["rstd_made"], RSTD_STEPS)
            for c in range(NC):
                at = start["xin"][:, 0, c, :]
                act.activation(at, at, ACT.Identity, bias=start["shift"][:, c:c + 1],
                               scale=start["rstd"][:, c:c + 1]).then_inc(start["xn_made"], 1)
            for n in range(2):
                act.wait_ge(std_in, n + 1)
                act.activation(rstd[:, 0, :], rstd[:, 0, :], ACT.Sqrt).then_inc(std_out, 1)
            for n in range(4):
                act.wait_ge(xnT_made, n + 1)
                act.copy(xnT[:, n * 448:(n + 1) * 448], psum[:, 4 + n, 0:448]).then_inc(xnT_out, 1)

        @block.vector
        def _(dve):
            own = Own(dve, own_v)
            own.mark(dve.memset(vx[:], 0.0))
            own.settle()
            own.link(dve.memset(vx[:, :, :, HD:HD + 1], 1.0))
            dve.wait_ge(v_made, 1)
            for at in (0, 64):
                own.mark(dve.tensor_copy(vx[at:at + T, :, :, 0:HD],
                                         psum[at:at + T, 6, 0:512].rearrange("p (b g d) -> p b g d", b=NP, g=NKV)))
            own.mark(dve.memset(prep["off_cols"][:], 0.0))
            own.settle()
            for name in ("xq", "xqp", "xk", "xkp", "xv"):
                own.mark(dve.tensor_scalar(prep[name][:], W(name), W("gamma"), None, ALU.mult))
            dve.wait_ge(bias_made, 1)
            dve.tensor_copy(prep["off"][:], psum[:, 0, 0:5]).then_inc(bias_out, 1)
            dve.wait_ge(bias_out, 1)
            dve.tensor_scalar(prep["off_cols"][:], prep["off_cols"][:], prep["off"][:, 4:5], None, ALU.add)\
               .then_inc(w_fold, 1)
            dve.wait_ge(bias_made, 2)
            dve.tensor_tensor(prep["b_att"][:], psum[0:TP, 1, 0:D], W("b_out")[0:TP], ALU.add).then_inc(bias_out, 1)
            dve.wait_ge(qk_out, 6)
            own.mark(dve.tensor_tensor(heads(t1), heads(qk), strided(C("cosa")[0:TP], [[0, NT * NHK], [1, HD]]),
                                       ALU.mult))
            dve.wait_ge(sq_made, 6)
            dve.tensor_reduce(nrm[:, 0, :], sq.rearrange("p (h d) -> p h d", d=HD), AX.X, ALU.add).then_inc(nrm_in, 1)
            dve.wait_ge(sin_made, 2)
            own.settle()
            own.mark(dve.tensor_tensor(flat(t1), flat(t1), flat(t2), ALU.add))
            dve.wait_ge(nrm_out, 1)
            own.link(dve.tensor_scalar(nrm[:, 2, :], nrm[:, 1, :], EPS_NORM, None, ALU.add))
            own.link(dve.reciprocal(nrm[:, 0, :], nrm[:, 2, :]))
            dve.tensor_tensor(qr[:].rearrange("p t (h d) -> p t h d", d=HD),
                              strided(t1[:], [[NQK, NT], [HD, NH], [1, HD]]),
                              strided(nrm[:, 0, :], [[NHK, NT], [1, NH], [0, HD]]), ALU.mult).then_inc(qk_rot, 1)
            for g in range(NKV):
                last = dve.tensor_tensor(
                    kr[:, :, 32 * g:32 * g + 32].rearrange("p t (r d) -> p t r d", r=GH),
                    strided(t1[:], [[NQK, NT], [0, GH], [1, HD]], D + HD * g),
                    strided(nrm[:, 0, :], [[NHK, NT], [0, GH], [0, HD]], NH + g), ALU.mult)
            last.then_inc(qk_rot, 1)
            dve.wait_ge(start["ctx_got"][0], 16)
            for c in range(NC):
                dve.bn_stats(start["stats"][:, c, :], start["xin"][:, 0, c, :]).then_inc(start["stats_made"], 1)
            dve.wait_ge(start["stats_made"], NC)
            for c in range(NC):
                dve.bn_aggr(start["mv"][:, c, :], start["stats"][:, c, :]).then_inc(start["var_made"], 1)
            dve.wait_ge(start["var_made"], NC)
            for step in range(3):
                guess(dve, start, 0, step)
            for n in range(4):
                dve.wait_ge(qkT_made, 4 + n + 1)
                dve.tensor_copy(kT[:, n * 448:(n + 1) * 448], psum[:, 4 + n, 0:448]).then_inc(kT_out, 1)
            dve.wait_ge(qT_out, 4)

            dve.memset(kT[:, N:], 0.0).then_inc(padded, 1)
            dve.wait_ge(table_put, 32)

            for n in range(NP + 1):
                if n < NP:
                    if n >= 2:
                        dve.wait_ge(s_made, n - 1)
                    dve.tensor_tensor(qbd[:, n % 2, 0, :, :],
                                      strided(qT[:, 2 * n * T:(2 * n + 1) * T], [[0, NH], [1, T]]),
                                      strided(C("mask16"), [[1, NH], [0, T]]), ALU.mult).then_inc(spread_v, 1)
                if n >= 1:
                    dve.wait_ge(e_made, n)
                    p = prob[:, (n - 1) % 3, :].rearrange("p (h q) -> p h q", h=NH)
                    dve.tensor_tensor(p, p, strided(C("causal"), [[0, NH], [1, T]]), ALU.mult).then_inc(masked, 1)
            for t in range(NT):
                dve.wait_ge(oT_made, t + 1)
                o4 = psum[0:TP, t % 4, 0:512].rearrange("p (l g c) -> p l g c", l=GH, g=NKV)
                own.link(dve.reciprocal(nrm[:, t % 3, 0:16].rearrange("p (l g) -> p l g", l=GH), o4[:, :, :, HD]))
                dve.tensor_tensor(y[:, t, 0:D].rearrange("p (g l d) -> p l g d", g=NKV, l=GH), o4[:, :, :, 0:HD],
                                  strided(nrm[:, t % 3, 0:16], [[4, GH], [1, NKV], [0, HD]]), ALU.mult)\
                   .then_inc(y_out, 1)
            dve.wait_ge(got_r, 16)
            for n in range(4):
                dve.wait_ge(pr_made, n + 1)
                own.mark(dve.tensor_tensor(res[:, 4 * n:4 * n + 4, 0:D],
                                           psum[0:TP, n, 0:512].rearrange("p (t d) -> p t d", t=4),
                                           xr[:, 4 * n:4 * n + 4, :], ALU.add))
            own.settle()
            layernorm_dve(own, TP, res[:, :, 0:D], x1, stats, mv, rstd, std_in, (std_out, 1))
            dve.wait_ge(yT_made, 4)
            layernorm_dve(own, TP, x1, y[:, :, 0:D], stats, mv, rstd, std_in, (std_out, 2), xn_made)
            for n in range(4):
                cols = slice(n * 448, (n + 1) * 448)
                q, hi, lo = oAll[:, 0, cols], kT[:, cols].bitcast(F32R), oAll[:, 1, cols].bitcast(F32R)
                dve.wait_ge(q_made, n + 1)
                for m, tab in ((0, "cosq"), (1, "sinq")):
                    own.mark(dve.scalar_tensor_tensor(
                        out=oAll[:, 2 + m, cols].rearrange("p (b q) -> p b q", q=T),
                        in0=psum[:, 4 * m + n, 0:448].rearrange("p (b q) -> p b q", q=T),
                        scalar=prep["off"][:, m:m + 1], in1=strided(C(tab), [[0, 8], [1, T]]),
                        op0=ALU.add, op1=ALU.mult))
                own.settle()
                own.link(dve.tensor_tensor(q, oAll[:, 2, cols], oAll[:, 3, cols], ALU.add))
                dve.tensor_copy(hi, q).then_inc(q_split, 1)
                dve.wait_ge(q_split, 2 * n + 1)
                dve.tensor_tensor(lo, q, hi.bitcast(F32), ALU.subtract).then_inc(q_split, 1)

        @block.gpsimd
        def _(pool):
            pool.wait_ge(qk_out, 6)
            for a in range(2):
                lo, hi = 4 * a, 4 - 4 * a
                pool.tensor_tensor(heads(t2)[:, :, lo:lo + 4], heads(qk)[:, :, hi:hi + 4],
                                   strided(C("sina")[0:TP], [[0, NT * NHK], [1, 4]], lo), ALU.mult)\
                    .then_inc(sin_made, 1)
            pool.memset(start["vx"][:], 1.0)
            pool.memset(start["whole"][:, 0, :], 0.0).then_inc(whole_made, 1)
            pool.memset(start["whole"][:, 1, :], 1.5).then_inc(whole_made, 1)
            pool.wait_ge(table_put, 32)
            pool.wait_ge(qT_out, 4)
            for n in range(NP):
                if n >= 2:
                    pool.wait_ge(s_made, n - 1)
                at = (2 * n + 1) * T
                pool.tensor_tensor(qbd[:, n % 2, 1, :, :], strided(qT[:, at:at + T], [[0, NH], [1, T]]),
                                   strided(C("mask16"), [[1, NH], [0, T]]), ALU.mult).then_inc(spread_p, 1)
            pool.wait_ge(whole_made, 2)
            inverse_deviation(pool, start, 0)


def cross_attention(nc, psum, wt, ct, xq_split, tables, o_dram, prep, start, ctx_in):
    hat_dram, node_dram = tables
    C = lambda n: ct[:, C_AT[n][0]:C_AT[n][1]]
    ident = C("ident")
    NVG = NH // VH
    OC = VH * T
    with ExitStack() as ctx:
        k = Core(nc, ctx)
        xin, tab, vx, whole, ctx_got, tab_got = (start[n] for n in ("xin", "tab", "vx", "whole", "ctx_got", "tab_got"))
        stats, mv, half, bits, newton, rstd, shift = (start[n] for n in CONTEXT_ARRAYS)
        stats_made, var_made, guess_made, rstd_made, xn_made = (start[n] for n in CONTEXT_SIGNALS)
        xT = k.sb("b_xT", [128, 2, S])
        kt = k.sb("b_kt", [128, NB, 2, KB])
        k32 = k.sb("b_k32", [128, KB])
        khi = k.sb("b_khi", [128, 2, S], F32R)
        klo = k.sb("b_klo", [128, 2, S], F32R)
        stack = k.sb("b_stack", [128, 2, NG, S], F32R)
        qs = k.sb("b_qs", [96, 2, NG, T])
        qh = k.sb("b_qh", [128, 2, T])
        qstack = k.sb("b_qstack", [97 + 2 * HAT, 2, QC, NG, GC], F32R)
        qmax = k.sb("b_qmax", [128, 2, NH, T], F32R)
        prob = k.sb("b_prob", [CH, 3, HQ])
        mx = k.sb("b_mx", [128, NMX, NB])
        mx1 = k.sb("b_mx1", [128, NMX])
        mneg = k.sb("b_mneg", [NMX, 128], F32R)
        o_sb = k.sb("b_o", [128, 2, 2 * OC])

        q_got = [k.sem("b_q_even"), k.sem("b_q_odd")]
        stack_got = [k.sem("b_stack_even"), k.sem("b_stack_odd")]
        m_got = [k.sem("b_m_even"), k.sem("b_m_odd")]
        o_put = [k.sem("b_o_even"), k.sem("b_o_odd")]
        bias_got = [[k.sem(f"b_bias_{b}_{j}") for j in range(QC)] for b in ("even", "odd")]
        hat_put = k.sem("b_hat_put")
        k_turned = k.sem("b_k_turned")
        xT_made, xT_out, k_made, k_rot, k_sum, k_hi, k_split = (
            k.sem("b_xT_made"), k.sem("b_xT_out"), k.sem("b_k_made"), k.sem("b_k_rot"), k.sem("b_k_sum"),
            k.sem("b_k_hi"), k.sem("b_k_split"))
        v_made, v_out = k.sem("b_v_made"), k.sem("b_v_out")
        qm_made, qk_made = k.sem("b_qm_made"), k.sem("b_qk_made")
        g_made, g_red, g_max, gT_made, m_made = (k.sem("b_g_made"), k.sem("b_g_red"), k.sem("b_g_max"),
                                                 k.sem("b_gT_made"), k.sem("b_m_made"))
        s_made, e_made, pv_made, o_out = k.sem("b_s_made"), k.sem("b_e_made"), k.sem("b_pv_made"), k.sem("b_o_out")
        block = ctx.enter_context(nc.Block())

        BX, BK = 5, (6, 7)
        MAXIMA = (3, 2, 2, 3, 2, 3, 3, 3, 0)
        assert sum(MAXIMA) == NB * NMX
        STATS_AT = (4, 6, 8, 10, 12, 14, 16)
        GUESS_AT = (17, 18, 19)
        FIRST, LAST = 2, 27

        def periods(eng, period):
            for p in range(-3, FIRST):
                period(0, p)
            with eng.Fori(FIRST // 2, (LAST + 1) // 2) as i:
                period(i, 0)
                period(i, 1)
            for p in range(LAST + 1, B):
                period(0, p)

        def live(i, n):
            return not isinstance(i, int) or 0 <= n < B

        def later(i, n):
            return live(i, n) and (not isinstance(i, int) or n > 0)

        def seq(i, n):
            return 2 * i + n

        def pair(i, n):
            return i + n // 2

        @block.sync
        def _(sp):
            for b in range(2):
                for g in range(NG):
                    sp.dma_start(stack[96:97 + 2 * HAT, b, g, :].bitcast(F32), hat_dram).then_inc(hat_put, 16)

            def bias(n, c):
                row = 32 * (c // BQ)
                sp.dma_start(qstack[97:97 + 2 * HAT, n % 2, c % QC, :, :].rearrange("p g c -> p (g c)").bitcast(F32),
                             node_dram[row:row + 2 * HAT, (c % BQ) * HQ:(c % BQ + 1) * HQ])\
                  .then_inc(bias_got[n % 2][c % QC], 16)

            for n in range(2):
                for c in range(QC):
                    bias(n, c)

            def next_context(i, n):
                positive(sp, xT_made, NB * (seq(i, n) - 1))
                sp.dma_start(xin[:, n % 2, :, :], ctx_in[seq(i, n)].rearrange("(c p) d -> p c d", p=CH))\
                  .then_inc(ctx_got[n % 2], 16)

            def next_queries(i, n):
                positive(sp, qk_made, QC * (seq(i, n) - 1))
                positive(sp, qm_made, seq(i, n) - 1)
                src = xq_split.rearrange("s (g r) (b t) -> s r b g t", g=NG, t=T)
                for row, part in ((0, 0), (1, 1), (2, 0)):
                    sp.dma_start(qs[32 * row:32 * row + 32, n % 2, :, :], src[part, :, seq(i, n)])\
                      .then_inc(q_got[n % 2], 16)
                sp.dma_start(qh[:, n % 2, :], xq_split.rearrange("s r (b t) -> s b r t", t=T)[0, seq(i, n)])\
                  .then_inc(q_got[n % 2], 16)

            def stack_keys(i, n, g):
                if g == 0:
                    sp.wait_ge(k_split, NB * (seq(i, n) + 1))
                    positive(sp, s_made, NC * (seq(i, n) - 1))
                for row, part in ((0, khi), (1, khi), (2, klo)):
                    sp.dma_start(stack[32 * row:32 * row + 32, n % 2, g, :].bitcast(F32),
                                 part[32 * g:32 * g + 32, n % 2, :].bitcast(F32)).then_inc(stack_got[n % 2], 16)

            def negated_maxima(i, n):
                sp.wait_ge(m_made, seq(i, n) + 1)
                for j in range(QC):
                    sp.dma_start(qstack[96:97, n % 2, j, :, :].rearrange("p g c -> p (g c)").bitcast(F32),
                                 mneg[:].bitcast(F32)).then_inc(m_got[n % 2], 16)

            def sums(i, n):
                sp.wait_ge(o_out, seq(i, n) + 1)
                sp.dma_start(o_dram[pair(i, n), :, :, n % 2, :],
                             o_sb[:, n % 2, :].rearrange("p (c t) -> p c t", t=T)).then_inc(o_put[n % 2], 16)

            def period(i, p):
                for c in range(NC):
                    if c == 1 and live(i, p + 2):
                        next_queries(i, p + 2)
                    if c == 2 and live(i, p - 1):
                        sums(i, p - 1)
                    if c == 7 and live(i, p + 4) and (not isinstance(i, int) or p + 4 >= 2):
                        next_context(i, p + 4)
                    if c == NC - 2 and live(i, p + 1):
                        negated_maxima(i, p + 1)
                    if live(i, p) and (c + QC < NC or live(i, p + 2)):
                        sp.wait_ge(s_made, NC * seq(i, p) + c + 1)
                        bias(p, (c + QC) % NC)
                    if c in (3, 5, 6, 8) and live(i, p + 1):
                        stack_keys(i, p + 1, (3, 5, 6, 8).index(c))

            periods(sp, period)
            sums(0, B - 1)
            for s in o_put:
                sp.wait_ge(s, 16 * B // 2)

        @block.tensor
        def _(pe):
            pe.wait_ge(hat_put, 16 * 2 * NG)

            def values(i, n, c):
                positive(pe, e_made, NC * seq(i, n) + c + 1)
                if c == 0:
                    pe.wait_ge(v_out, NB * (seq(i, n) + 1))
                    positive(pe, o_out, seq(i, n))
                for half in range(NVG // 4):
                    for j in range(4):
                        g = 2 * j + half
                        mm = pe.matmul(psum[32 * j:32 * j + 32, 4, half * OC:(half + 1) * OC],
                                       vx[:, n % 2, c, VH * VW * g:VH * VW * g + 32],
                                       prob[:, c % 3, OC * g:OC * (g + 1)],
                                       start=(c == 0 and half == 0), stop=(c == NC - 1), skip_group_check=True)
                mm.then_inc(pv_made, 1)

            def scores(i, n, c):
                if c == 0:
                    pe.wait_ge(stack_got[n % 2], 16 * 3 * NG * (pair(i, n) + 1))
                    pe.wait_ge(qk_made, QC * (seq(i, n) + 1))
                    pe.wait_ge(m_got[n % 2], 16 * QC * (pair(i, n) + 1))
                pe.wait_ge(bias_got[n % 2][c % QC], 16 * (CQ * pair(i, n) + c // QC + 1))
                positive(pe, e_made, NC * seq(i, n) + c - 1)
                for g in range(NG):
                    mm = pe.matmul(psum[0:CH, 2 * (c % 2) + g // 2, GC * (g % 2):GC * (g % 2 + 1)],
                                   stack[0:97 + 2 * HAT, n % 2, g, c * CH:(c + 1) * CH],
                                   qstack[:, n % 2, c % QC, g, :], start=True, stop=True)
                mm.then_inc(s_made, 1)

            def turn(i, n, r):
                if r == 0:
                    pe.wait_ge(xn_made, NC * (seq(i, n) + 1))
                    positive(pe, v_out, NB * (seq(i, n) - 1))
                positive(pe, xT_out, NB * seq(i, n) + r)
                for c in range(4):
                    mm = pe.transpose(psum[:, BX, c * CH:(c + 1) * CH], xin[:, n % 2, 4 * r + c, :],
                                      ident[0:CH, 0:CH])
                mm.then_inc(xT_made, 1)

            def keys(i, n, r):
                pe.wait_ge(xT_out, NB * seq(i, n) + r + 1)
                if r == 1:
                    positive(pe, m_made, seq(i, n))
                if r < 2:
                    positive(pe, g_red, NB * NMX * seq(i, n) - 1 + r)
                else:
                    pe.wait_ge(k_rot, 2 * (NB * seq(i, n) + 1))
                pe.matmul(psum[:, BK[(r + 1) % 2], 0:KB], prep["xk"][:], xT[:, n % 2, r * KB:(r + 1) * KB],
                          start=True, stop=True).then_inc(k_made, 1)

            def vals(i, n, r):
                if r == 0:
                    positive(pe, xT_out, NB * min(seq(i, n) + 2, B) if isinstance(i, int) else NB * (seq(i, n) + 2))
                positive(pe, v_out, NB * seq(i, n) + r)
                for c in range(4):
                    at = (4 * r + c) * CH
                    mm = pe.matmul(psum[0:CH, BX, c * D:(c + 1) * D], xT[:, n % 2, at:at + CH], prep["xv"][:],
                                   start=True, stop=True)
                mm.then_inc(v_made, 1)

            def maxima(i, n, j):
                r, m = divmod(j, NMX)
                if j == 0:
                    pe.wait_ge(qm_made, seq(i, n) + 1)
                    positive(pe, k_rot, 2 * (NB * seq(i, n) + 2))
                if j == 1:
                    pe.wait_ge(k_rot, 2 * NB * (seq(i, n) + 1))
                if m == 0:
                    pe.wait_ge(k_hi, NB * seq(i, n) + r + 1)
                positive(pe, g_red, NB * NMX * seq(i, n) + j - 1)
                pe.matmul(psum[:, BK[j % 2], 0:KB],
                          qmax[:, n % 2, :, :].rearrange("p h q -> p (h q)")[:, m * 128:(m + 1) * 128],
                          khi[:, n % 2, r * KB:(r + 1) * KB], start=True, stop=True).then_inc(g_made, 1)

            def period(i, p):
                for c in range(NC):
                    first, beyond = sum(MAXIMA[:c]), sum(MAXIMA[:c + 1])
                    if not live(i, p + 1):
                        beyond = first
                    if live(i, p):
                        scores(i, p, c)
                    if 8 <= c < 11 and live(i, p + 2):
                        keys(i, p + 2, c - 8)
                    for j in range(first, min(first + 1, beyond)):
                        maxima(i, p + 1, j)
                    if c == 0 and live(i, p - 1):
                        values(i, p - 1, NC - 1)
                    if c > 0 and live(i, p):
                        values(i, p, c - 1)
                    for j in range(first + 1, min(first + 2, beyond)):
                        maxima(i, p + 1, j)
                    if c == 8 and live(i, p + 1):
                        pe.wait_ge(g_max, seq(i, p + 1) + 1)
                        pe.transpose(psum[0:NMX, BK[0], 0:128], mx1[:], ident).then_inc(gT_made, 1)
                    if 6 <= c < 9 and live(i, p + 1):
                        vals(i, p + 1, c - 6)
                    if 3 <= c < 6 and live(i, p + 2):
                        turn(i, p + 2, c - 3)
                    for j in range(first + 2, beyond):
                        maxima(i, p + 1, j)

            periods(pe, period)
            values(0, B - 1, NC - 1)

        @block.scalar
        def _(act):
            def out(i, n):
                act.wait_ge(pv_made, NC * (seq(i, n) + 1))
                positive(act, o_put[n % 2], 16 * pair(i, n))
                act.copy(o_sb[:, n % 2, :], psum[:, 4, 0:2 * OC]).then_inc(o_out, 1)

            def period(i, p):
                for c in range(NC):
                    if live(i, p):
                        act.wait_ge(s_made, NC * seq(i, p) + c + 1)
                        positive(act, pv_made, NC * seq(i, p) + c - 2)
                        act.activation(prob[:, c % 3, :].rearrange("p (a c) -> p a c", a=2),
                                       psum[0:CH, 2 * (c % 2):2 * (c % 2) + 2, 0:HALF], ACT.Exp).then_inc(e_made, 1)
                    if c == 0 and live(i, p - 1):
                        out(i, p - 1)
                    n, step = (p + 3, c - 9) if c >= 9 else (p + 2, c + 3)
                    if step < NC // 2 and later(i, n):
                        act.wait_ge(rstd_made, RSTD_STEPS * (seq(i, n) + 1))
                        for t in (2 * step, 2 * step + 1):
                            at = xin[:, n % 2, t, :]
                            act.activation(at, at, ACT.Identity, bias=shift[:, t:t + 1], scale=rstd[:, t:t + 1])\
                               .then_inc(xn_made, 1)
                    if live(i, p + 2) and 3 <= c < 6:
                        r, n = c - 3, p + 2
                        act.wait_ge(xT_made, NB * seq(i, n) + r + 1)
                        act.copy(xT[:, n % 2, r * KB:(r + 1) * KB], psum[:, BX, 0:KB]).then_inc(xT_out, 1)
                    if live(i, p + 1) and 6 <= c < 9:
                        r, n = c - 6, p + 1
                        act.wait_ge(v_made, NB * seq(i, n) + r + 1)
                        act.copy(vx[:, n % 2, 4 * r:4 * r + 4, 0:NH * VW]
                                 .rearrange("p c (h d) -> p c h d", h=NH)[:, :, :, 0:HD],
                                 psum[0:CH, BX, 0:512].rearrange("p (c h d) -> p c h d", c=4, h=NH))\
                           .then_inc(v_out, 1)

            periods(act, period)
            out(0, B - 1)

        @block.vector
        def _(dve):
            partner = [f // HD * HD + (f % HD + HD // 2) % HD for f in range(32)]

            def period(i, p):
                for j in range(NB * NMX):
                    n = p + 3
                    step = STATS_AT.index(j) if j in STATS_AT and later(i, n) else None
                    if step == 0:
                        dve.wait_ge(ctx_got[n % 2], 16 * (pair(i, n) + 1))
                    elif step is not None:
                        dve.wait_ge(stats_made, NC * seq(i, n) + 2 * step)
                    if live(i, p + 1):
                        m = p + 1
                        dve.wait_ge(g_made, NB * NMX * seq(i, m) + j + 1)
                        dve.tensor_reduce(mx[:, j % NMX, j // NMX:j // NMX + 1], psum[:, BK[j % 2], 0:KB], AX.X,
                                          ALU.max).then_inc(g_red, 1)
                    if step == 0:
                        positive(dve, rstd_made, RSTD_STEPS * seq(i, n))
                    if step is not None and step < NC // 2:
                        for c in (2 * step, 2 * step + 1):
                            dve.bn_stats(stats[:, c, :], xin[:, n % 2, c, :]).then_inc(stats_made, 1)
                    if step:
                        for c in (2 * step - 2, 2 * step - 1):
                            dve.bn_aggr(mv[:, c, :], stats[:, c, :]).then_inc(var_made, 1)
                    if later(i, n) and j in GUESS_AT:
                        step = GUESS_AT.index(j)
                        if step == 0:
                            dve.wait_ge(var_made, NC * (seq(i, n) + 1))
                            positive(dve, xn_made, NC * seq(i, n))
                        guess(dve, start, seq(i, n), step)
                n = p + 1
                if live(i, n):
                    dve.wait_ge(g_red, NB * NMX * (seq(i, n) + 1))
                    dve.tensor_reduce(mx1[:], mx[:], AX.X, ALU.max).then_inc(g_max, 1)

                def negate():
                    n = p + 1
                    dve.wait_ge(gT_made, seq(i, n) + 1)
                    positive(dve, m_got[(n - 1) % 2], 16 * QC * (pair(i, n - 1) + 1))
                    dve.tensor_scalar(mneg[:], psum[0:NMX, BK[0], 0:128], -1.0, None, ALU.mult).then_inc(m_made, 1)

                if live(i, p + 1) and not live(i, p + 2):
                    negate()
                n = p + 2
                if live(i, n):
                    for r in range(NB):
                        keys, t = psum[:, BK[(r + 1) % 2], 0:KB], kt[:, r, :, :]
                        rope = tab[:, :, r * KB:(r + 1) * KB]
                        dve.wait_ge(k_made, NB * seq(i, n) + r + 1)
                        positive(dve, k_sum, NB * seq(i, n) + r - 2)
                        dve.scalar_tensor_tensor(out=t[:, 0, :], in0=keys, scalar=prep["off"][:, 2:3],
                                                 in1=rope[:, 0, :], op0=ALU.add, op1=ALU.mult).then_inc(k_rot, 1)
                        if r == 0 and live(i, p + 1):
                            negate()
                        dve.stream_shuffle(mask=partner, out=t[:, 1, :], in_=keys).then_inc(k_rot, 1)
                        dve.wait_ge(k_rot, 2 * (NB * seq(i, n) + r + 1))
                        dve.scalar_tensor_tensor(out=t[:, 1, :], in0=t[:, 1, :], scalar=prep["off"][:, 3:4],
                                                 in1=rope[:, 1, :], op0=ALU.add, op1=ALU.mult).then_inc(k_turned, 1)
            dve.wait_ge(tab_got, 16)
            periods(dve, period)

        @block.gpsimd
        def _(pool):
            mask4 = C("mask4")

            def spread_max(i, n):
                pool.wait_ge(q_got[n % 2], 64 * (pair(i, n) + 1))
                positive(pool, g_made, NB * NMX * (seq(i, n) - 1))
                pool.tensor_tensor(qmax[:, n % 2, :, :], strided(qh[:, n % 2, :], [[0, NH], [1, T]]),
                                   strided(C("mask16"), [[1, NH], [0, T]]), ALU.mult).then_inc(qm_made, 1)

            def period(i, p):
                n = p + 1
                if live(i, n):
                    positive(pool, s_made, NC * (seq(i, n) - 1))
                    pool.wait_ge(q_got[n % 2], 64 * (pair(i, n) + 1))
                    for j in range(QC):
                        pool.tensor_tensor(qstack[0:96, n % 2, j, :, :].rearrange("p g (h q) -> p g h q", h=GH),
                                           strided(qs[:, n % 2, :, :], [[T, NG], [0, GH], [1, T]]),
                                           strided(mask4[0:96], [[0, NG], [1, GH], [0, T]]), ALU.mult)\
                            .then_inc(qk_made, 1)
                if live(i, p + 2):
                    spread_max(i, p + 2)
                if later(i, p + 3):
                    inverse_deviation(pool, start, seq(i, p + 3))
                n = p + 2
                if live(i, n):
                    for r in range(NB):
                        cols = slice(r * KB, (r + 1) * KB)
                        t = kt[:, r, :, :]
                        pool.wait_ge(k_turned, NB * seq(i, n) + r + 1)
                        if r == 0:
                            positive(pool, stack_got[n % 2], 16 * 3 * NG * pair(i, n))
                            positive(pool, g_made, NB * NMX * (seq(i, n) - 1))
                        positive(pool, k_split, NB * seq(i, n) + r)
                        pool.tensor_tensor(khi[:, n % 2, cols], t[:, 0, :], t[:, 1, :], ALU.add).then_inc(k_hi, 1)
                        pool.tensor_tensor(k32[:], t[:, 0, :], t[:, 1, :], ALU.add).then_inc(k_sum, 1)
                        pool.wait_ge(k_hi, NB * seq(i, n) + r + 1)
                        pool.wait_ge(k_sum, NB * seq(i, n) + r + 1)
                        pool.tensor_tensor(klo[:, n % 2, cols], k32[:], khi[:, n % 2, cols].bitcast(F32),
                                           ALU.subtract).then_inc(k_split, 1)

            periods(pool, period)


def mix_and_experts(nc, psum, wt, ct, x1, o_dram, queue, made, prep, ins, out):
    w1, b1, w2, b2 = ins
    queue_rows = queue.rearrange("(j p) d -> p j d", p=TP)
    made_rows = made.rearrange("(n t p) d -> p n t d", n=TOPK, p=TP)
    W = lambda n: wt[:, W_AT[n][0]:W_AT[n][1]]
    C = lambda n: ct[:, C_AT[n][0]:C_AT[n][1]]
    ident = C("ident")
    OC = VH * T
    SEG = N // 4
    with ExitStack() as ctx:
        k = Core(nc, ctx)
        o = k.sb("c_o", [128, NT, 2 * VH, TP])
        att = k.sb("c_att", [TP, NT, D])
        gated = k.sb("c_gated", [TP, NT, D])
        x2 = k.sb("c_x2", [TP, NT, D])
        cT = k.sb("c_cT", [128, N])
        x2T = cT
        rden = k.sb("c_rden", [TP, 2, NH])
        mv = k.sb("c_mv", [TP, NT, 2])
        stats = k.sb("c_stats", [TP, NT, 6])
        rstd = k.sb("c_rstd", [TP, 2, NT])
        rt = k.sb("c_rt", [TP, 8, NT, E])
        col = k.sb("c_col", [TP, 2, NT])
        top = k.sb("c_top", [TP, NT, 8])
        topi = k.sb("c_topi", [TP, NT, 8], U32)
        topf = k.sb("c_topf", [TP, NT, 8])
        rowf = k.sb("c_rowf", [TP, TOPK, NT])
        row = k.sb("c_row", [TP, TOPK, NT], U32)
        back = k.sb("c_back", [TP, NQ], U32)
        wk = k.sb("c_wk", [TP, TOPK, NT])
        w1s = k.sb("c_w1", [128, E, F])
        w2s = k.sb("c_w2", [128, E, FT, D])
        b1s = k.sb("c_b1", [128, E, FT])
        b2s = k.sb("c_b2", [128, E])
        hid = k.sb("c_hid", [128, 2, FT, CAP])
        xb = k.sb("c_xb", [TP, NQ, D + 1])
        xbT = k.sb("c_xbT", [128, SLOTS])
        obT = k.sb("c_obT", [128, SLOTS])
        picked = o[0:TP].rearrange("p b c t -> p (b c t)")[:, 0:TOPK * NT * D]\
                        .rearrange("p (n t d) -> p n t d", n=TOPK, t=NT)
        xs = o[0:TP].rearrange("p b c t -> p (b c t)")[:, 0:TOPK * NT * (D + 1)]\
                    .rearrange("p (n t d) -> p n t d", n=TOPK, t=NT)
        y = att

        got_o, got_f = [k.sem(f"c_got_o_{n}") for n in range(4)], k.sem("c_got_f")
        own_v = k.sem("c_own_v")
        oT_made, att_out, aT_made, aT_out, w_made, a_out, cT_made, cT_out, g_made, g_out, sig_out = (
            k.sem("c_oT_made"), k.sem("c_att_out"), k.sem("c_aT_made"), k.sem("c_aT_out"), k.sem("c_w_made"),
            k.sem("c_a_out"), k.sem("c_cT_made"), k.sem("c_cT_out"), k.sem("c_g_made"), k.sem("c_g_out"),
            k.sem("c_sig_out"))
        std_in, std_out, x2_made, x2T_made, x2T_out, l_made = (
            k.sem("c_std_in"), k.sem("c_std_out"), k.sem("c_x2_made"), k.sem("c_x2T_made"), k.sem("c_x2T_out"),
            k.sem("c_l_made"))
        e_in, e_out, sel_made, p_made, rows_made = (
            k.sem("c_e_in"), k.sem("c_e_out"), k.sem("c_sel"), k.sem("c_p_made"), k.sem("c_rows"))
        cleared, zeroed, sent = k.sem("c_cleared"), k.sem("c_zeroed"), k.sem("c_sent")
        queued = [k.sem(f"c_queued_{n}") for n in range(NQ // 4)]
        bT_made, bT_out, h_made, h_out, z_made, z_out = (k.sem("c_bT_made"), k.sem("c_bT_out"), k.sem("c_h_made"),
                                                         k.sem("c_h_out"), k.sem("c_z_made"), k.sem("c_z_out"))
        zT_made, zT_out = k.sem("c_zT_made"), k.sem("c_zT_out")
        less_made = k.sem("c_less_made")
        placed, xs_made, back_made, shifted = (k.sem("c_placed"), k.sem("c_xs_made"), k.sem("c_back_made"),
                                               k.sem("c_shifted"))
        got = [k.sem(f"c_got_{n}") for n in range(4)]
        fin, stored = k.sem("c_fin"), k.sem("c_stored")
        block = ctx.enter_context(nc.Block())

        @block.sync
        def _(sp):
            for n in range(4):
                sp.dma_start(o[:, 4 * n:4 * n + 4].rearrange("p b c t -> p b (c t)"),
                             o_dram[4 * n:4 * n + 4].rearrange("b p c s t -> p b (c s t)")).then_inc(got_o[n], 16)
            sp.wait_ge(cleared, 1)
            sp.dma_start(queue_rows, xb[:]).then_inc(zeroed, 16)
            for n in range(TOPK):
                sp.dma_start(made_rows[:, n], xb[:, 0:NT, 0:D]).then_inc(zeroed, 16)
            sp.dma_start(w1s[:], w1).then_inc(got_f, 16)
            sp.dma_start(w2s[:], w2).then_inc(got_f, 16)
            sp.dma_start(b1s[:], b1).then_inc(got_f, 16)
            sp.dma_start(b2s[:], b2).then_inc(got_f, 16)
            sp.wait_ge(sent, 16 * TOPK * NT)
            for n in range(NQ // 4):
                sp.dma_start(xb[:, 4 * n:4 * n + 4, :], queue_rows[:, 4 * n:4 * n + 4, :]).then_inc(queued[n], 16)
            sp.wait_ge(placed, 16 * NQ)
            for n in range(4):
                for c in range(TOPK):
                    sp.dma_start(picked[:, c, 4 * n:4 * n + 4, :], made_rows[:, c, 4 * n:4 * n + 4, :])\
                      .then_inc(got[n], 16)
            out_rows = out.rearrange("(t p) d -> p t d", p=TP)
            for n in range(4):
                sp.wait_ge(fin, 4 * n + 4)
                sp.dma_start(out_rows[:, 4 * n:4 * n + 4, :], gated[:, 4 * n:4 * n + 4, :]).then_inc(stored, 16)
            sp.wait_ge(zeroed, 16 * (1 + TOPK))
            sp.wait_ge(stored, 64)

        @block.gpsimd
        def _(pool):
            pool.wait_ge(cT_made, 4)
            pool.tensor_tensor(gated[:], gated[:], x1[:], ALU.subtract).then_inc(less_made, 1)
            pool.wait_ge(rows_made, 1)
            pool.wait_ge(xs_made, 3)
            pool.wait_ge(zeroed, 16 * (1 + TOPK))
            for t in range(NT):
                for n in range(TOPK):
                    pool.indirect_dma_start(
                        out=queue, out_offset=bass.IndirectOffsetOnAxis(ap=row[:, n, t:t + 1], axis=0),
                        in_=xs[:, n, t, :], in_offset=None, bounds_check=SLOTS - 1, oob_is_err=False)\
                        .then_inc(sent, 16)
            for n in range(NQ // 4):
                pool.wait_ge(back_made, n + 1)
                pool.wait_ge(zT_out, n + 1)
                for j in range(4 * n, 4 * n + 4):
                    pool.indirect_dma_start(
                        out=made, out_offset=bass.IndirectOffsetOnAxis(ap=back[:, j:j + 1], axis=0),
                        in_=xb[:, j, 0:D], in_offset=None, bounds_check=TOPK * N - 1, oob_is_err=False)\
                        .then_inc(placed, 16)

        def turn(pe, made, waited, src, rows, bank):
            for t in range(NT):
                pe.wait_ge(waited, t + 1)
                mm = pe.transpose(psum[:, bank + t // 4, (t % 4) * TP:(t % 4 + 1) * TP], src[:, t, :],
                                  ident[0:rows, 0:rows])
                if t % 4 == 3:
                    mm.then_inc(made, 1)

        def product(pe, made, ready, src, weights, bank):
            for t in range(NT):
                if t % 4 == 0:
                    pe.wait_ge(ready, t // 4 + 1)
                mm = pe.matmul(psum[0:TP, bank + t // 4, (t % 4) * D:(t % 4 + 1) * D], src[:, t * TP:(t + 1) * TP],
                               weights, start=True, stop=True)
                if t % 4 == 3:
                    mm.then_inc(made, 1)

        @block.tensor
        def _(pe):
            for t in range(NT):
                if t % 4 == 0:
                    pe.wait_ge(got_o[t // 4], 16)
                if t >= 2:
                    pe.wait_ge(att_out, t - 1)
                for l in range(2 * VH):
                    cols = 128 - VW
                    first = VW * (l % 2)
                    mm = pe.matmul(psum[0:TP, t % 2, l * 128:l * 128 + cols], o[:, t, l, :],
                                   ident[:, first:first + cols], start=True, stop=True)
                mm.then_inc(oT_made, 1)
            turn(pe, aT_made, att_out, att, TP, 4)
            product(pe, w_made, aT_out, cT, W("out"), 0)
            turn(pe, cT_made, a_out, gated, TP, 4)
            product(pe, g_made, cT_out, cT, W("gate"), 0)
            pe.wait_ge(g_out, 4)
            for n in range(5):
                for t in range(4 * n, min(4 * n + 4, NT)):
                    pe.wait_ge(x2_made, t + 1)
                    mm = pe.transpose(psum[:, 4 + n, (t % 4) * TP:(t % 4 + 1) * TP], x2[:, t, :], ident[0:TP, 0:TP])
                    if t % 4 == 3:
                        mm.then_inc(x2T_made, 1)
                if n >= 1:
                    pe.wait_ge(x2T_out, n)
                    for t in range(4 * n - 4, 4 * n):
                        mm = pe.matmul(psum[0:TP, 0, t * E:(t + 1) * E], x2T[:, t * TP:(t + 1) * TP], W("router"),
                                       start=True, stop=True)
            mm.then_inc(l_made, 1)
            pe.wait_ge(sel_made, 1)
            pe.matmul(psum[0:TP, 1, 0:NT * E], C("before")[0:TP], rt[:, 2, :, :], start=True, stop=True)
            pe.matmul(psum[0:TP, 2, 0:NT * E], C("ones")[0:TP], rt[:, 2, :, :], start=True, stop=True)\
              .then_inc(p_made, 1)
            for j in range(NQ):
                if j % 4 == 0:
                    pe.wait_ge(queued[j // 4], 16)
                mm = pe.transpose(psum[:, 3 + j // 4, (j % 4) * TP:(j % 4 + 1) * TP], xb[:, j, 0:D], ident[0:TP, 0:TP])
                if j % 4 == 3:
                    mm.then_inc(bT_made, 1)
            pe.wait_ge(got_f, 64)
            pe.wait_ge(bT_out, NQ // 4)

            def hidden(e):
                for f in range(FT):
                    if e >= 1:
                        pe.wait_ge(h_out, FT * (e - 1) + f + 1)
                    pe.matmul(psum[:, f, 0:CAP], w1s[:, e, f * 128:(f + 1) * 128], xbT[:, e * CAP:(e + 1) * CAP],
                              start=True, stop=True).then_inc(h_made, 1)

            def outcome(e):
                if e >= 2:
                    pe.wait_ge(z_out, e - 1)
                for f in range(FT):
                    pe.wait_ge(h_out, FT * e + f + 1)
                    mm = pe.matmul(psum[:, 4 + e % 2, 0:CAP], w2s[:, e, f, :], hid[:, e % 2, f, :],
                                   start=(f == 0), stop=(f == FT - 1))
                mm.then_inc(z_made, 1)

            turned = 0
            for e in range(E + 1):
                if e < E:
                    hidden(e)
                if e >= 1:
                    outcome(e - 1)
                whole = e - 1 if e < E else E
                if e == E:
                    pe.wait_ge(z_out, E)
                elif whole > 0:
                    pe.wait_ge(z_out, whole)
                while whole > 0 and turned < NQ and (turned // 4 + 1) * 4 * TP <= whole * CAP:
                    n = turned // 4
                    if n >= 2:
                        pe.wait_ge(zT_out, n - 1)
                    for j in range(4):
                        mm = pe.transpose(psum[0:TP, 6 + n % 2, j * D:(j + 1) * D],
                                          obT[:, (turned + j) * TP:(turned + j + 1) * TP], ident)
                    mm.then_inc(zT_made, 1)
                    turned += 4

        @block.scalar
        def _(act):
            def evacuate(made, out_sem, dst):
                for n in range(4):
                    act.wait_ge(made, n + 1)
                    act.copy(dst[:, n * SEG:(n + 1) * SEG], psum[:, 4 + n, 0:SEG]).then_inc(out_sem, 1)

            evacuate(aT_made, aT_out, cT)
            act.wait_ge(w_made, 4)
            evacuate(cT_made, cT_out, cT)
            act.wait_ge(g_out, 4)
            act.activation(x2[:], x2[:], ACT.Sigmoid).then_inc(sig_out, 1)
            act.wait_ge(std_in, 1)
            act.activation(rstd[:, 0, :], rstd[:, 0, :], ACT.Sqrt).then_inc(std_out, 1)
            evacuate(x2T_made, x2T_out, x2T)
            act.wait_ge(e_in, 1)
            act.activation(rt[:, 1, :, :], rt[:, 0, :, :], ACT.Exp).then_inc(e_out, 1)
            for n in range(TOPK):
                act.copy(xs[:, n, :, 0:D], x2[:]).then_inc(xs_made, 1)
            act.copy(xs[:, :, :, D], C("dest")[0:TP].rearrange("p (n t) -> p n t", n=TOPK)).then_inc(xs_made, 1)
            for n in range(NQ // 4):
                act.wait_ge(bT_made, n + 1)
                act.copy(xbT[:, n * SEG:(n + 1) * SEG], psum[:, 3 + n, 0:SEG]).then_inc(bT_out, 1)
            act.wait_ge(got_f, 64)
            for e in range(E):
                for f in range(FT):
                    act.wait_ge(h_made, FT * e + f + 1)
                    if e >= 2:
                        act.wait_ge(z_made, e - 1)
                    act.activation(hid[:, e % 2, f, :], psum[:, f, 0:CAP], ACT.Gelu, bias=b1s[:, e, f:f + 1])\
                       .then_inc(h_out, 1)

            def finish(n):
                act.wait_ge(shifted, n + 1)
                for t in range(4 * n, 4 * n + 4):
                    act.activation(gated[:, t, :], y[:, t, :], ACT.Identity, bias=col[:, 0, t:t + 1],
                                   scale=rstd[:, 1, t:t + 1]).then_inc(fin, 1)

            for n in range(4):
                act.wait_ge(std_in, 2 + n)
                act.activation(rstd[:, 0, 4 * n:4 * n + 4], rstd[:, 0, 4 * n:4 * n + 4], ACT.Sqrt).then_inc(std_out, 1)
                if n >= 1:
                    finish(n - 1)
            finish(3)

        @block.vector
        def _(dve):
            own = Own(dve, own_v)
            own.mark(dve.memset(xb[:], 0.0))
            own.settle()
            dve.memset(xb[:, :, D], float(2 * TOPK * N)).then_inc(cleared, 1)
            for t in range(NT):
                dve.wait_ge(oT_made, t + 1)
                p = psum[0:TP, t % 2, :]
                own.link(dve.reciprocal(strided(rden[:, t % 2, :], [[4, 4], [1, 4]]),
                                        strided(p, [[32, 4], [128, 4]], HD)))
                dve.tensor_tensor(strided(att[:, t, :], [[4 * HD, 4], [HD, 4], [1, HD]]),
                                  strided(p, [[32, 4], [128, 4], [1, HD]]),
                                  strided(rden[:, t % 2, :], [[4, 4], [1, 4], [0, HD]]), ALU.mult)\
                   .then_inc(att_out, 1)
            four = lambda a, n: a[:, 4 * n:4 * n + 4, :]
            rows = lambda name: strided(W(name)[0:TP], [[0, 4], [1, D]])
            bank4 = lambda n: psum[0:TP, n, 0:512].rearrange("p (t d) -> p t d", t=4)
            for n in range(4):
                dve.wait_ge(w_made, n + 1)
                dve.tensor_tensor(four(gated, n), bank4(n), strided(prep["b_att"][:], [[0, 4], [1, D]]),
                                  ALU.add).then_inc(a_out, 4)
            for n in range(4):
                dve.wait_ge(g_made, n + 1)
                dve.tensor_tensor(four(x2, n), bank4(n), rows("b_gate"), ALU.add).then_inc(g_out, 1)
            dve.wait_ge(sig_out, 1)
            dve.wait_ge(less_made, 1)
            own.link(dve.tensor_tensor(gated[:], gated[:], x2[:], ALU.mult))
            own.link(dve.scalar_tensor_tensor(out=gated[:], in0=x1[:], scalar=2.0, in1=gated[:],
                                              op0=ALU.mult, op1=ALU.add))
            layernorm_dve(own, TP, gated, x2, stats, mv, rstd, std_in, (std_out, 1), x2_made)
            dve.wait_ge(l_made, 1)
            own.link(dve.tensor_tensor(rt[:, 3, :, :], psum[0:TP, 0, 0:NT * E].rearrange("p (t e) -> p t e", e=E),
                                       strided(W("b_router")[0:TP], [[0, NT], [1, E]]), ALU.add))
            own.link(dve.tensor_reduce(col[:, 0, :], rt[:, 3, :, :], AX.X, ALU.max))
            spread = lambda n: strided(col[:, n, :], [[1, NT], [0, E]])
            dve.tensor_tensor(rt[:, 0, :, :], rt[:, 3, :, :], spread(0), ALU.subtract).then_inc(e_in, 1)
            dve.wait_ge(e_out, 1)
            own.link(dve.tensor_reduce(col[:, 0, :], rt[:, 1, :, :], AX.X, ALU.add))
            own.link(dve.reciprocal(col[:, 1, :], col[:, 0, :]))
            own.link(dve.tensor_tensor(rt[:, 1, :, :], rt[:, 1, :, :], spread(1), ALU.mult))
            for t in range(NT):
                own.mark(dve.max(top[:, t, :], rt[:, 1, t, :]))
            own.settle()
            for t in range(NT):
                own.mark(dve.max_index(topi[:, t, :], top[:, t, :], rt[:, 1, t, :]))
            own.settle()
            own.link(dve.tensor_copy(topf[:], topi[:]))
            iota = strided(C("iota")[0:TP], [[0, NT], [1, E]])
            for n in range(TOPK):
                own.mark(dve.tensor_tensor(rt[:, 6 + n, :, :], iota, strided(topf[:, :, n:n + 1], [[8, NT], [0, E]]),
                                           ALU.is_equal))
            own.settle()
            dve.tensor_tensor(rt[:, 2, :, :], rt[:, 6, :, :], rt[:, 7, :, :], ALU.add).then_inc(sel_made, 1)
            dve.wait_ge(p_made, 1)
            own.link(dve.memset(rt[:, 3, 0, :], 0.0))
            own.link(dve.tensor_copy(rt[:, 4, :, :], psum[0:TP, 2, 0:NT * E].rearrange("p (t e) -> p t e", e=E)))
            for t in range(1, NT):
                own.link(dve.tensor_tensor(rt[:, 3, t, :], rt[:, 3, t - 1, :], rt[:, 4, t - 1, :], ALU.add))
            own.link(dve.tensor_tensor(rt[:, 4, :, :], psum[0:TP, 1, 0:NT * E].rearrange("p (t e) -> p t e", e=E),
                                       rt[:, 3, :, :], ALU.add))
            own.link(dve.tensor_scalar(rt[:, 0, :, :], rt[:, 4, :, :], float(CAP), float(FAR), ALU.is_ge, ALU.mult))
            own.link(dve.tensor_tensor(rt[:, 0, :, :], rt[:, 0, :, :], rt[:, 4, :, :], ALU.add))
            own.link(dve.tensor_tensor(rt[:, 0, :, :], rt[:, 0, :, :], strided(C("slot")[0:TP], [[0, NT], [1, E]]),
                                       ALU.add))
            for n in range(TOPK):
                own.mark(dve.tensor_tensor(rt[:, 2 + n, :, :], rt[:, 0, :, :], rt[:, 6 + n, :, :], ALU.mult))
            own.settle()
            own.link(dve.tensor_reduce(rowf[:], rt[:, 2:4, :, :], AX.X, ALU.add))
            dve.tensor_copy(row[:], rowf[:]).then_inc(rows_made, 1)
            own.link(dve.scalar_tensor_tensor(out=rt[:, 4, :, :], in0=rt[:, 4, :, :], scalar=float(CAP),
                                              in1=rt[:, 1, :, :], op0=ALU.is_lt, op1=ALU.mult))
            for n in range(TOPK):
                own.mark(dve.tensor_tensor(rt[:, 2 + n, :, :], rt[:, 4, :, :], rt[:, 6 + n, :, :], ALU.mult))
            own.settle()
            own.link(dve.tensor_reduce(wk[:], rt[:, 2:4, :, :], AX.X, ALU.add))
            own.link(dve.tensor_tensor(col[:, 0, :], wk[:, 0, :], wk[:, 1, :], ALU.add))
            own.link(dve.tensor_scalar(col[:, 1, :], col[:, 0, :], 1e-6, None, ALU.max))
            own.link(dve.reciprocal(col[:, 0, :], col[:, 1, :]))
            own.link(dve.tensor_tensor(wk[:], wk[:], strided(col[:, 0, :], [[0, TOPK], [1, NT]]), ALU.mult))

            def expert_out(e):
                dve.wait_ge(z_made, e + 1)
                dve.tensor_scalar(obT[:, e * CAP:(e + 1) * CAP], psum[:, 4 + e % 2, 0:CAP], b2s[:, e:e + 1], None,
                                  ALU.add).then_inc(z_out, 1)

            def rows_out(n):
                dve.wait_ge(zT_made, n + 1)
                dve.tensor_copy(xb[:, 4 * n:4 * n + 4, 0:D],
                                psum[0:TP, 6 + n % 2, 0:512].rearrange("p (t d) -> p t d", t=4)).then_inc(zT_out, 1)

            for n in range(NQ // 4):
                dve.wait_ge(queued[n], 16)
                dve.tensor_copy(back[:, 4 * n:4 * n + 4], xb[:, 4 * n:4 * n + 4, D]).then_inc(back_made, 1)
            dve.wait_ge(bT_made, NQ // 4)
            done = 0
            for e in range(E):
                expert_out(e)
                while done < NQ // 4 and (done + 1) * 4 * TP <= (e - 1) * CAP:
                    rows_out(done)
                    done += 1
            for n in range(done, NQ // 4):
                rows_out(n)
            def finish(n):
                q = slice(4 * n, 4 * n + 4)
                dve.wait_ge(std_out, 2 + n)
                own.link(dve.reciprocal(rstd[:, 1, q], rstd[:, 0, q]))
                dve.scalar_tensor_tensor(out=col[:, 0, q], in0=mv[:, q, 0], scalar=-1.0, in1=rstd[:, 1, q],
                                         op0=ALU.mult, op1=ALU.mult).then_inc(shifted, 1)

            for n in range(4):
                tiles = range(4 * n, 4 * n + 4)
                dve.wait_ge(got[n], 16 * TOPK)
                for c in range(TOPK):
                    for t in tiles:
                        own.mark(dve.scalar_tensor_tensor(out=y[:, t, :], in0=picked[:, c, t, :],
                                                          scalar=wk[:, c, t:t + 1],
                                                          in1=x2[:, t, :] if c == 0 else y[:, t, :],
                                                          op0=ALU.mult, op1=ALU.add))
                    own.settle()
                for t in tiles:
                    own.mark(dve.bn_stats(stats[:, t, :], y[:, t, :]))
                own.settle()
                for t in tiles:
                    own.mark(dve.bn_aggr(mv[:, t, :], stats[:, t, :]))
                own.settle()
                dve.tensor_scalar(rstd[:, 0, 4 * n:4 * n + 4], mv[:, 4 * n:4 * n + 4, 1], EPS_LN, None, ALU.add)\
                   .then_inc(std_in, 1)
                if n >= 1:
                    finish(n - 1)
            finish(3)


def decoder_layer(nc, x_rows, x_cols, ctx_in, wpack, cpack, rope, hats, nodes, w1, b1, w2, b2, out):
    xq_split = nc.dram_tensor("xq_split", [2, 128, N], F32, kind="Internal").ap()
    node_dram = nc.dram_tensor("bias_nodes", [128, BQ * HQ], F32, kind="Internal").ap()
    o_dram = nc.dram_tensor("o_sums", [NT, 128, 2 * VH, 2, T], F32, kind="Internal").ap()
    queue = nc.dram_tensor("queue", [SLOTS, D + 1], F32, kind="Internal").ap()
    made = nc.dram_tensor("made", [TOPK * N, D], F32, kind="Internal").ap()
    with ExitStack() as ctx:
        k = Core(nc, ctx)
        psum = ctx.enter_context(nc.psum_tensor("psum", [128, 8, 512], F32))
        wt = k.sb("wt", [128, W_N])
        ct = k.sb("ct", [128, C_N])
        x1 = k.sb("x1", [TP, NT, D])
        prep = {n: k.sb("w_" + n, [128, D]) for n in ("xq", "xqp", "xk", "xkp", "xv")}
        start = {"xin": k.sb("xin", [CH, 2, NC, D]), "tab": k.sb("tab", [128, 2, S]),
                 "vx": k.sb("cross_vx", [CH, 2, NC, VROW]), "whole": k.sb("whole", [CH, 2, NC]),
                 "ctx_got": [k.sem("ctx_even"), k.sem("ctx_odd")], "tab_got": k.sem("tab_got")}
        for name in CONTEXT_ARRAYS:
            shape = [CH, NC] + {"stats": [6], "mv": [2]}.get(name, [])
            start[name] = k.sb("ctx_" + name, shape, I32 if name == "bits" else F32)
        for name in CONTEXT_SIGNALS:
            start[name] = k.sem("ctx_" + name)
        hat_dram = nc.dram_tensor("bias_hats", [1 + 2 * HAT, S], F32, kind="Internal").ap()
        prep["off_cols"] = k.sb("off_cols", [128, TP])
        prep["off"] = k.sb("off", [128, 5])
        prep["b_att"] = k.sb("b_att", [TP, D])
        self_attention(nc, psum, wt, ct, x1, xq_split, prep, start, (hat_dram, node_dram),
                       (x_rows, x_cols, wpack, cpack, ctx_in, rope, hats, nodes))
        cross_attention(nc, psum, wt, ct, xq_split, (hat_dram, node_dram), o_dram, prep, start, ctx_in)
        mix_and_experts(nc, psum, wt, ct, x1, o_dram, queue, made, prep, (w1, b1, w2, b2), out)


def resize_weights(n_in, n_out):
    step = n_in / n_out
    at = (np.arange(n_out) + 0.5) * step - 0.5
    w = np.maximum(0.0, 1.0 - np.abs(at[None, :] - np.arange(n_in)[:, None]) / max(step, 1.0))
    return w / w.sum(0, keepdims=True)


def rotary(positions, width):
    half = width // 2
    inv = (np.float32(1.0) / np.float32(10000.0) ** (np.arange(0, width, 2, dtype=np.float32) / np.float32(width)))
    ang = (np.arange(positions, dtype=np.float32)[:, None] * inv[None, :].astype(np.float32)).astype(np.float32)
    cos, sin = np.cos(ang.astype(np.float64)), np.sin(ang.astype(np.float64))
    return np.concatenate([cos, cos], 1), np.concatenate([-sin, sin], 1), half


def half_precision_pair(a):
    a = a.astype(np.float32)
    bits = a.view(np.uint32).astype(np.uint64)
    hi = ((bits + 0x800) & 0xFFFFF000).astype(np.uint32).view(np.float32)
    return hi, (a - hi).astype(np.float32)


def constants():
    c = np.zeros((128, C_N), np.float32)

    def put(name, a):
        lo, _ = C_AT[name]
        c[:a.shape[0], lo:lo + a.shape[1]] = a

    p = np.arange(128)
    put("ident", np.eye(128))
    put("mask16", (p[:, None] // HD == np.arange(NH)[None, :]) * 1.0)
    put("mask4", ((p[:, None] % 32) // HD == np.arange(GH)[None, :]) * 1.0)
    cq, sq, _ = rotary(T, HD)
    put("cosq", cq[:, p % HD].T * HD ** -0.5)
    put("sinq", sq[:, p % HD].T * HD ** -0.5)
    t = np.arange(T)
    causal = np.zeros((128, T))
    causal[0:T] = causal[64:64 + T] = t[:, None] <= t[None, :]
    put("causal", causal)
    put("cosa", cq[np.arange(TP) % T])
    put("sina", sq[np.arange(TP) % T])
    put("before", (np.arange(TP)[:, None] < np.arange(TP)[None, :]) * 1.0)
    put("ones", np.ones((TP, TP)))
    put("iota", np.tile(np.arange(E), (128, 1)))
    put("slot", np.tile(np.arange(E) * CAP, (128, 1)))
    put("dest", np.arange(TP)[:, None] + TP * np.arange(TOPK * NT)[None, :])
    ck, sk, _ = rotary(S, HD)
    rope = np.stack([ck[:, p % HD].T, sk[:, p % HD].T], 1).astype(np.float32)

    pos = np.arange(BIAS_LEN, dtype=np.float32)
    dist = np.abs(pos[None, :] - pos[:, None])
    bias = np.exp(-dist * np.float32(0.1)) - dist * np.float32(0.05)
    whole = 2 * S // 4
    hat = np.rint(resize_weights(BIAS_LEN, S) * whole)
    base = (bias.astype(np.float64) @ resize_weights(BIAS_LEN, T)) / whole
    hi, lo = half_precision_pair(base)
    hats = np.ones((1 + 2 * HAT, S), np.float32)
    hats[1:] = 0.0
    nodes = np.zeros((4, 32, BQ, T), np.float32)
    for n in range(NC):
        cols = slice(n * CH, (n + 1) * CH)
        touched = np.nonzero(hat[:, cols].sum(1))[0]
        assert len(touched) <= HAT
        for r, j in enumerate(touched):
            for off, part in ((0, hi), (HAT, lo)):
                hats[1 + off + r, cols] = hat[j, cols]
                nodes[n // BQ, off + r, n % BQ, :] = part[j]
    return c, rope, hats, nodes.reshape(128, BQ * T)


def kernel(x, ctx_1024, L0_attn_Wq, L0_attn_Wkv, L0_attn_Wproj, L0_xattn_Wqkv, L0_xattn_Wout, L0_xattn_b_out,
           L0_xattn_Wgate, L0_xattn_b_gate, L0_xattn_gamma, L0_xattn_beta, L0_ffn_w_router, L0_ffn_b_router,
           L0_ffn_w1, L0_ffn_b1, L0_ffn_w2, L0_ffn_b2):
    import concourse.bacc as bacc
    from concourse.bass_utils import run_bass_kernel_spmd

    a = {n: np.asarray(v) for n, v in locals().items() if n[0] in "xcL" and not n.startswith("concourse")}
    x = a["x"].reshape(N, D)
    wqkv = a["L0_xattn_Wqkv"]
    partner = np.arange(D) // HD * HD + (np.arange(D) % HD + HD // 2) % HD
    wq, wk, wv = wqkv[:D], wqkv[D:2 * D], wqkv[2 * D:]
    rows = lambda v: np.broadcast_to(v[None, :], (128, v.shape[0]))
    wpack = np.concatenate(
        [a["L0_attn_Wq"].T, a["L0_attn_Wkv"].T, a["L0_attn_Wproj"].T, wq.T, wq[partner].T, wk.T, wk[partner].T,
         wv.T, a["L0_xattn_Wout"].T, a["L0_xattn_Wgate"].T, a["L0_xattn_gamma"][:, None],
         a["L0_xattn_beta"][:, None], rows(a["L0_xattn_b_out"]), rows(a["L0_xattn_b_gate"]),
         a["L0_ffn_w_router"], rows(a["L0_ffn_b_router"])], axis=1)
    cpack, rope, hats, nodes = constants()
    arrays = {
        "x_rows": x, "x_cols": x.T, "ctx_in": a["ctx_1024"], "wpack": wpack, "cpack": cpack, "rope": rope,
        "hats": hats, "nodes": nodes,
        "w1": a["L0_ffn_w1"].transpose(1, 0, 2),
        "b1": a["L0_ffn_b1"].reshape(E, FT, 128).transpose(2, 0, 1),
        "w2": a["L0_ffn_w2"].reshape(E, FT, 128, D).transpose(2, 0, 1, 3),
        "b2": a["L0_ffn_b2"].T,
    }
    arrays = {n: np.ascontiguousarray(v) for n, v in arrays.items()}
    nc = bacc.Bacc("TRN2", target_bir_lowering=False, num_devices=1)
    args = [nc.dram_tensor(n, v.shape, F32, kind="ExternalInput").ap() for n, v in arrays.items()]
    out = nc.dram_tensor("out", (N, D), F32, kind="ExternalOutput").ap()
    decoder_layer(nc, *args, out)
    r = run_bass_kernel_spmd(nc, [arrays], core_ids=[0])
    return r.results[0]["out"].reshape(B, T, D)
```
